# Optimizing a Trainium2 kernel written in Bass

```python
import numpy as np
import jax
import jax.numpy as jnp

def _softmax(x, axis=-1):
    return jax.nn.softmax(x, axis=axis)

def _gelu(x):
    return jax.nn.gelu(x, approximate=True)

def _silu(x):
    return jax.nn.silu(x)

def _sigmoid(x):
    return jax.nn.sigmoid(x)

def _layernorm(x, axis=-1, eps=1e-05):
    m = jnp.mean(x, axis=axis, keepdims=True)
    v = jnp.var(x, axis=axis, keepdims=True)
    return (x - m) / jnp.sqrt(v + eps)

def _scatter_add(tgt, idx, src, axis=0):
    return tgt.at[idx].add(src)

def _segment_sum(src, seg, n):
    return jax.ops.segment_sum(src, seg, n)
kernel_name = 'mk_recurrent_d2_jaxref_r8_089332'

def setup_inputs(seed: int=0):
    np.random.seed(seed)
    _w = jnp.asarray

    def _L0_attn_setup():
        import jax, jax.numpy as jnp
        import numpy as np
        N_HEADS = 16
        D_HEAD = 128
        D_MODEL = 256
        MAXLEN = 256
        key = jax.random.key(seed)
        ks = jax.random.split(key, 9)
        b, t = (2, 256)
        hd = N_HEADS * D_HEAD
        init = 0.02
        return {'x': jax.random.normal(ks[0], (b, t, D_MODEL), dtype=jnp.float32), 'Wq': jax.random.normal(ks[1], (D_MODEL, hd), dtype=jnp.float32) * init, 'bq': jnp.zeros((hd,), dtype=jnp.float32), 'Wk': jax.random.normal(ks[2], (D_MODEL, hd), dtype=jnp.float32) * init, 'bk': jnp.zeros((hd,), dtype=jnp.float32), 'Wv': jax.random.normal(ks[3], (D_MODEL, hd), dtype=jnp.float32) * init, 'bv': jnp.zeros((hd,), dtype=jnp.float32), 'Wo': jax.random.normal(ks[4], (hd, D_MODEL), dtype=jnp.float32) * init, 'bo': jnp.zeros((D_MODEL,), dtype=jnp.float32)}
    _L0_attn_in = _L0_attn_setup()

    def _L0_ffn_setup():
        import jax, jax.numpy as jnp
        import numpy as np
        HIDDEN = 256
        N_EXPERTS = 8
        N_SHARED = 2
        TOP_K = 2
        MOE_FF = 176
        SHARED_FF = N_SHARED * MOE_FF
        SCALE = 2.5
        BATCH, SEQ = (2, 128)
        key = jax.random.key(seed)
        ks = jax.random.split(key, 8)
        s = 0.02
        return {'hidden_states': jax.random.normal(ks[0], (BATCH, SEQ, HIDDEN), jnp.float32), 'gate_w': jax.random.normal(ks[1], (N_EXPERTS, HIDDEN), jnp.float32) * s, 'shared_wg': jax.random.normal(ks[2], (SHARED_FF, HIDDEN), jnp.float32) * s, 'shared_wu': jax.random.normal(ks[3], (SHARED_FF, HIDDEN), jnp.float32) * s, 'shared_wd': jax.random.normal(ks[4], (HIDDEN, SHARED_FF), jnp.float32) * s, 'exp_wg': jax.random.normal(ks[5], (N_EXPERTS, MOE_FF, HIDDEN), jnp.float32) * s, 'exp_wu': jax.random.normal(ks[6], (N_EXPERTS, MOE_FF, HIDDEN), jnp.float32) * s, 'exp_wd': jax.random.normal(ks[7], (N_EXPERTS, HIDDEN, MOE_FF), jnp.float32) * s}
    _L0_ffn_in = _L0_ffn_setup()

    def _L1_attn_setup():
        import jax, jax.numpy as jnp
        import numpy as np
        import math
        B, T = (4, 128)
        D_MODEL = 256
        HEAD_DIM = 64
        N_HEADS = 32
        N_KV = 8
        Q_MULT = N_HEADS // N_KV
        SLIDING_WINDOW = 128
        CAUSAL = True
        SM_SCALE = 1.0 / math.sqrt(HEAD_DIM)
        ROPE_THETA = 150000.0
        SCALING = 32.0
        NTK_ALPHA = 1.0
        NTK_BETA = 32.0
        ICL = 128

        def _rope_cos_sin(t_len):
            d_half = HEAD_DIM // 2
            freq = ROPE_THETA ** (np.arange(0, HEAD_DIM, 2, dtype=np.float32) / HEAD_DIM)
            concentration = 0.1 * math.log(SCALING) + 1.0
            low = d_half * math.log(ICL / (NTK_BETA * 2 * math.pi)) / math.log(ROPE_THETA)
            high = d_half * math.log(ICL / (NTK_ALPHA * 2 * math.pi)) / math.log(ROPE_THETA)
            interpolation = 1.0 / (SCALING * freq)
            extrapolation = 1.0 / freq
            ramp = np.clip((np.arange(d_half, dtype=np.float32) - low) / (high - low), 0.0, 1.0)
            mask = 1.0 - ramp
            inv_freq = interpolation * (1.0 - mask) + extrapolation * mask
            freqs = np.outer(np.arange(t_len, dtype=np.float32), inv_freq)
            return (jnp.asarray(np.cos(freqs) * concentration, jnp.float32), jnp.asarray(np.sin(freqs) * concentration, jnp.float32))

        def _apply_rope(x, cos, sin):
            x1, x2 = jnp.split(x, 2, axis=-1)
            return jnp.concatenate([x1 * cos - x2 * sin, x2 * cos + x1 * sin], axis=-1)
        key = jax.random.key(seed)
        ks = jax.random.split(key, 6)
        qkv_dim = HEAD_DIM * (N_HEADS + 2 * N_KV)
        return {'x': jax.random.normal(ks[0], (B, T, D_MODEL), jnp.float32), 'qkv_w': jax.random.normal(ks[1], (qkv_dim, D_MODEL), jnp.float32) * 0.02, 'qkv_b': jax.random.normal(ks[2], (qkv_dim,), jnp.float32) * 0.02, 'out_w': jax.random.normal(ks[3], (D_MODEL, N_HEADS * HEAD_DIM), jnp.float32) * 0.02, 'out_b': jax.random.normal(ks[4], (D_MODEL,), jnp.float32) * 0.02, 'sinks': jax.random.normal(ks[5], (N_HEADS,), jnp.float32) * (1.0 / math.sqrt(HEAD_DIM))}
    _L1_attn_in = _L1_attn_setup()

    def _L1_ffn_setup():
        import jax, jax.numpy as jnp
        import numpy as np
        E = 16
        D = 256
        H = 176
        HS = 2 * 176
        TOP_K = 6
        ROUTE_SCALE = 1.0
        key = jax.random.key(seed)
        ks = jax.random.split(key, 16)
        s = 0.02
        return {'x': jax.random.normal(ks[0], (4, 128, D), dtype=jnp.float32), 'gate_w': jax.random.normal(ks[1], (E, D), dtype=jnp.float32) * s, 'gate_b': jax.random.normal(ks[2], (E,), dtype=jnp.float32) * s, 'w1': jax.random.normal(ks[3], (E, H, D), dtype=jnp.float32) * s, 'b1': jax.random.normal(ks[4], (E, H), dtype=jnp.float32) * s, 'w2': jax.random.normal(ks[5], (E, D, H), dtype=jnp.float32) * s, 'b2': jax.random.normal(ks[6], (E, D), dtype=jnp.float32) * s, 'w3': jax.random.normal(ks[7], (E, H, D), dtype=jnp.float32) * s, 'b3': jax.random.normal(ks[8], (E, H), dtype=jnp.float32) * s, 'ws1': jax.random.normal(ks[9], (HS, D), dtype=jnp.float32) * s, 'bs1': jax.random.normal(ks[10], (HS,), dtype=jnp.float32) * s, 'ws2': jax.random.normal(ks[11], (D, HS), dtype=jnp.float32) * s, 'bs2': jax.random.normal(ks[12], (D,), dtype=jnp.float32) * s, 'ws3': jax.random.normal(ks[13], (HS, D), dtype=jnp.float32) * s, 'bs3': jax.random.normal(ks[14], (HS,), dtype=jnp.float32) * s}
    _L1_ffn_in = _L1_ffn_setup()
    _d = {'L0_attn_x': _L0_attn_in['x'], 'L0_attn_Wq': _L0_attn_in['Wq'], 'L0_attn_bq': _L0_attn_in['bq'], 'L0_attn_Wk': _L0_attn_in['Wk'], 'L0_attn_bk': _L0_attn_in['bk'], 'L0_attn_Wv': _L0_attn_in['Wv'], 'L0_attn_bv': _L0_attn_in['bv'], 'L0_attn_Wo': _L0_attn_in['Wo'], 'L0_attn_bo': _L0_attn_in['bo'], 'L0_ffn_gate_w': _L0_ffn_in['gate_w'], 'L0_ffn_shared_wg': _L0_ffn_in['shared_wg'], 'L0_ffn_shared_wu': _L0_ffn_in['shared_wu'], 'L0_ffn_shared_wd': _L0_ffn_in['shared_wd'], 'L0_ffn_exp_wg': _L0_ffn_in['exp_wg'], 'L0_ffn_exp_wu': _L0_ffn_in['exp_wu'], 'L0_ffn_exp_wd': _L0_ffn_in['exp_wd'], 'L1_attn_qkv_w': _L1_attn_in['qkv_w'], 'L1_attn_qkv_b': _L1_attn_in['qkv_b'], 'L1_attn_out_w': _L1_attn_in['out_w'], 'L1_attn_out_b': _L1_attn_in['out_b'], 'L1_attn_sinks': _L1_attn_in['sinks'], 'L1_ffn_gate_w': _L1_ffn_in['gate_w'], 'L1_ffn_gate_b': _L1_ffn_in['gate_b'], 'L1_ffn_w1': _L1_ffn_in['w1'], 'L1_ffn_b1': _L1_ffn_in['b1'], 'L1_ffn_w2': _L1_ffn_in['w2'], 'L1_ffn_b2': _L1_ffn_in['b2'], 'L1_ffn_w3': _L1_ffn_in['w3'], 'L1_ffn_b3': _L1_ffn_in['b3'], 'L1_ffn_ws1': _L1_ffn_in['ws1'], 'L1_ffn_bs1': _L1_ffn_in['bs1'], 'L1_ffn_ws2': _L1_ffn_in['ws2'], 'L1_ffn_bs2': _L1_ffn_in['bs2'], 'L1_ffn_ws3': _L1_ffn_in['ws3'], 'L1_ffn_bs3': _L1_ffn_in['bs3']}
    _x0 = _d['L0_attn_x']
    _d['L0_attn_x'] = jax.random.normal(jax.random.fold_in(jax.random.key(seed), 1), (4, 256, 256), dtype=_x0.dtype)
    del _x0
    return _d

def reference(L0_attn_x, L0_attn_Wq, L0_attn_bq, L0_attn_Wk, L0_attn_bk, L0_attn_Wv, L0_attn_bv, L0_attn_Wo, L0_attn_bo, L0_ffn_gate_w, L0_ffn_shared_wg, L0_ffn_shared_wu, L0_ffn_shared_wd, L0_ffn_exp_wg, L0_ffn_exp_wu, L0_ffn_exp_wd, L1_attn_qkv_w, L1_attn_qkv_b, L1_attn_out_w, L1_attn_out_b, L1_attn_sinks, L1_ffn_gate_w, L1_ffn_gate_b, L1_ffn_w1, L1_ffn_b1, L1_ffn_w2, L1_ffn_b2, L1_ffn_w3, L1_ffn_b3, L1_ffn_ws1, L1_ffn_bs1, L1_ffn_ws2, L1_ffn_bs2, L1_ffn_ws3, L1_ffn_bs3):

    def _L0_attn_ref(x, Wq, bq, Wk, bk, Wv, bv, Wo, bo):
        import jax, jax.numpy as jnp
        import numpy as np
        N_HEADS = 16
        D_HEAD = 128
        D_MODEL = 256
        MAXLEN = 256
        b, t, _ = x.shape
        h, dh = (N_HEADS, D_HEAD)
        scale = 1.0 / np.sqrt(dh).astype(np.float32)
        q = (x @ Wq + bq).reshape(b, h, t, dh)
        k = (x @ Wk + bk).reshape(b, t, h, dh).transpose(0, 2, 3, 1)
        v = (x @ Wv + bv).reshape(b, t, h, dh).transpose(0, 2, 1, 3)
        logits = jnp.einsum('bhtd,bhds->bhts', q, k) * scale
        mask = jnp.triu(jnp.full((t, t), -jnp.inf, dtype=x.dtype), k=1)
        weights = jax.nn.softmax(logits + mask, axis=-1)
        out = jnp.einsum('bhts,bhsd->bhtd', weights, v)
        out = out.transpose(0, 2, 1, 3).reshape(b, t, h * dh)
        return out @ Wo + bo

    def _L0_ffn_ref(hidden_states, gate_w, shared_wg, shared_wu, shared_wd, exp_wg, exp_wu, exp_wd):
        import jax, jax.numpy as jnp
        import numpy as np
        HIDDEN = 256
        N_EXPERTS = 8
        N_SHARED = 2
        TOP_K = 2
        MOE_FF = 176
        SHARED_FF = N_SHARED * MOE_FF
        SCALE = 2.5
        BATCH, SEQ = (2, 128)
        B, S, D = hidden_states.shape
        T = B * S
        xf = hidden_states.reshape(T, D)
        scores = jax.nn.sigmoid(xf @ gate_w.T)
        topk_w, topk_idx = jax.lax.top_k(scores, TOP_K)
        topk_w = topk_w / (topk_w.sum(axis=-1, keepdims=True) + 1e-20)
        topk_w = topk_w * SCALE
        shared_out = jax.nn.silu(xf @ shared_wg.T) * (xf @ shared_wu.T) @ shared_wd.T
        h = jax.nn.silu(jnp.einsum('td,efd->etf', xf, exp_wg)) * jnp.einsum('td,efd->etf', xf, exp_wu)
        all_out = jnp.einsum('etf,edf->etd', h, exp_wd)
        picked = all_out[topk_idx, jnp.arange(T)[:, None]]
        routed_out = (topk_w[..., None] * picked).sum(axis=1)
        return (shared_out + routed_out).reshape(B, S, D)

    def _L1_attn_ref(x, qkv_w, qkv_b, out_w, out_b, sinks):
        import jax, jax.numpy as jnp
        import numpy as np
        import math
        B, T = (4, 128)
        D_MODEL = 256
        HEAD_DIM = 64
        N_HEADS = 32
        N_KV = 8
        Q_MULT = N_HEADS // N_KV
        SLIDING_WINDOW = 128
        CAUSAL = True
        SM_SCALE = 1.0 / math.sqrt(HEAD_DIM)
        ROPE_THETA = 150000.0
        SCALING = 32.0
        NTK_ALPHA = 1.0
        NTK_BETA = 32.0
        ICL = 128

        def _rope_cos_sin(t_len):
            d_half = HEAD_DIM // 2
            freq = ROPE_THETA ** (np.arange(0, HEAD_DIM, 2, dtype=np.float32) / HEAD_DIM)
            concentration = 0.1 * math.log(SCALING) + 1.0
            low = d_half * math.log(ICL / (NTK_BETA * 2 * math.pi)) / math.log(ROPE_THETA)
            high = d_half * math.log(ICL / (NTK_ALPHA * 2 * math.pi)) / math.log(ROPE_THETA)
            interpolation = 1.0 / (SCALING * freq)
            extrapolation = 1.0 / freq
            ramp = np.clip((np.arange(d_half, dtype=np.float32) - low) / (high - low), 0.0, 1.0)
            mask = 1.0 - ramp
            inv_freq = interpolation * (1.0 - mask) + extrapolation * mask
            freqs = np.outer(np.arange(t_len, dtype=np.float32), inv_freq)
            return (jnp.asarray(np.cos(freqs) * concentration, jnp.float32), jnp.asarray(np.sin(freqs) * concentration, jnp.float32))

        def _apply_rope(x, cos, sin):
            x1, x2 = jnp.split(x, 2, axis=-1)
            return jnp.concatenate([x1 * cos - x2 * sin, x2 * cos + x1 * sin], axis=-1)
        Bv, Tv, _ = x.shape
        qkv = x @ qkv_w.T + qkv_b
        q = qkv[..., :N_HEADS * HEAD_DIM].reshape(Bv, Tv, N_KV, Q_MULT, HEAD_DIM)
        k = qkv[..., N_HEADS * HEAD_DIM:(N_HEADS + N_KV) * HEAD_DIM].reshape(Bv, Tv, N_KV, HEAD_DIM)
        v = qkv[..., (N_HEADS + N_KV) * HEAD_DIM:].reshape(Bv, Tv, N_KV, HEAD_DIM)
        cos, sin = _rope_cos_sin(Tv)
        q = _apply_rope(q, cos[:, None, None, :], sin[:, None, None, :])
        k = _apply_rope(k, cos[:, None, :], sin[:, None, :])
        logits = jnp.einsum('bqhmd,bkhd->bhmqk', q, k) * SM_SCALE
        i = jnp.arange(Tv)[:, None]
        j = jnp.arange(Tv)[None, :]
        mask = jnp.zeros((Tv, Tv), dtype=bool)
        if CAUSAL:
            mask = mask | (j > i)
        if SLIDING_WINDOW > 0:
            mask = mask | (j <= i - SLIDING_WINDOW)
        logits = jnp.where(mask, -jnp.inf, logits)
        m = jnp.max(logits, axis=-1, keepdims=True)
        e = jnp.exp(logits - m)
        s = sinks.reshape(N_KV, Q_MULT)[None, :, :, None, None]
        exp_sink = jnp.exp(s - m)
        w = e / (jnp.sum(e, axis=-1, keepdims=True) + exp_sink)
        out = jnp.einsum('bhmqk,bkhd->bqhmd', w, v).reshape(Bv, Tv, N_HEADS * HEAD_DIM)
        return out @ out_w.T + out_b

    def _L1_ffn_ref(x, gate_w, gate_b, w1, b1, w2, b2, w3, b3, ws1, bs1, ws2, bs2, ws3, bs3):
        import jax, jax.numpy as jnp
        import numpy as np
        E = 16
        D = 256
        H = 176
        HS = 2 * 176
        TOP_K = 6
        ROUTE_SCALE = 1.0
        shape = x.shape
        xf = x.reshape(-1, shape[-1])
        scores = xf @ gate_w.T
        probs = jax.nn.softmax(scores.astype(jnp.float32), axis=-1)
        biased = probs + gate_b
        _, idx = jax.lax.top_k(biased, TOP_K)
        weights = jnp.take_along_axis(probs, idx, axis=1) * ROUTE_SCALE
        weights = weights.astype(x.dtype)
        onehot = jax.nn.one_hot(idx, E, dtype=weights.dtype)
        cw = jnp.einsum('tk,tke->te', weights, onehot)

        def expert_step(y, params):
            W1, B1, W2, B2, W3, B3, c = params
            h = jax.nn.silu(xf @ W1.T + B1) * (xf @ W3.T + B3)
            out = h @ W2.T + B2
            return (y + c[:, None] * out, None)
        y0 = jnp.zeros_like(xf)
        y, _ = jax.lax.scan(expert_step, y0, (w1, b1, w2, b2, w3, b3, cw.T))
        z = jax.nn.silu(xf @ ws1.T + bs1) * (xf @ ws3.T + bs3) @ ws2.T + bs2
        return (y + z).reshape(shape)
    x = L0_attn_x
    xn = _layernorm(x, axis=-1)
    s = _L0_attn_ref(xn, L0_attn_Wq, L0_attn_bq, L0_attn_Wk, L0_attn_bk, L0_attn_Wv, L0_attn_bv, L0_attn_Wo, L0_attn_bo)
    g = _silu(_L0_ffn_ref(xn, L0_ffn_gate_w, L0_ffn_shared_wg, L0_ffn_shared_wu, L0_ffn_shared_wd, L0_ffn_exp_wg, L0_ffn_exp_wu, L0_ffn_exp_wd))
    x = x + s * g
    xn = _layernorm(x, axis=-1)
    s = _L1_attn_ref(xn, L1_attn_qkv_w, L1_attn_qkv_b, L1_attn_out_w, L1_attn_out_b, L1_attn_sinks)
    g = _silu(_L1_ffn_ref(xn, L1_ffn_gate_w, L1_ffn_gate_b, L1_ffn_w1, L1_ffn_b1, L1_ffn_w2, L1_ffn_b2, L1_ffn_w3, L1_ffn_b3, L1_ffn_ws1, L1_ffn_bs1, L1_ffn_ws2, L1_ffn_bs2, L1_ffn_ws3, L1_ffn_bs3))
    x = x + s * g
    return x

_drawn_inputs = setup_inputs


def setup_inputs(seed=0):
    import zlib

    import numpy as np

    out = dict(_drawn_inputs(seed))
    spreads = {'L0_attn_bq': (0.0, 0.8),
     'L0_attn_bk': (0.0, 2.0),
     'L0_attn_bv': (0.0, 0.8),
     'L0_attn_bo': (0.0, 0.8)}
    factors = {'L0_attn_Wq': 8.0,
     'L0_attn_Wk': 8.0,
     'L0_attn_Wv': 8.0,
     'L0_attn_Wo': 8.0,
     'L0_ffn_gate_w': 8.0,
     'L0_ffn_shared_wg': 8.0,
     'L0_ffn_shared_wu': 8.0,
     'L0_ffn_shared_wd': 8.0,
     'L0_ffn_exp_wg': 8.0,
     'L0_ffn_exp_wu': 8.0,
     'L0_ffn_exp_wd': 8.0,
     'L1_attn_qkv_w': 8.0,
     'L1_attn_qkv_b': 8.0,
     'L1_attn_out_w': 8.0,
     'L1_attn_out_b': 64.0,
     'L1_attn_sinks': 64.0,
     'L1_ffn_gate_w': 8.0,
     'L1_ffn_gate_b': 8.0,
     'L1_ffn_w1': 8.0,
     'L1_ffn_b1': 30.341,
     'L1_ffn_w2': 8.0,
     'L1_ffn_b2': 64.0,
     'L1_ffn_w3': 8.0,
     'L1_ffn_b3': 30.912,
     'L1_ffn_ws1': 8.0,
     'L1_ffn_bs1': 8.0,
     'L1_ffn_ws2': 8.0,
     'L1_ffn_bs2': 64.0,
     'L1_ffn_ws3': 8.0,
     'L1_ffn_bs3': 8.0}
    for name, (base, spread) in spreads.items():
        noise = np.random.default_rng([zlib.crc32(name.encode()), seed]).standard_normal(out[name].shape)
        drawn = base * np.exp(spread * noise) if base else spread * noise
        out[name] = jnp.asarray(drawn.astype(out[name].dtype))
    for name, factor in factors.items():
        out[name] = (out[name] * factor).astype(out[name].dtype)
    return out
```

```python
import math
from contextlib import ExitStack

import concourse.bass as bass
import numpy as np
from concourse import mybir

F32 = mybir.dt.float32
F32R = mybir.dt.float32r
BF16 = mybir.dt.bfloat16
ALU = mybir.AluOpType
ACT = mybir.ActivationFunctionType
AX = mybir.AxisListType

P = 128
B, T, D = 4, 256, 256
TOK = B * T
NT = TOK // P
KD = D // P
HALF = TOK // 2
H0, DH0 = 16, 128
G1, M1, DH1 = 8, 4, 64
WINDOW = 128
FF = 176
E = (8, 16)
TOPK = (2, 6)
NJ = tuple(-(-(e + 2) * FF // P) for e in E)
ROUTE_SCALE0 = 2.5
EPS = 1e-5
SCALE0 = 1.0 / math.sqrt(DH0)
MASKED = -1e30
PAD = -1e30
CHOSEN = 1e30
WQ, WKV, WOC, WFF, WQKV = 512, 1024, 1024, 896, 768
QKV1 = (M1 + 2) * DH1
QK1 = (M1 + 1) * DH1
UNITS = 8

N_Q0, N_KV0, N_OUT, N_QKV1 = 8, 8, 4, 8
AT_Q0 = 0
AT_KV0 = AT_Q0 + N_Q0
AT_OUT = (AT_KV0 + N_KV0, AT_KV0 + N_KV0 + N_OUT + NJ[0] + N_QKV1)
AT_FF = (AT_OUT[0] + N_OUT, AT_OUT[1] + N_OUT)
AT_QKV1 = AT_FF[0] + NJ[0]
assert all(n % 2 == 0 for n in (AT_KV0, *AT_OUT, *AT_FF, AT_QKV1))


def program(nc, x, wq0, wkv0, bq0, bk0, bv0, wo, bo, wff, b1, b3, b2, gates, gate_b,
            wqkv1, bqkv1, sinks, rope_cos, rope_sin, out):
    with ExitStack() as ctx:
        def sb(name, shape, dt=F32):
            return ctx.enter_context(nc.sbuf_tensor(name, shape, dt))

        sems = {}

        def sem(name):
            if name not in sems:
                sems[name] = ctx.enter_context(nc.semaphore(name))
            return sems[name]

        xres = sb("xres", [P, NT, D])
        xt_hi = sb("xt_hi", [P, KD, TOK], F32R)
        xt_lo = sb("xt_lo", [P, KD, TOK], F32R)
        raw = sb("raw", [P, 2, 1024])
        w_hi = sb("w_hi", [P, 2, 1024], F32R)
        w_lo = sb("w_lo", [P, 2, 1024], F32R)
        qo = sb("qo", [P, 16 * TOK])
        cw_t = sb("cw_t", [P, TOK], F32R)
        ident = sb("ident", [P, P])
        ident_r = sb("ident_r", [P, P], F32R)
        ident_b = sb("ident_b", [P, P], BF16)
        mask_b = sb("mask_b", [P, 2 * P], BF16)
        zeros_b = sb("zeros_b", [P, HALF], BF16)
        eps_c = sb("eps_c", [P, 1])
        warm = sb("warm", [P, 2])
        bq_c, bq_s, bk_c, bv_c = (sb(n, [P, H0]) for n in ("bq_c", "bq_s", "bk_c", "bv_c"))
        bo_c = sb("bo_c", [P, 2, KD])
        b1_c = [sb(f"b1_c{l}", [P, NJ[l]]) for l in (0, 1)]
        b3_c = [sb(f"b3_c{l}", [P, NJ[l]]) for l in (0, 1)]
        b2_f = sb("b2_f", [P, D])
        b2_hi = sb("b2_hi", [P, D], F32R)
        b2_st = sb("b2_st", [P, D], F32R)
        gate_f = sb("gate_f", [P, 2, KD * P])
        gate_hi = sb("gate_hi", [P, 2, KD * P], F32R)
        gate_lo = sb("gate_lo", [P, 2, KD * P], F32R)
        gate_b_c = sb("gate_b_c", [P, E[1]])
        bqkv_c = sb("bqkv_c", [P, G1 * QKV1])
        sinks_c = sb("sinks_c", [P, G1 * M1])
        cos_c = sb("cos_c", [P, 2, QK1])
        sin_c = sb("sin_c", [P, 2, QK1])
        stats = sb("stats", [P, NT, 6])
        mv = sb("mv", [P, NT, 2])
        std = sb("std", [P, NT])
        rstd = sb("rstd", [P, NT])
        lg = sb("lg", [P, NT, E[1]])
        val = sb("val", [P, NT, E[1] + 8])
        rep = sb("rep", [P, NT, E[1] + 8])
        top8 = sb("top8", [P, NT, 8])
        red = sb("red", [P, 4, NT])
        prob = sb("prob", [P, NT, E[1]])
        cw = sb("cw", [P, NT, E[1]])
        cw_s = sb("cw_s", [P, NT, P], F32R)
        negmax = sb("negmax", [P, 2, 2, 2])
        rsum = sb("rsum", [P, 2, 2, 2])
        rinv = sb("rinv", [P, 2, 2, 2])
        sink_d = sb("sink_d", [P, 2, 2, 2])
        sink_e = sb("sink_e", [P, 2, 2, 2])
        den = sb("den", [P, 2, 2, 2])
        vp = sb("vp", [P, NT, 3 * DH1])

        def group(**tiles):
            with ExitStack() as some:
                return [some.enter_context(nc.sbuf_tensor(n, shape, dt)) for n, (shape, dt) in tiles.items()]

        kt0, v0, qs, prb1, pt1 = group(
            kt0=([P, 2, TOK], F32), v0=([P, NT, 2 * DH0], F32), qs=([P, 2, T], F32),
            prb1=([P, 2, 1, 3 * P], F32), pt1=([P, 2, 1, 3 * P], F32))
        kt1, qt1, prb2, pt2, qkb, ra, rb, qkr = group(
            kt1=([P, 2, TOK], F32), qt1=([P, 2, TOK], F32), prb2=([P, 2, 2, 3 * P], F32), pt2=([P, 2, 2, 3 * P], F32),
            qkb=([P, 2, QK1], F32), ra=([P, 2, QK1], F32), rb=([P, 2, QK1], F32), qkr=([P, NT, QKV1], F32))
        with nc.sbuf_tensor("xn", [P, NT, D], F32) as xn, nc.sbuf_tensor("lg_t", [P, TOK], F32) as lg_t, \
                nc.sbuf_tensor("s_t", [P, KD, TOK], F32) as s_t:
            o_hi, o_lo, mask_f = group(o_hi=([P, 2, TOK], F32R), o_lo=([P, 2, TOK], F32R), mask_f=([P, 2 * P], F32))
            sg, hf, hw, h_hi, h_lo = group(
                sg=([P, 2, HALF], F32), hf=([P, 2, HALF], F32), hw=([P, 2, HALF], F32),
                h_hi=([P, 2, HALF], F32R), h_lo=([P, 2, HALF], F32R))
        prb, pt = {1: prb1, 2: prb2}, {1: pt1, 2: pt2}
        ps = ctx.enter_context(nc.psum_tensor("ps", [P, 8, 512], F32))

        s_x, s_small, s_out = sem("x_in"), sem("small_in"), sem("out_written")
        w_in = [sem("w_in0"), sem("w_in1")]
        w_half, w_split, w_used = sem("w_half"), sem("w_split"), sem("w_used")
        w_rest = sem("w_rest")
        NSMALL = 18

        def wait_apart(eng, semaphore, value):
            eng.wait_ge(semaphore, value)
            eng.sem_inc(sem("waits_apart"), 1)

        def load_chunk(sp, src, n_static, n, slot, width):
            if n_static is None or n_static >= 2:
                sp.wait_ge(w_split, n - 1)
            sp.dma_start(raw[:, slot, 0:width], src).then_inc(w_in[slot], 16)

        def split_chunk(pool, n_static, n, pair, slot, width, hi_only=0):
            pool.wait_ge(w_in[slot], pair * 16 + 16)
            if n_static is None or n_static >= 2:
                wait_apart(pool, w_used, n - 1)
            nc.gpsimd.tensor_copy(w_hi[:, slot, 0:width], raw[:, slot, 0:width]).then_inc(w_half, 1)
            pool.wait_ge(w_half, n + 1)
            nc.gpsimd.tensor_tensor(w_lo[:, slot, 0:width - hi_only], raw[:, slot, 0:width - hi_only],
                                    w_hi[:, slot, 0:width - hi_only].bitcast(F32), ALU.subtract).then_inc(w_split, 1)

        def mm3(dst, l_hi, l_lo, r_hi, r_lo, start, stop):
            nc.tensor.matmul(dst, l_hi, r_hi, start=start, stop=False)
            nc.tensor.matmul(dst, l_hi, r_lo, start=False, stop=False)
            return nc.tensor.matmul(dst, l_lo, r_hi, start=False, stop=stop)

        def proj(dst, slot, col, width, stride, half):
            for k in range(KD):
                c = col + k * stride
                last = mm3(dst, w_hi[:, slot, c:c + width], w_lo[:, slot, c:c + width],
                           xt_hi[:, k, half * HALF:(half + 1) * HALF],
                           xt_lo[:, k, half * HALF:(half + 1) * HALF], k == 0, k == KD - 1)
            return last

        def proj_tok(dst, slot, col, width, t):
            for k in range(KD):
                c = col + k * width
                last = mm3(dst, xt_hi[:, k, t * P:(t + 1) * P], xt_lo[:, k, t * P:(t + 1) * P],
                           w_hi[:, slot, c:c + width], w_lo[:, slot, c:c + width], k == 0, k == KD - 1)
            return last

        block = ctx.enter_context(nc.Block())

        @block.sync
        def _(sp):
            sp.dma_start(xres[:, :, :], x.rearrange("(t p) d -> p t d", p=P)).then_inc(s_x, 16)
            load_chunk(sp, wq0[0], 0, 0, 0, WQ)
            load_chunk(sp, wq0[1], 1, 1, 1, WQ)
            for dst, src in ((bq_c[:], bq0), (bk_c[:], bk0), (bv_c[:], bv0), (bo_c[:], bo),
                             (b1_c[0][:], b1[0]), (b1_c[1][:], b1[1]), (b3_c[0][:], b3[0]), (b3_c[1][:], b3[1]),
                             (b2_f[:], b2), (gate_f[:, 0, :], gates[0]), (gate_f[:, 1, :], gates[1]),
                             (gate_b_c[:], gate_b.to_broadcast([P, E[1]])),
                             (bqkv_c[:], bqkv1.to_broadcast([P, G1 * QKV1])),
                             (sinks_c[:], sinks.to_broadcast([P, G1 * M1])),
                             (cos_c[:, 0, :], rope_cos[0]), (cos_c[:, 1, :], rope_cos[1]),
                             (sin_c[:, 0, :], rope_sin[0]), (sin_c[:, 1, :], rope_sin[1])):
                sp.dma_start(dst, src).then_inc(s_small, 16)

            def stream(src, at, first, pairs, width, odd=0):
                with sp.Fori(first, pairs) as i:
                    for slot in (0, 1):
                        load_chunk(sp, src[bass.ds(i * 2 + slot, 1)].rearrange("a p n -> (a p) n"),
                                   None, i * 2 + (at + slot), slot, width)
                if odd:
                    load_chunk(sp, src[2 * pairs], None, at + 2 * pairs, 0, width)

            stream(wq0, AT_Q0, 1, N_Q0 // 2, WQ)
            stream(wkv0, AT_KV0, 0, N_KV0 // 2, WKV)
            stream(wo[0], AT_OUT[0], 0, N_OUT // 2, WOC)
            stream(wff[0], AT_FF[0], 0, NJ[0] // 2, WFF)
            stream(wqkv1, AT_QKV1, 0, N_QKV1 // 2, WQKV)
            stream(wo[1], AT_OUT[1], 0, 1, WOC)
            sp.wait_ge(w_rest, 2)
            stream(wo[1], AT_OUT[1], 1, N_OUT // 2, WOC)
            stream(wff[1], AT_FF[1], 0, NJ[1] // 2, WFF, odd=NJ[1] % 2)
            for half in (0, 1):
                sp.wait_ge(sem("res1"), 2 * half + 2)
                sp.dma_start(out.rearrange("(t p) d -> p t d", p=P)[:, half * 4:half * 4 + 4, :],
                             xres[:, half * 4:half * 4 + 4, :]).then_inc(s_out, 16)
            sp.wait_ge(s_out, 32)

        @block.gpsimd
        def _(pool):
            consts = sem("consts")
            nc.gpsimd.memset(ident[:], 0.0).then_inc(consts, 1)
            nc.gpsimd.memset(mask_f[:], 0.0).then_inc(consts, 1)
            nc.gpsimd.memset(eps_c[:], EPS).then_inc(consts, 1)
            pool.wait_ge(consts, 3)
            nc.gpsimd.affine_select(out=ident[:], in_=ident[:], compare_op=ALU.not_equal, fill=1.0,
                                    base=0, pattern=[[-1, P]], channel_multiplier=1).then_inc(consts, 1)
            nc.gpsimd.affine_select(out=mask_f[:, 0:P], in_=mask_f[:, 0:P], compare_op=ALU.is_gt, fill=MASKED,
                                    base=0, pattern=[[1, P]], channel_multiplier=-1).then_inc(consts, 1)
            nc.gpsimd.affine_select(out=mask_f[:, P:2 * P], in_=mask_f[:, P:2 * P], compare_op=ALU.is_ge, fill=MASKED,
                                    base=0, pattern=[[-1, P]], channel_multiplier=1).then_inc(consts, 1)
            pool.wait_ge(consts, 6)
            nc.gpsimd.tensor_copy(ident_r[:], ident[:]).then_inc(consts, 1)
            nc.gpsimd.tensor_copy(ident_b[:], ident[:]).then_inc(consts, 1)
            nc.gpsimd.tensor_copy(mask_b[:], mask_f[:]).then_inc(consts, 1)
            nc.gpsimd.memset(zeros_b[:], 0.0).then_inc(consts, 1)
            nc.gpsimd.memset(cw_s[:].bitcast(F32), 0.0).then_inc(consts, 1)
            nc.gpsimd.memset(vp[:], 0.0).then_inc(consts, 1)
            split_chunk(pool, 0, 0, 0, 0, WQ)
            split_chunk(pool, 1, 1, 0, 1, WQ)
            pool.wait_ge(s_small, 16 * NSMALL)
            nc.gpsimd.tensor_copy(gate_hi[:], gate_f[:]).then_inc(consts, 1)
            nc.gpsimd.tensor_copy(b2_hi[:], b2_f[:]).then_inc(consts, 1)
            pool.wait_ge(consts, 14)
            nc.gpsimd.tensor_tensor(gate_lo[:], gate_f[:], gate_hi[:].bitcast(F32), ALU.subtract).then_inc(consts, 1)
            nc.gpsimd.tensor_scalar(bq_s[:], bq_c[:], SCALE0, None, ALU.mult).then_inc(consts, 1)

            with pool.Fori(1, N_Q0 // 2) as i:
                for slot in (0, 1):
                    split_chunk(pool, None, i * 2 + slot, i, slot, WQ)

            def normalise(u, U, q0sem, parts):
                wait_apart(pool, sem(f"recip{parts}"), U + 1)
                for hh in range(parts):
                    for qt in (0, 1):
                        c = slice(0, P) if qt == 0 else slice(P, 3 * P)
                        last = nc.gpsimd.tensor_scalar(prb[parts][:, u % 2, hh, c], prb[parts][:, u % 2, hh, c],
                                                       rinv[:, u % 2, qt, hh:hh + 1], None, ALU.mult)
                last.then_inc(sem(f"normed{parts}"), 1)

            split_chunk(pool, None, AT_KV0, AT_KV0 // 2, 0, WKV)
            with pool.Fori(0, N_KV0 // 2) as i:
                for slot in (0, 1):
                    for v in range(-1, UNITS + 1):
                        if v + 1 < UNITS:
                            u = v + 1
                            U = i * 16 + (slot * 8 + u)
                            b, hh = u // 2, u % 2
                            if u == 0:
                                pool.wait_ge(sem("q0_evac_act"), N_Q0 * 2)
                                pool.wait_ge(sem("q0_evac_dve"), N_Q0 * 2)
                            if u >= 2:
                                pool.wait_ge(sem("scores1"), U - 1)
                            nc.gpsimd.tensor_copy(
                                qs[:, u % 2, :], qo[:, bass.ds(i * 4 * T + (b * H0 * T + (2 * slot + hh) * T), T)],
                            ).then_inc(sem("q_slot"), 1)
                        if v >= 1:
                            normalise(v - 1, i * 16 + (slot * 8 + v - 1), None, 1)
                        if v == 2:
                            n = AT_KV0 + slot + 1
                            split_chunk(pool, None, i * 2 + n, i + n // 2, 1 - slot, WKV)
            def splits(at, first, count, width, hi_only=0):
                j = first
                if j % 2:
                    split_chunk(pool, None, at + j, (at + j) // 2, 1, width, hi_only)
                    j += 1
                pairs = (count - j) // 2
                with pool.Fori(0, pairs) as i:
                    for slot in (0, 1):
                        split_chunk(pool, None, i * 2 + (at + j + slot), i + (at + j) // 2, slot, width, hi_only)
                j += 2 * pairs
                if j < count:
                    split_chunk(pool, None, at + j, (at + j) // 2, 0, width, hi_only)

            splits(AT_OUT[0], 1, N_OUT, WOC)
            splits(AT_FF[0], 0, NJ[0], WFF, P)

            split_chunk(pool, None, AT_QKV1, AT_QKV1 // 2, 0, WQKV)
            with pool.Fori(0, N_QKV1 // 2) as i:
                for slot in (0, 1):
                    for t in range(NT):
                        N = i * 16 + (slot * 8 + t)
                        pool.wait_ge(sem("rope_cos"), N + 1)
                        qv = qkb[:, t % 2, :].rearrange("p (h s d) -> p h s d", s=2, d=DH1 // 2)
                        rv = rb[:, t % 2, :].rearrange("p (h s d) -> p h s d", s=2, d=DH1 // 2)
                        sv = sin_c[:, t % 2, :].rearrange("p (h s d) -> p h s d", s=2, d=DH1 // 2)
                        for s in (0, 1):
                            nc.gpsimd.tensor_tensor(rv[:, :, s, :], qv[:, :, 1 - s, :], sv[:, :, s, :],
                                                    ALU.mult).then_inc(sem("rope_sin"), 1)
                        pool.wait_ge(sem("rope_sin"), i * 32 + (slot * 16 + 2 * t + 2))
                        nc.gpsimd.tensor_tensor(qkr[:, t, 0:QK1], ra[:, t % 2, :], rb[:, t % 2, :], ALU.add)\
                            .then_inc(sem("rope_sum"), 1)
                        nc.gpsimd.tensor_tensor(qkr[:, t, QK1:QKV1], ra[:, t % 2, M1 * DH1:QK1], rb[:, t % 2, M1 * DH1:QK1],
                                                ALU.add).then_inc(sem("roped"), 1)
                    for v in range(1, UNITS + 1):
                        normalise(v - 1, i * 16 + (slot * 8 + v - 1), None, 2)
                        if v == 2:
                            n = AT_QKV1 + slot + 1
                            split_chunk(pool, None, i * 2 + n, i + n // 2, 1 - slot, WQKV)
            nc.gpsimd.tensor_copy(w_hi[:, 0, WQKV:WOC], raw[:, 0, WQKV:WOC]).then_inc(w_rest, 1)
            pool.wait_ge(w_rest, 1)
            nc.gpsimd.tensor_tensor(w_lo[:, 0, WQKV:WOC], raw[:, 0, WQKV:WOC],
                                    w_hi[:, 0, WQKV:WOC].bitcast(F32), ALU.subtract).then_inc(w_rest, 1)
            splits(AT_OUT[1], 1, N_OUT, WOC)
            splits(AT_FF[1], 0, NJ[1], WFF, P)

        @block.tensor
        def _(pe):
            def norm_and_logits(l):
                pe.wait_ge(sem("consts"), 16)
                for t in range(NT):
                    pe.wait_ge(sem(f"xn{l}"), t + 1)
                    for k in range(KD):
                        last = nc.tensor.transpose(ps[:, k + 2 * (t // 4), (t % 4) * P:(t % 4 + 1) * P],
                                                   xn[:, t, k * P:(k + 1) * P], ident[:])
                    if t % 4 == 3:
                        last.then_inc(sem(f"xn_t{l}"), 1)
                for half in (0, 1):
                    pe.wait_ge(sem(f"xt{l}"), 2 * half + 2)
                    for k in range(KD):
                        g = slice(k * P, (k + 1) * P)
                        r = slice(half * HALF, (half + 1) * HALF)
                        last = mm3(ps[:, 4 + half, :], gate_hi[:, l, g], gate_lo[:, l, g],
                                   xt_hi[:, k, r], xt_lo[:, k, r], k == 0, k == KD - 1)
                    last.then_inc(sem(f"lg{l}"), 1)
                for half in (0, 1):
                    pe.wait_ge(sem(f"lg_t{l}"), half + 1)
                    for t in range(4):
                        last = nc.tensor.transpose(ps[:, 6 + half, t * P:(t + 1) * P],
                                                   lg_t[:, (half * 4 + t) * P:(half * 4 + t + 1) * P], ident[:])
                    last.then_inc(sem(f"lg_tok{l}"), 1)

            def transposes_of(u, U, parts, bank):
                pe.wait_ge(sem(f"normed{parts}"), U + 1)
                for hh in range(parts):
                    for c in range(3):
                        last = nc.tensor.transpose(ps[:, bank + hh, c * P:(c + 1) * P],
                                                   prb[parts][:, u % 2, hh, c * P:(c + 1) * P], ident[:])
                last.then_inc(sem(f"p_t{parts}"), 1)

            def out_projection(l):
                for bank in range(4):
                    nc.tensor.matmul(ps[:, bank, :], zeros_b[:, 0:P], zeros_b[:], start=True, stop=False)
                with pe.Fori(0, N_OUT // 2) as i:
                    for slot in (0, 1):
                        pe.wait_ge(w_split, i * 2 + (AT_OUT[l] + slot + 1))
                        if l == 1 and slot == 0:
                            pe.wait_ge(w_rest, 2)
                        for r in range(4):
                            pe.wait_ge(sem(f"o_split{l}"), i * 8 + (slot * 4 + r + 1))
                            for m in range(KD):
                                c = r * D + m * P
                                for half in (0, 1):
                                    h = slice(half * HALF, (half + 1) * HALF)
                                    last = mm3(ps[:, m + 2 * half, :], w_hi[:, slot, c:c + P], w_lo[:, slot, c:c + P],
                                               o_hi[:, r % 2, h], o_lo[:, r % 2, h], False, False)
                            last.then_inc(sem(f"o_used{l}") if r < 3 else w_used, 1)
                for bank in range(4):
                    last = nc.tensor.matmul(ps[:, bank, :], zeros_b[:, 0:P], zeros_b[:], start=False, stop=True)
                last.then_inc(sem(f"s_acc{l}"), 1)

            def experts(l):
                pe.wait_ge(sem(f"cw{l}"), 1)
                for t in range(NT):
                    last = nc.tensor.transpose(ps[:, 4 + t // 4, (t % 4) * P:(t % 4 + 1) * P].bitcast(F32R),
                                               cw_s[:, t, :], ident_r[:])
                last.then_inc(sem(f"cw_tp{l}"), 1)
                pe.wait_ge(sem(f"cw_t{l}"), 2)
                pe.wait_ge(sem("b2"), 2)
                pe.wait_ge(sem(f"s_t{l}"), 4)
                for half in (0, 1):
                    for m in range(KD):
                        if l == 1:
                            nc.tensor.matmul(ps[:, m + 2 * half, :], b2_st[:, m * P:(m + 1) * P],
                                             cw_t[:, half * HALF:(half + 1) * HALF], start=True, stop=False)
                        else:
                            nc.tensor.matmul(ps[:, m + 2 * half, :], zeros_b[:, 0:P], zeros_b[:], start=True, stop=False)

                def up(j, slot, half, st, first=False):
                    if half == 0:
                        pe.wait_ge(w_split, j + (AT_FF[l] + 1))
                    proj(ps[:, 4 if half == 0 else 7, :], slot, 0, P, P, half).then_inc(sem(f"g{l}"), 1)
                    if not first:
                        pe.wait_ge(sem(f"gu{l}"), st)
                    proj(ps[:, 5, :], slot, 2 * P, P, P, half).then_inc(sem(f"u{l}"), 1)
                    if not first:
                        pe.wait_ge(sem(f"gw{l}"), st)
                    nc.tensor.matmul(ps[:, 6, :], w_hi[:, slot, 6 * P:7 * P], cw_t[:, half * HALF:(half + 1) * HALF],
                                     start=True, stop=True).then_inc(sem(f"wr{l}"), 1)

                def down(slot, half, st, stop=False):
                    pe.wait_ge(sem(f"h_lo{l}"), st + 1)
                    for m in range(KD):
                        c = 4 * P + m * P
                        last = mm3(ps[:, m + 2 * half, :], w_hi[:, slot, c:c + P], w_lo[:, slot, c:c + P],
                                   h_hi[:, half, :], h_lo[:, half, :], False, stop)
                    last.then_inc(w_used if half else sem(f"h_used{l}"), 1)

                steps = 2 * NJ[l]
                loops = (steps - 1) // 4
                up(0, 0, 0, 0, first=True)
                def four(i):
                    for k in (1, 2, 3, 4):
                        st = i * 4 + k
                        jj = k // 2
                        up(i * 2 + jj, jj % 2, k % 2, st)
                        down(((k - 1) // 2) % 2, (k - 1) % 2, st - 1)
                with pe.Fori(0, loops) as i:
                    four(i)
                for st in range(4 * loops + 1, steps):
                    up(st // 2, (st // 2) % 2, st % 2, st)
                    down(((st - 1) // 2) % 2, (st - 1) % 2, st - 1, stop=st - 1 >= steps - 2)
                down(((steps - 1) // 2) % 2, 1, steps - 1, stop=True)

            def gate_and_back(l):
                for half in (0, 1):
                    pe.wait_ge(sem(f"prod{l}"), 2 * half + 2)
                    for t in range(4):
                        for m in range(KD):
                            c = (half * 4 + t) * P
                            last = nc.tensor.transpose(ps[:, 4 + half * 2 + t // 2, (t % 2) * D + m * P:(t % 2) * D + (m + 1) * P],
                                                       s_t[:, m, c:c + P], ident[:])
                        if t % 2:
                            last.then_inc(sem(f"prod_t{l}"), 1)

            norm_and_logits(0)
            def queries(i, first):
                for slot in (0, 1):
                    pe.wait_ge(w_split, i * 2 + (slot + 1))
                    for cc in (0, 1):
                        for half in (0, 1):
                            if not (first and slot == 0):
                                pe.wait_ge(sem("q0_evac_act" if half == 0 else "q0_evac_dve"), i * 4 + (slot * 2 + cc - 1))
                            last = proj(ps[:, cc * 2 + half, :], slot, cc * 2 * P, P, P, half)
                            last.then_inc(w_used if (cc, half) == (1, 1) else sem(f"q0_ps{half}"), 1)
            pe.wait_ge(sem("xt0"), 4)
            queries(0, True)
            with pe.Fori(1, N_Q0 // 2) as i:
                queries(i, False)

            with pe.Fori(0, N_KV0 // 2) as i:
                for slot in (0, 1):
                    base = slot * 8

                    def scores(u):
                        b, hh = u // 2, u % 2
                        U = i * 16 + (base + u)
                        pe.wait_ge(sem("q_slot"), U + 1)
                        if u == 0:
                            pe.wait_ge(sem("k0"), i * 8 + (slot * 4 + 4))
                        if u >= 2:
                            pe.wait_ge(sem("exp1"), U - 1)
                        bank = u % 2
                        nc.tensor.matmul(ps[:, bank, 0:P], qs[:, u % 2, 0:P], kt0[:, hh, b * T:b * T + P], start=True, stop=False)
                        nc.tensor.matmul(ps[:, bank, 0:P], ident_b[:], mask_b[:, P:2 * P], start=False, stop=True)
                        nc.tensor.matmul(ps[:, bank, P:3 * P], qs[:, u % 2, P:T], kt0[:, hh, b * T:b * T + T], start=True, stop=False)
                        nc.tensor.matmul(ps[:, bank, 2 * P:3 * P], ident_b[:], mask_b[:, P:2 * P], start=False, stop=True)\
                            .then_inc(sem("scores1"), 1)

                    def heads_out(u):
                        b, hh = u // 2, u % 2
                        U = i * 16 + (base + u)
                        pe.wait_ge(sem("pt1"), U + 1)
                        if u >= 2:
                            pe.wait_ge(sem("o_evac1"), U - 1)
                        if u == 0:
                            pe.wait_ge(sem("v0"), i * 8 + (slot * 4 + 4))
                        bank = 4 + u % 2
                        nc.tensor.matmul(ps[:, bank, 0:T], v0[:, 2 * b, hh * P:(hh + 1) * P], pt1[:, u % 2, 0, 0:T],
                                         start=True, stop=False)
                        nc.tensor.matmul(ps[:, bank, P:T], v0[:, 2 * b + 1, hh * P:(hh + 1) * P], pt1[:, u % 2, 0, T:3 * P],
                                         start=False, stop=True).then_inc(sem("o_ps1"), 1)

                    pe.wait_ge(w_split, i * 2 + (AT_KV0 + slot + 1))
                    for n, (hh, half) in enumerate(((0, 0), (0, 1), (1, 0), (1, 1))):
                        if n >= 2:
                            pe.wait_ge(sem("k0"), i * 8 + (slot * 4 + n - 1))
                        proj(ps[:, 6 + n % 2, :], slot, hh * KD * P, P, P, half).then_inc(sem("k0_ps"), 1)
                    scores(0)
                    for n in range(NT // 2):
                        if n >= 2:
                            pe.wait_ge(sem("v0"), i * 8 + (slot * 4 + n - 1))
                        proj_tok(ps[:, 6 + n % 2, 0:T], slot, 4 * P, T, 2 * n)
                        proj_tok(ps[:, 6 + n % 2, T:2 * T], slot, 4 * P, T, 2 * n + 1)\
                            .then_inc(sem("v0_ps") if n < 3 else w_used, 1)
                    for v in range(1, UNITS + 2):
                        if v < UNITS:
                            scores(v)
                        if v - 1 < UNITS:
                            u = v - 1
                            U = i * 16 + (base + u)
                            if u >= 2:
                                pe.wait_ge(sem("pt1"), U - 1)
                            transposes_of(u, U, 1, 2 + u % 2)
                        if v >= 2:
                            heads_out(v - 2)
            pe.wait_ge(sem("o_evac1"), N_KV0 * UNITS)
            out_projection(0)
            experts(0)
            gate_and_back(0)

            norm_and_logits(1)
            pe.wait_ge(sem("xt1"), 4)
            with pe.Fori(0, N_QKV1 // 2) as i:
                for slot in (0, 1):
                    base = slot * 8

                    def tok_projection(t):
                        if t >= 2:
                            pe.wait_ge(sem("qkv1"), i * 16 + (base + t - 1))
                        proj_tok(ps[:, t % 2, 0:QKV1], slot, 0, QKV1, t)\
                            .then_inc(sem("qkv1_ps") if t < NT - 1 else w_used, 1)

                    def tok_transposes(t):
                        pe.wait_ge(sem("roped"), i * 16 + (base + t + 1))
                        if t == 4:
                            pe.wait_ge(sem("qt1"), i * 8 + (slot * 4 + 2))
                            pe.wait_ge(sem("kt1"), i * 8 + (slot * 4 + 2))
                        for c in range(3):
                            last = nc.tensor.transpose(ps[:, 2 + c, (t % 4) * P:(t % 4 + 1) * P],
                                                       qkr[:, t, c * P:(c + 1) * P], ident[:])
                        if t % 4 == 3:
                            last.then_inc(sem("qk_t"), 1)

                    def scores(u):
                        b, pr = u // 2, u % 2
                        U = i * 16 + (base + u)
                        if u == 0:
                            pe.wait_ge(sem("qt1"), i * 8 + (slot * 4 + 4))
                            pe.wait_ge(sem("kt1"), i * 8 + (slot * 4 + 4))
                        if u >= 2:
                            pe.wait_ge(sem("exp2"), U - 1)
                        for hh in (0, 1):
                            bank = (u % 2) * 2 + hh
                            nc.tensor.matmul(ps[:, bank, 0:P], qt1[:, pr, b * T:b * T + P], kt1[:, hh, b * T:b * T + P],
                                             start=True, stop=False)
                            nc.tensor.matmul(ps[:, bank, 0:P], ident_b[:], mask_b[:, P:2 * P], start=False, stop=True)
                            nc.tensor.matmul(ps[:, bank, P:3 * P], qt1[:, pr, b * T + P:b * T + T], kt1[:, hh, b * T:b * T + T],
                                             start=True, stop=False)
                            last = nc.tensor.matmul(ps[:, bank, P:3 * P], ident_b[:], mask_b[:, :], start=False, stop=True)
                        last.then_inc(sem("scores2"), 1)

                    def heads_out(u):
                        b = u // 2
                        U = i * 16 + (base + u)
                        pe.wait_ge(sem("pt2"), U + 1)
                        if u >= 2:
                            pe.wait_ge(sem("o_evac2"), U - 1)
                        bank = 6 + u % 2
                        for n, hh in enumerate((0, 1)):
                            c = slice(DH1 * (1 - hh), DH1 * (1 - hh) + P)
                            nc.tensor.matmul(ps[:, bank, 0:T], vp[:, 2 * b, c], pt2[:, u % 2, hh, 0:T],
                                             start=n == 0, stop=False)
                            last = nc.tensor.matmul(ps[:, bank, P:T], vp[:, 2 * b + 1, c], pt2[:, u % 2, hh, T:3 * P],
                                                    start=False, stop=n == 1)
                        last.then_inc(sem("o_ps2"), 1)

                    pe.wait_ge(w_split, i * 2 + (AT_QKV1 + slot + 1))
                    for t in range(NT):
                        tok_projection(t)
                        if t >= 4:
                            tok_transposes(t - 4)
                    for t in range(4, NT):
                        tok_transposes(t)
                    for v in range(0, UNITS + 2):
                        if v < UNITS:
                            scores(v)
                        if 0 <= v - 1 < UNITS:
                            u = v - 1
                            U = i * 16 + (base + u)
                            if u >= 1:
                                pe.wait_ge(sem("pt2"), U)
                            transposes_of(u, U, 2, 4)
                        if v >= 2:
                            heads_out(v - 2)
            pe.wait_ge(sem("o_evac2"), N_QKV1 * UNITS)
            out_projection(1)
            experts(1)
            gate_and_back(1)

        @block.scalar
        def _(act):
            def load_table(func):
                nc.scalar.activation(warm[:, 1:2], warm[:, 0:1], func)

            def norm_and_logits(l):
                act.wait_ge(sem(f"mv{l}"), NT)
                nc.scalar.activation(std[:], mv[:, :, 1], ACT.Sqrt, bias=eps_c[:], scale=1.0).then_inc(sem(f"std{l}"), 1)
                for half in (0, 1):
                    act.wait_ge(sem(f"xn_t{l}"), half + 1)
                    for k in range(KD):
                        nc.scalar.activation(xt_hi[:, k, half * HALF:(half + 1) * HALF], ps[:, k + 2 * half, :], ACT.Copy)\
                            .then_inc(sem(f"xt_hi{l}"), 1)
                for half in (0, 1):
                    act.wait_ge(sem(f"lg{l}"), half + 1)
                    nc.scalar.activation(lg_t[:, half * HALF:(half + 1) * HALF], ps[:, 4 + half, :], ACT.Copy)\
                        .then_inc(sem(f"lg_t{l}"), 1)
                if l == 0:
                    act.wait_ge(sem("lg_tok0"), 2)
                    for half in (0, 1):
                        nc.scalar.activation(prob[:, half * 4:half * 4 + 4, 0:E[0]],
                                             ps[:, 6 + half, :].rearrange("p (t c) -> p t c", c=P)[:, :, 0:E[0]],
                                             ACT.Sigmoid).then_inc(sem("prob0"), 1)
                else:
                    act.wait_ge(sem("shifted"), 1)
                    nc.scalar.activation(prob[:], lg[:], ACT.Exp).then_inc(sem("prob1"), 1)

            def exps(u, U, parts):
                act.wait_ge(sem(f"max{parts}"), U + 1)
                if u >= 2:
                    act.wait_ge(sem(f"p_t{parts}"), U - 1)
                for hh in range(parts):
                    bank = u % 2 if parts == 1 else (u % 2) * 2 + hh
                    for qt in (0, 1):
                        c = slice(0, P) if qt == 0 else slice(P, 3 * P)
                        last = nc.scalar.activation(prb[parts][:, u % 2, hh, c], ps[:, bank, c], ACT.Exp,
                                                    bias=negmax[:, u % 2, qt, hh:hh + 1], scale=1.0,
                                                    accum_out=rsum[:, u % 2, qt, hh:hh + 1])
                if parts == 2:
                    last = nc.scalar.activation(sink_e[:, u % 2], sink_d[:, u % 2], ACT.Exp)
                last.then_inc(sem(f"exp{parts}"), 1)

            def evac_transposed(u, U, parts, bank):
                act.wait_ge(sem(f"p_t{parts}"), U + 1)
                if u >= 2:
                    act.wait_ge(sem(f"o_ps{parts}"), U - 1)
                nc.scalar.activation(pt[parts][:, u % 2, 0:parts, :], ps[:, bank:bank + parts, 0:3 * P], ACT.Copy)\
                    .then_inc(sem(f"pt{parts}"), 1)

            def out_projection(l):
                def high(i, r, first=False):
                    if first and r < 2:
                        act.wait_ge(sem(f"o_evac{l + 1}"), N_KV0 * UNITS)
                    else:
                        c, at = divmod(r - 2, 4)
                        if at < 3:
                            act.wait_ge(sem(f"o_used{l}"), i * 6 + (3 * c + at + 1))
                        else:
                            act.wait_ge(w_used, i * 2 + (AT_OUT[l] + c + 1))
                    nc.scalar.activation(o_hi[:, r % 2, :].rearrange("p (b t) -> p b t", b=B), heads(l, i, r), ACT.Copy)\
                        .then_inc(sem(f"o_hi{l}"), 1)
                for r in range(8):
                    high(0, r, first=True)
                with act.Fori(1, N_OUT // 2) as i:
                    for r in range(8):
                        high(i, r)
                act.wait_ge(sem(f"s_acc{l}"), 1)
                for half in (0, 1):
                    for m in range(KD):
                        nc.scalar.activation(s_t[:, m, half * HALF:(half + 1) * HALF], ps[:, m + 2 * half, :], ACT.Identity,
                                             bias=bo_c[:, l, m:m + 1], scale=1.0).then_inc(sem(f"s_t{l}"), 1)

            def experts(l):
                act.wait_ge(sem(f"cw_tp{l}"), 1)
                for half in (0, 1):
                    nc.scalar.activation(cw_t[:, half * HALF:(half + 1) * HALF], ps[:, 4 + half, :], ACT.Copy)\
                        .then_inc(sem(f"cw_t{l}"), 1)
                load_table(ACT.Silu)

                def silu(j, half, st):
                    if not (isinstance(st, int) and st < 2):
                        act.wait_ge(sem(f"gu{l}"), st - 1)
                    wait_apart(act, sem(f"g{l}"), st + 1)
                    nc.scalar.activation(sg[:, half, :], ps[:, 4 if half == 0 else 7, :], ACT.Silu,
                                         bias=b1_c[l][:, bass.ds(j, 1)], scale=1.0).then_inc(sem(f"silu{l}"), 1)

                def high(j, half, st):
                    act.wait_ge(sem(f"gw{l}"), st + 1)
                    if not (isinstance(st, int) and st < 2):
                        if half:
                            act.wait_ge(w_used, j + AT_FF[l])
                        else:
                            act.wait_ge(sem(f"h_used{l}"), j)
                    nc.scalar.activation(h_hi[:, half, :], hw[:, half, :], ACT.Copy).then_inc(sem(f"h_hi{l}"), 1)

                def four(i, first):
                    for k in range(4):
                        st = k if first else i * 4 + k
                        j = (0 if first else i * 2) + k // 2
                        silu(j, k % 2, st)
                        high(j, k % 2, st)
                four(0, True)
                steps = 2 * NJ[l]
                with act.Fori(1, steps // 4) as i:
                    four(i, False)
                for st in range(steps // 4 * 4, steps):
                    silu(st // 2, st % 2, st)
                    high(st // 2, st % 2, st)
                act.wait_ge(w_used, AT_FF[l] + NJ[l])
                for half in (0, 1):
                    for m in range(KD):
                        nc.scalar.activation(xn[:, half * 4 + m * 2:half * 4 + m * 2 + 2, :].rearrange("p a b -> p (a b)"),
                                             ps[:, m + 2 * half, :], ACT.Silu).then_inc(sem(f"gate{l}"), 1)

            def heads(l, i, r):
                if l == 0:
                    return qo[:].rearrange("p (b h t) -> p b h t", b=B, t=T)[:, :, bass.ds(i * 8 + r, 1), :]\
                        .rearrange("p b h t -> p b (h t)")
                return qo[:].rearrange("p (g n) -> p g n", n=TOK)[:, bass.ds(i * 8 + r, 1), :]\
                    .rearrange("p g (b t) -> p (g b) t", b=B)

            act.wait_ge(sem("consts"), 16)
            nc.scalar.activation(warm[:, 0:1], eps_c[:], ACT.Copy).then_inc(sem("warm"), 1)
            act.wait_ge(sem("warm"), 1)
            act.wait_ge(s_small, 16 * NSMALL)
            norm_and_logits(0)

            q_view = qo[:].rearrange("p (t c) -> p t c", c=H0)
            load_table(ACT.Exp)
            with act.Fori(0, N_Q0 // 2) as i:
                for c in range(4):
                    act.wait_ge(sem("q0_ps0"), i * 4 + (c + 1))
                    nc.scalar.activation(q_view[:, 0:HALF, bass.ds(i * 4 + c, 1)].rearrange("p t c -> p (t c)"), ps[:, (c % 2) * 2, :],
                                         ACT.Identity, bias=bq_s[:, bass.ds(i * 4 + c, 1)], scale=SCALE0)\
                        .then_inc(sem("q0_evac_act"), 1)
            with act.Fori(0, N_KV0 // 2) as i:
                for slot in (0, 1):
                    for n, (hh, half) in enumerate(((0, 0), (0, 1), (1, 0), (1, 1))):
                        wait_apart(act, sem("k0_ps"), i * 8 + (slot * 4 + n + 1))
                        nc.scalar.activation(kt0[:, hh, half * HALF:(half + 1) * HALF], ps[:, 6 + n % 2, :], ACT.Identity,
                                             bias=bk_c[:, bass.ds(i * 4 + (slot * 2 + hh), 1)], scale=1.0).then_inc(sem("k0"), 1)
                    for v in range(UNITS + 1):
                        if v < UNITS:
                            exps(v, i * 16 + (slot * 8 + v), 1)
                        if v >= 1:
                            evac_transposed(v - 1, i * 16 + (slot * 8 + v - 1), 1, 2 + (v - 1) % 2)
            out_projection(0)
            experts(0)

            norm_and_logits(1)
            load_table(ACT.Exp)
            with act.Fori(0, N_QKV1 // 2) as i:
                for slot in (0, 1):
                    for half in (0, 1):
                        act.wait_ge(sem("qk_t"), i * 4 + (slot * 2 + half + 1))
                        for c in (0, 1):
                            nc.scalar.activation(qt1[:, c, half * HALF:(half + 1) * HALF], ps[:, 2 + c, :], ACT.Copy)\
                                .then_inc(sem("qt1"), 1)
                    for v in range(UNITS + 1):
                        if v < UNITS:
                            exps(v, i * 16 + (slot * 8 + v), 2)
                        if v >= 1:
                            evac_transposed(v - 1, i * 16 + (slot * 8 + v - 1), 2, 4)
            out_projection(1)
            experts(1)

        @block.vector
        def _(dve):
            def heads(l, i, r):
                if l == 0:
                    return qo[:].rearrange("p (b h t) -> p b h t", b=B, t=T)[:, :, bass.ds(i * 8 + r, 1), :]\
                        .rearrange("p b h t -> p b (h t)")
                return qo[:].rearrange("p (g n) -> p g n", n=TOK)[:, bass.ds(i * 8 + r, 1), :]\
                    .rearrange("p g (b t) -> p (g b) t", b=B)

            def norm(l):
                for t in range(NT):
                    if l == 1 and t % 2 == 0:
                        dve.wait_ge(sem("res0"), t // 2 + 1)
                    nc.vector.bn_stats(stats[:, t, :], xres[:, t, :]).then_inc(sem(f"stats{l}"), 1)
                for t in range(NT):
                    dve.wait_ge(sem(f"stats{l}"), t + 1)
                    nc.vector.bn_aggr(mv[:, t, :], stats[:, t, :]).then_inc(sem(f"mv{l}"), 1)
                dve.wait_ge(sem(f"std{l}"), 1)
                nc.vector.reciprocal(rstd[:], std[:]).then_inc(sem(f"rstd{l}"), 1)
                dve.wait_ge(sem(f"rstd{l}"), 1)
                for t in range(NT):
                    nc.vector.tensor_scalar(xn[:, t, :], xres[:, t, :], mv[:, t, 0:1], rstd[:, t:t + 1],
                                            ALU.subtract, ALU.mult).then_inc(sem(f"xn{l}"), 1)
                for half in (0, 1):
                    for k in range(KD):
                        h = slice(half * HALF, (half + 1) * HALF)
                        dve.wait_ge(sem(f"xt_hi{l}"), 2 * half + k + 1)
                        nc.vector.tensor_tensor(xt_lo[:, k, h], ps[:, k + 2 * half, :], xt_hi[:, k, h].bitcast(F32),
                                                ALU.subtract).then_inc(sem(f"xt{l}"), 1)

            def route(l):
                e = E[l]
                chain = sem(f"route{l}")
                n = [0]

                def step(ins):
                    n[0] += 1
                    ins.then_inc(chain, 1)

                def settle():
                    dve.wait_ge(chain, n[0])

                sc = prob[:, :, 0:e]
                if l == 1:
                    dve.wait_ge(sem("lg_tok1"), 2)
                    for half in (0, 1):
                        src = ps[:, 6 + half, :].rearrange("p (t c) -> p t c", c=P)[:, :, 0:e]
                        step(nc.vector.tensor_copy(lg[:, half * 4:half * 4 + 4, :], src))
                    settle()
                    step(nc.vector.tensor_reduce(red[:, 0, :], lg[:], AX.X, ALU.max))
                    settle()
                    nc.vector.tensor_tensor(lg[:], lg[:], red[:, 0, :].unsqueeze(2).to_broadcast([P, NT, e]),
                                            ALU.subtract).then_inc(sem("shifted"), 1)
                    dve.wait_ge(sem("prob1"), 1)
                    step(nc.vector.tensor_reduce(red[:, 1, :], sc, AX.X, ALU.add))
                    settle()
                    step(nc.vector.reciprocal(red[:, 2, :], red[:, 1, :]))
                    settle()
                    step(nc.vector.tensor_tensor(sc, sc, red[:, 2, :].unsqueeze(2).to_broadcast([P, NT, e]), ALU.mult))
                    settle()
                    step(nc.vector.tensor_tensor(val[:, :, 0:e], sc, gate_b_c[:].unsqueeze(1).to_broadcast([P, NT, e]), ALU.add))
                else:
                    dve.wait_ge(sem("prob0"), 2)
                    step(nc.vector.tensor_copy(val[:, :, 0:e], sc))
                step(nc.vector.memset(val[:, :, e:e + 8], PAD))
                settle()
                for t in range(NT):
                    step(nc.vector.max(top8[:, t, :], val[:, t, 0:e + 8]))
                settle()
                step(nc.vector.memset(top8[:, :, TOPK[l]:8], PAD))
                settle()
                for t in range(NT):
                    step(nc.vector.match_replace(rep[:, t, 0:e + 8], top8[:, t, :], val[:, t, 0:e + 8], CHOSEN))
                settle()
                step(nc.vector.tensor_scalar(cw[:, :, 0:e], rep[:, :, 0:e], CHOSEN, None, ALU.is_equal))
                settle()
                step(nc.vector.tensor_tensor(cw[:, :, 0:e], cw[:, :, 0:e], sc, ALU.mult))
                settle()
                if l == 0:
                    step(nc.vector.tensor_reduce(red[:, 0, :], cw[:, :, 0:e], AX.X, ALU.add))
                    settle()
                    step(nc.vector.tensor_scalar(red[:, 1, :], red[:, 0, :], 1e-20, None, ALU.add))
                    settle()
                    step(nc.vector.reciprocal(red[:, 2, :], red[:, 1, :]))
                    settle()
                    step(nc.vector.tensor_tensor(cw[:, :, 0:e], cw[:, :, 0:e],
                                                 red[:, 2, :].unsqueeze(2).to_broadcast([P, NT, e]), ALU.mult))
                    settle()
                    step(nc.vector.tensor_scalar(cw[:, :, 0:e], cw[:, :, 0:e], ROUTE_SCALE0, None, ALU.mult))
                    settle()
                else:
                    step(nc.vector.memset(cw_s[:, :, 0:P].bitcast(F32), 0.0))
                    settle()
                for q in (0, 2):
                    step(nc.vector.tensor_copy(cw_s[:, :, 32 * q:32 * q + e], cw[:, :, 0:e]))
                    step(nc.vector.memset(cw_s[:, :, 32 * q + e:32 * q + e + 1].bitcast(F32), 1.0))
                settle()
                for q in (1, 3):
                    step(nc.vector.tensor_tensor(cw_s[:, :, 32 * q:32 * q + e], cw[:, :, 0:e],
                                                 cw_s[:, :, 0:e].bitcast(F32), ALU.subtract))
                settle()
                nc.vector.memset(red[:, 3, 0:1], 0.0).then_inc(sem(f"cw{l}"), 1)

            def maxima(u, U, parts, slot, i):
                dve.wait_ge(sem(f"scores{parts}"), U + 1)
                b0 = u % 2 if parts == 1 else (u % 2) * 2
                nc.vector.tensor_reduce(negmax[:, u % 2, 0, 0:parts], ps[:, b0:b0 + parts, 0:P], AX.X, ALU.max, negate=True)\
                    .then_inc(sem(f"negmax{parts}"), 1)
                last = nc.vector.tensor_reduce(negmax[:, u % 2, 1, 0:parts], ps[:, b0:b0 + parts, P:3 * P], AX.X, ALU.max,
                                               negate=True)
                if parts == 2:
                    last.then_inc(sem("negmax2"), 1)
                    dve.wait_ge(sem("negmax2"), U * 2 + 2)
                    if u >= 2:
                        dve.wait_ge(sem("exp2"), U - 1)
                    sk = sinks_c[:, bass.ds(i * 8 + (slot * 4 + (u % 2) * 2), 2)]
                    last = nc.vector.tensor_tensor(sink_d[:, u % 2], negmax[:, u % 2], sk.unsqueeze(1).to_broadcast([P, 2, 2]), ALU.add)
                last.then_inc(sem(f"max{parts}"), 1)

            def reciprocals(u, U, parts):
                dve.wait_ge(sem(f"exp{parts}"), U + 1)
                src = rsum[:, u % 2, :, 0:parts]
                if parts == 2:
                    nc.vector.tensor_tensor(den[:, u % 2], rsum[:, u % 2], sink_e[:, u % 2], ALU.add).then_inc(sem("den2"), 1)
                    dve.wait_ge(sem("den2"), U + 1)
                    src = den[:, u % 2]
                nc.vector.reciprocal(rinv[:, u % 2, :, 0:parts], src).then_inc(sem(f"recip{parts}"), 1)

            def out_projection(l):
                with dve.Fori(0, N_OUT // 2) as i:
                    for r in range(8):
                        dve.wait_ge(sem(f"o_hi{l}"), i * 8 + (r + 1))
                        nc.vector.tensor_tensor(o_lo[:, r % 2, :].rearrange("p (b t) -> p b t", b=B), heads(l, i, r),
                                                o_hi[:, r % 2, :].bitcast(F32).rearrange("p (b t) -> p b t", b=B), ALU.subtract)\
                            .then_inc(sem(f"o_split{l}"), 1)

            def experts(l):
                def step(j, half, st):
                    first = isinstance(st, int) and st < 2
                    dve.wait_ge(sem(f"silu{l}"), st + 1)
                    dve.wait_ge(sem(f"u{l}"), st + 1)
                    nc.vector.scalar_tensor_tensor(hf[:, half, :], ps[:, 5, :], b3_c[l][:, bass.ds(j, 1)], sg[:, half, :],
                                                   ALU.add, ALU.mult).then_inc(sem(f"gu{l}"), 1)
                    dve.wait_ge(sem(f"gu{l}"), st + 1)
                    dve.wait_ge(sem(f"wr{l}"), st + 1)
                    if not first:
                        dve.wait_ge(sem(f"h_hi{l}"), st - 1)
                    nc.vector.tensor_tensor(hw[:, half, :], ps[:, 6, :], hf[:, half, :], ALU.mult).then_inc(sem(f"gw{l}"), 1)
                    dve.wait_ge(sem(f"h_hi{l}"), st + 1)
                    nc.vector.tensor_tensor(h_lo[:, half, :], hw[:, half, :], h_hi[:, half, :].bitcast(F32), ALU.subtract)\
                        .then_inc(sem(f"h_lo{l}"), 1)

                def four(i, first):
                    for k in range(4):
                        step((0 if first else i * 2) + k // 2, k % 2, k if first else i * 4 + k)
                four(0, True)
                steps = 2 * NJ[l]
                with dve.Fori(1, steps // 4) as i:
                    four(i, False)
                for st in range(steps // 4 * 4, steps):
                    step(st // 2, st % 2, st)
                for half in (0, 1):
                    for m in range(KD):
                        dve.wait_ge(sem(f"gate{l}"), 2 * half + m + 1)
                        h = slice(half * HALF, (half + 1) * HALF)
                        nc.vector.tensor_tensor(s_t[:, m, h], s_t[:, m, h],
                                                xn[:, half * 4 + m * 2:half * 4 + m * 2 + 2, :].rearrange("p a b -> p (a b)"),
                                                ALU.mult).then_inc(sem(f"prod{l}"), 1)
                for n in range(4):
                    dve.wait_ge(sem(f"prod_t{l}"), n + 1)
                    xv = xres[:, 2 * n:2 * n + 2, :].rearrange("p a b -> p (a b)")
                    nc.vector.tensor_tensor(xv, xv, ps[:, 4 + n, :], ALU.add).then_inc(sem(f"res{l}"), 1)

            dve.wait_ge(s_x, 16)
            norm(0)
            dve.wait_ge(sem("consts"), 16)
            dve.wait_ge(s_small, 16 * NSMALL)
            nc.vector.tensor_copy(b2_st[0:64, :], b2_f[0:64, :]).then_inc(sem("b2"), 1)
            nc.vector.tensor_tensor(b2_st[64:P, :], b2_f[64:P, :], b2_hi[64:P, :].bitcast(F32), ALU.subtract)\
                .then_inc(sem("b2"), 1)
            route(0)
            q_view = qo[:].rearrange("p (t c) -> p t c", c=H0)
            with dve.Fori(0, N_Q0 // 2) as i:
                for c in range(4):
                    if c % 2:
                        dve.wait_ge(w_used, i * 2 + (AT_Q0 + c // 2 + 1))
                    else:
                        dve.wait_ge(sem("q0_ps1"), i * 2 + (c // 2 + 1))
                    nc.vector.tensor_scalar(q_view[:, HALF:TOK, bass.ds(i * 4 + c, 1)].rearrange("p t c -> p (t c)"),
                                            ps[:, (c % 2) * 2 + 1, :], bq_c[:, bass.ds(i * 4 + c, 1)], SCALE0, ALU.add,
                                            ALU.mult)\
                        .then_inc(sem("q0_evac_dve"), 1)

            with dve.Fori(0, N_KV0 // 2) as i:
                for slot in (0, 1):
                    def evac_out(u):
                        b, hh = u // 2, u % 2
                        dve.wait_ge(sem("o_ps1"), i * 16 + (slot * 8 + u + 1))
                        nc.vector.tensor_scalar(qo[:, bass.ds(i * 4 * T + (b * H0 * T + (2 * slot + hh) * T), T)],
                                                ps[:, 4 + u % 2, 0:T], bv_c[:, bass.ds(i * 4 + (slot * 2 + hh), 1)], None,
                                                ALU.add).then_inc(sem("o_evac1"), 1)
                    maxima(0, i * 16 + slot * 8, 1, slot, i)
                    for n in range(NT // 2):
                        if n < 3:
                            dve.wait_ge(sem("v0_ps"), i * 6 + (slot * 3 + n + 1))
                        else:
                            dve.wait_ge(w_used, i * 2 + (AT_KV0 + slot + 1))
                        nc.vector.tensor_copy(v0[:, 2 * n:2 * n + 2, :].rearrange("p a b -> p (a b)"), ps[:, 6 + n % 2, :])\
                            .then_inc(sem("v0"), 1)
                    for v in range(1, UNITS + 2):
                        if v < UNITS:
                            maxima(v, i * 16 + (slot * 8 + v), 1, slot, i)
                        if v - 1 < UNITS:
                            reciprocals(v - 1, i * 16 + (slot * 8 + v - 1), 1)
                        if v >= 2:
                            evac_out(v - 2)
            out_projection(0)
            experts(0)

            norm(1)
            route(1)
            nc.vector.memset(kt1[64:P, 0, :], 0.0)
            nc.vector.memset(kt1[0:64, 1, :], 0.0)
            with dve.Fori(0, N_QKV1 // 2) as i:
                for slot in (0, 1):
                    for t in range(NT):
                        N = i * 16 + (slot * 8 + t)
                        bias = bqkv_c[:, bass.ds(i * 2 * QKV1 + slot * QKV1, QKV1)]
                        if t < NT - 1:
                            dve.wait_ge(sem("qkv1_ps"), i * 14 + (slot * 7 + t + 1))
                        else:
                            dve.wait_ge(w_used, i * 2 + (AT_QKV1 + slot + 1))
                        if t >= 2:
                            dve.wait_ge(sem("roped"), N - 1)
                        nc.vector.tensor_tensor(qkb[:, t % 2, :], ps[:, t % 2, 0:QK1], bias[:, 0:QK1], ALU.add).then_inc(sem("qkb"), 1)
                        nc.vector.tensor_tensor(vp[:, t, DH1:2 * DH1], ps[:, t % 2, QK1:QKV1], bias[:, QK1:QKV1], ALU.add)\
                            .then_inc(sem("qkv1"), 1)
                        dve.wait_ge(sem("qkb"), N + 1)
                        nc.vector.tensor_tensor(ra[:, t % 2, :], qkb[:, t % 2, :], cos_c[:, t % 2, :], ALU.mult).then_inc(sem("rope_cos"), 1)
                    for half in (0, 1):
                        dve.wait_ge(sem("qk_t"), i * 4 + (slot * 2 + half + 1))
                        h = slice(half * HALF, (half + 1) * HALF)
                        for a in (0, 1):
                            r = slice(64 * a, 64 * a + 64)
                            nc.vector.tensor_copy(kt1[r, a, h], ps[r, 4, :]).then_inc(sem("kt1"), 1)

                    def evac_out(u):
                        b, pr = u // 2, u % 2
                        dve.wait_ge(sem("o_ps2"), i * 16 + (slot * 8 + u + 1))
                        nc.vector.tensor_copy(qo[:, bass.ds(i * 4 * TOK + ((2 * slot + pr) * TOK + b * T), T)], ps[:, 6 + u % 2, 0:T])\
                            .then_inc(sem("o_evac2"), 1)
                    for v in range(0, UNITS + 2):
                        if v < UNITS:
                            maxima(v, i * 16 + (slot * 8 + v), 2, slot, i)
                        if 0 <= v - 1 < UNITS:
                            reciprocals(v - 1, i * 16 + (slot * 8 + v - 1), 2)
                        if v >= 2:
                            evac_out(v - 2)
            out_projection(1)
            experts(1)


def rope_tables():
    theta, scaling, alpha, beta, icl = 150000.0, 32.0, 1.0, 32.0, 128
    d_half = DH1 // 2
    freq = theta ** (np.arange(0, DH1, 2, dtype=np.float32) / DH1)
    concentration = 0.1 * math.log(scaling) + 1.0
    low = d_half * math.log(icl / (beta * 2 * math.pi)) / math.log(theta)
    high = d_half * math.log(icl / (alpha * 2 * math.pi)) / math.log(theta)
    ramp = np.clip((np.arange(d_half, dtype=np.float32) - low) / (high - low), 0.0, 1.0)
    mask = 1.0 - ramp
    inv_freq = 1.0 / (scaling * freq) * (1.0 - mask) + 1.0 / freq * mask
    freqs = np.outer(np.arange(T, dtype=np.float32), inv_freq)
    cos = np.asarray(np.cos(freqs) * concentration, np.float32)
    sin = np.asarray(np.sin(freqs) * concentration, np.float32)
    c = np.concatenate([cos, cos], 1)
    s = np.concatenate([-sin, sin], 1)
    q = np.float32(1.0 / math.sqrt(DH1))
    c = np.concatenate([c * q] * M1 + [c], 1).astype(np.float32)
    s = np.concatenate([s * q] * M1 + [s], 1).astype(np.float32)
    return c.reshape(2, P, QK1), s.reshape(2, P, QK1)


def selection(l):
    sel = np.zeros((NJ[l] * P, P), np.float32)
    for f in range((E[l] + 2) * FF):
        e = min(f // FF, E[l])
        sel[f, e] = sel[f, 32 + e] = 1.0
    return sel.reshape(NJ[l], P, P).transpose(0, 2, 1)


def rows(parts, l):
    width = parts[0].shape[-1]
    parts = [a.reshape(-1, width) for a in parts]
    have = sum(a.shape[0] for a in parts)
    return np.concatenate(parts + [np.zeros((NJ[l] * P - have, width), np.float32)], 0)


def pack_experts(l, gate, up, down):
    g, u, d = (rows(a, l) for a in (gate, up, down))

    def stationary(a):
        return a.reshape(NJ[l], P, KD, P).transpose(0, 3, 2, 1).reshape(NJ[l], P, KD * P)
    return np.concatenate([stationary(g), stationary(u), d.reshape(NJ[l], P, D), selection(l)], 2)


def columns(v, l):
    return rows([a.reshape(-1, 1) for a in v], l).reshape(NJ[l], P).T


def kernel(**inputs):
    import concourse.bacc as bacc
    from concourse.bass_utils import run_bass_kernel_spmd

    a = {k: np.asarray(v) for k, v in inputs.items()}
    f = lambda k: a[k]

    def by_pairs(w):
        return w.reshape(KD, P, 8, 2, P).transpose(2, 1, 3, 0, 4).reshape(8, P, 4 * P)

    def out_rows(w):
        return w.reshape(4, 4, P, D).transpose(0, 2, 1, 3).reshape(4, P, 4 * D)

    wv = f("L0_attn_Wv").reshape(KD, P, 8, 2 * P).transpose(2, 1, 0, 3).reshape(8, P, 4 * P)
    w1, b1 = f("L1_attn_qkv_w"), f("L1_attn_qkv_b")
    nq, nkv = G1 * M1 * DH1, G1 * DH1
    wg = np.concatenate([w1[:nq].reshape(G1, M1 * DH1, D), w1[nq:nq + nkv].reshape(G1, DH1, D),
                         w1[nq + nkv:].reshape(G1, DH1, D)], 1)
    bg = np.concatenate([b1[:nq].reshape(G1, M1 * DH1), b1[nq:nq + nkv].reshape(G1, DH1),
                         b1[nq + nkv:].reshape(G1, DH1)], 1)
    b2_rows = np.zeros((4, 32, D), np.float32)
    b2_rows[:, :E[1]] = f("L1_ffn_b2")
    b2_rows[:, E[1]] = f("L1_ffn_bs2")
    gates = np.zeros((2, KD, P, P), np.float32)
    for l, name in enumerate(("L0_ffn_gate_w", "L1_ffn_gate_w")):
        gates[l, :, :, :E[l]] = f(name).T.reshape(KD, P, E[l])
    t = lambda w: w.transpose(0, 2, 1)
    nothing = np.zeros(((E[0] + 2) * FF,), np.float32)
    cos, sin = rope_tables()
    arrays = {
        "x": f("L0_attn_x").reshape(TOK, D),
        "wq0": by_pairs(f("L0_attn_Wq")),
        "wkv0": np.concatenate([by_pairs(f("L0_attn_Wk")), wv], 2),
        "bq0": f("L0_attn_bq").reshape(H0, P).T, "bk0": f("L0_attn_bk").reshape(H0, P).T,
        "bv0": f("L0_attn_bv").reshape(H0, P).T,
        "wo_0": out_rows(f("L0_attn_Wo")), "wo_1": out_rows(f("L1_attn_out_w").T),
        "bo": np.stack([f("L0_attn_bo").reshape(KD, P).T, f("L1_attn_out_b").reshape(KD, P).T], 1),
        "wff_0": pack_experts(0, [f("L0_ffn_exp_wg"), f("L0_ffn_shared_wg")], [f("L0_ffn_exp_wu"), f("L0_ffn_shared_wu")],
                              [t(f("L0_ffn_exp_wd")), f("L0_ffn_shared_wd").T]),
        "wff_1": pack_experts(1, [f("L1_ffn_w1"), f("L1_ffn_ws1")], [f("L1_ffn_w3"), f("L1_ffn_ws3")],
                              [t(f("L1_ffn_w2")), f("L1_ffn_ws2").T]),
        "b1_0": columns([nothing], 0), "b3_0": columns([nothing], 0),
        "b1_1": columns([f("L1_ffn_b1"), f("L1_ffn_bs1")], 1), "b3_1": columns([f("L1_ffn_b3"), f("L1_ffn_bs3")], 1),
        "b2": b2_rows.reshape(P, D),
        "gates": gates.transpose(0, 2, 1, 3).reshape(2, P, KD * P),
        "gate_b": f("L1_ffn_gate_b").reshape(1, E[1]),
        "wqkv1": wg.reshape(G1, QKV1, KD, P).transpose(0, 3, 2, 1).reshape(G1, P, KD * QKV1),
        "bqkv1": bg.reshape(1, G1 * QKV1), "sinks": f("L1_attn_sinks").reshape(1, G1 * M1),
        "rope_cos": cos, "rope_sin": sin,
    }
    nc = bacc.Bacc("TRN2", target_bir_lowering=False, num_devices=1)
    ap, host = {}, {}
    for name, v in arrays.items():
        v = np.ascontiguousarray(v)
        host[f"in_{name}"] = v
        ap[name] = nc.dram_tensor(f"in_{name}", v.shape, mybir.dt.from_np(v.dtype), kind="ExternalInput").ap()
    out = nc.dram_tensor("out", (TOK, D), F32, kind="ExternalOutput").ap()
    program(nc, ap["x"], ap["wq0"], ap["wkv0"], ap["bq0"], ap["bk0"], ap["bv0"], (ap["wo_0"], ap["wo_1"]), ap["bo"],
            (ap["wff_0"], ap["wff_1"]), (ap["b1_0"], ap["b1_1"]), (ap["b3_0"], ap["b3_1"]), ap["b2"], ap["gates"],
            ap["gate_b"], ap["wqkv1"], ap["bqkv1"], ap["sinks"], ap["rope_cos"], ap["rope_sin"], out)
    r = run_bass_kernel_spmd(nc, [host], core_ids=[0])
    return r.results[0]["out"].reshape(B, T, D)
```

```python
import math
from contextlib import ExitStack

import concourse.bass as bass
import numpy as np
from concourse import mybir

F32 = mybir.dt.float32
F32R = mybir.dt.float32r
BF16 = mybir.dt.bfloat16
ALU = mybir.AluOpType
ACT = mybir.ActivationFunctionType
AX = mybir.AxisListType

P = 128
B, T, D = 4, 256, 256
TOK = B * T
NT = TOK // P
KD = D // P
HALF = TOK // 2
H0, DH0 = 16, 128
G1, M1, DH1 = 8, 4, 64
WINDOW = 128
FF = 176
E = (8, 16)
TOPK = (2, 6)
NJ = tuple(-(-(e + 2) * FF // P) for e in E)
ROUTE_SCALE0 = 2.5
EPS = 1e-5
SCALE0 = 1.0 / math.sqrt(DH0)
MASKED = -1e30
PAD = -1e30
CHOSEN = 1e30
WQ, WKV, WOC, WFF, WQKV = 512, 1024, 1024, 896, 768
QKV1 = (M1 + 2) * DH1
QK1 = (M1 + 1) * DH1
UNITS = 8

N_Q0, N_KV0, N_OUT, N_QKV1 = 8, 8, 4, 8
AT_Q0 = 0
AT_KV0 = AT_Q0 + N_Q0
AT_OUT = (AT_KV0 + N_KV0, AT_KV0 + N_KV0 + N_OUT + NJ[0] + N_QKV1)
AT_FF = (AT_OUT[0] + N_OUT, AT_OUT[1] + N_OUT)
AT_QKV1 = AT_FF[0] + NJ[0]
assert all(n % 2 == 0 for n in (AT_KV0, *AT_OUT, *AT_FF, AT_QKV1))


def program(nc, x, wq0, wkv0, bq0, bk0, bv0, wo, bo, wff, b1, b3, b2, gates, gate_b,
            wqkv1, bqkv1, sinks, rope_cos, rope_sin, out):
    with ExitStack() as ctx:
        def sb(name, shape, dt=F32):
            return ctx.enter_context(nc.sbuf_tensor(name, shape, dt))

        sems = {}

        def sem(name):
            if name not in sems:
                sems[name] = ctx.enter_context(nc.semaphore(name))
            return sems[name]

        xres = sb("xres", [P, NT, D])
        xt_hi = sb("xt_hi", [P, KD, TOK], F32R)
        xt_lo = sb("xt_lo", [P, KD, TOK], F32R)
        raw = sb("raw", [P, 2, 1024])
        w_hi = sb("w_hi", [P, 2, 1024], F32R)
        w_lo = sb("w_lo", [P, 2, 1024], F32R)
        qo = sb("qo", [P, 16 * TOK])
        cw_t = sb("cw_t", [P, TOK], F32R)
        ident = sb("ident", [P, P])
        ident_r = sb("ident_r", [P, P], F32R)
        ident_b = sb("ident_b", [P, P], BF16)
        mask_b = sb("mask_b", [P, 2 * P], BF16)
        zeros_b = sb("zeros_b", [P, HALF], BF16)
        eps_c = sb("eps_c", [P, 1])
        warm = sb("warm", [P, 2])
        bq_c, bq_s, bk_c, bv_c = (sb(n, [P, H0]) for n in ("bq_c", "bq_s", "bk_c", "bv_c"))
        bo_c = sb("bo_c", [P, 2, KD])
        b1_c = [sb(f"b1_c{l}", [P, NJ[l]]) for l in (0, 1)]
        b3_c = [sb(f"b3_c{l}", [P, NJ[l]]) for l in (0, 1)]
        b2_f = sb("b2_f", [P, D])
        b2_hi = sb("b2_hi", [P, D], F32R)
        b2_st = sb("b2_st", [P, D], F32R)
        gate_f = sb("gate_f", [P, 2, KD * P])
        gate_hi = sb("gate_hi", [P, 2, KD * P], F32R)
        gate_lo = sb("gate_lo", [P, 2, KD * P], F32R)
        gate_b_c = sb("gate_b_c", [P, E[1]])
        bqkv_c = sb("bqkv_c", [P, G1 * QKV1])
        sinks_c = sb("sinks_c", [P, G1 * M1])
        cos_c = sb("cos_c", [P, 2, QK1])
        sin_c = sb("sin_c", [P, 2, QK1])
        stats = sb("stats", [P, NT, 6])
        mv = sb("mv", [P, NT, 2])
        std = sb("std", [P, NT])
        rstd = sb("rstd", [P, NT])
        lg = sb("lg", [P, NT, E[1]])
        val = sb("val", [P, NT, E[1] + 8])
        rep = sb("rep", [P, NT, E[1] + 8])
        top8 = sb("top8", [P, NT, 8])
        red = sb("red", [P, 4, NT])
        prob = sb("prob", [P, NT, E[1]])
        cw = sb("cw", [P, NT, E[1]])
        cw_s = sb("cw_s", [P, NT, P], F32R)
        negmax = sb("negmax", [P, 2, 2, 2])
        rsum = sb("rsum", [P, 2, 2, 2])
        rinv = sb("rinv", [P, 2, 2, 2])
        sink_d = sb("sink_d", [P, 2, 2, 2])
        sink_e = sb("sink_e", [P, 2, 2, 2])
        den = sb("den", [P, 2, 2, 2])
        vp = sb("vp", [P, NT, 3 * DH1])

        def group(**tiles):
            with ExitStack() as some:
                return [some.enter_context(nc.sbuf_tensor(n, shape, dt)) for n, (shape, dt) in tiles.items()]

        kt0, v0, qs, prb1, pt1 = group(
            kt0=([P, 2, TOK], F32), v0=([P, NT, 2 * DH0], F32), qs=([P, 2, T], F32),
            prb1=([P, 2, 1, 3 * P], F32), pt1=([P, 2, 1, 3 * P], F32))
        kt1, qt1, prb2, pt2, qkb, ra, rb, qkr = group(
            kt1=([P, 2, TOK], F32), qt1=([P, 2, TOK], F32), prb2=([P, 2, 2, 3 * P], F32), pt2=([P, 2, 2, 3 * P], F32),
            qkb=([P, 2, QK1], F32), ra=([P, 2, QK1], F32), rb=([P, 2, QK1], F32), qkr=([P, 4, QKV1], F32))
        with nc.sbuf_tensor("xn", [P, NT, D], F32) as xn, nc.sbuf_tensor("lg_t", [P, TOK], F32) as lg_t, \
                nc.sbuf_tensor("s_t", [P, KD, TOK], F32) as s_t:
            o_hi, o_lo, mask_f = group(o_hi=([P, 2, TOK], F32R), o_lo=([P, 2, TOK], F32R), mask_f=([P, 2 * P], F32))
            sg, hf, hw, h_hi, h_lo = group(
                sg=([P, 2, HALF], F32), hf=([P, 2, HALF], F32), hw=([P, 2, HALF], F32),
                h_hi=([P, 2, HALF], F32R), h_lo=([P, 2, HALF], F32R))
        prb, pt = {1: prb1, 2: prb2}, {1: pt1, 2: pt2}
        ps = ctx.enter_context(nc.psum_tensor("ps", [P, 8, 512], F32))

        s_x, s_small, s_out = sem("x_in"), sem("small_in"), sem("out_written")
        w_in = [sem("w_in0"), sem("w_in1")]
        w_half, w_split, w_used = sem("w_half"), sem("w_split"), sem("w_used")
        w_rest = sem("w_rest")
        NSMALL = 18

        def wait_apart(eng, semaphore, value):
            eng.wait_ge(semaphore, value)
            eng.sem_inc(sem("waits_apart"), 1)

        def load_chunk(sp, src, n_static, n, slot, width):
            if n_static is None or n_static >= 2:
                sp.wait_ge(w_split, n - 1)
            sp.dma_start(raw[:, slot, 0:width], src).then_inc(w_in[slot], 16)

        def split_chunk(pool, n_static, n, pair, slot, width, hi_only=0):
            pool.wait_ge(w_in[slot], pair * 16 + 16)
            if n_static is None or n_static >= 2:
                wait_apart(pool, w_used, n - 1)
            nc.gpsimd.tensor_copy(w_hi[:, slot, 0:width], raw[:, slot, 0:width]).then_inc(w_half, 1)
            pool.wait_ge(w_half, n + 1)
            nc.gpsimd.tensor_tensor(w_lo[:, slot, 0:width - hi_only], raw[:, slot, 0:width - hi_only],
                                    w_hi[:, slot, 0:width - hi_only].bitcast(F32), ALU.subtract).then_inc(w_split, 1)

        def mm3(dst, l_hi, l_lo, r_hi, r_lo, start, stop):
            nc.tensor.matmul(dst, l_hi, r_hi, start=start, stop=False)
            nc.tensor.matmul(dst, l_hi, r_lo, start=False, stop=False)
            return nc.tensor.matmul(dst, l_lo, r_hi, start=False, stop=stop)

        def proj(dst, slot, col, width, stride, half):
            for k in range(KD):
                c = col + k * stride
                last = mm3(dst, w_hi[:, slot, c:c + width], w_lo[:, slot, c:c + width],
                           xt_hi[:, k, half * HALF:(half + 1) * HALF],
                           xt_lo[:, k, half * HALF:(half + 1) * HALF], k == 0, k == KD - 1)
            return last

        def proj_tok(dst, slot, col, width, t):
            for k in range(KD):
                c = col + k * width
                last = mm3(dst, xt_hi[:, k, t * P:(t + 1) * P], xt_lo[:, k, t * P:(t + 1) * P],
                           w_hi[:, slot, c:c + width], w_lo[:, slot, c:c + width], k == 0, k == KD - 1)
            return last

        def groups(eng, body):
            body(0, 0, first=True)
            with eng.Fori(0, N_KV0 // 2 - 1) as i:
                body(i * 2 + 1, 1)
                body(i * 2 + 2, 0)
            body(N_KV0 - 1, 1, last=True)

        block = ctx.enter_context(nc.Block())

        @block.sync
        def _(sp):
            sp.dma_start(xres[:, :, :], x.rearrange("(t p) d -> p t d", p=P)).then_inc(s_x, 16)
            load_chunk(sp, wq0[0], 0, 0, 0, WQ)
            load_chunk(sp, wq0[1], 1, 1, 1, WQ)
            for dst, src in ((bq_c[:], bq0), (bk_c[:], bk0), (bv_c[:], bv0), (bo_c[:], bo),
                             (b1_c[0][:], b1[0]), (b1_c[1][:], b1[1]), (b3_c[0][:], b3[0]), (b3_c[1][:], b3[1]),
                             (b2_f[:], b2), (gate_f[:, 0, :], gates[0]), (gate_f[:, 1, :], gates[1]),
                             (gate_b_c[:], gate_b.to_broadcast([P, E[1]])),
                             (bqkv_c[:], bqkv1.to_broadcast([P, G1 * QKV1])),
                             (sinks_c[:], sinks.to_broadcast([P, G1 * M1])),
                             (cos_c[:, 0, :], rope_cos[0]), (cos_c[:, 1, :], rope_cos[1]),
                             (sin_c[:, 0, :], rope_sin[0]), (sin_c[:, 1, :], rope_sin[1])):
                sp.dma_start(dst, src).then_inc(s_small, 16)

            def stream(src, at, first, pairs, width, odd=0):
                with sp.Fori(first, pairs) as i:
                    for slot in (0, 1):
                        load_chunk(sp, src[bass.ds(i * 2 + slot, 1)].rearrange("a p n -> (a p) n"),
                                   None, i * 2 + (at + slot), slot, width)
                if odd:
                    load_chunk(sp, src[2 * pairs], None, at + 2 * pairs, 0, width)

            stream(wq0, AT_Q0, 1, N_Q0 // 2, WQ)
            stream(wkv0, AT_KV0, 0, N_KV0 // 2, WKV)
            stream(wo[0], AT_OUT[0], 0, N_OUT // 2, WOC)
            stream(wff[0], AT_FF[0], 0, NJ[0] // 2, WFF)
            stream(wqkv1, AT_QKV1, 0, N_QKV1 // 2, WQKV)
            stream(wo[1], AT_OUT[1], 0, 1, WOC)
            sp.wait_ge(w_rest, 2)
            stream(wo[1], AT_OUT[1], 1, N_OUT // 2, WOC)
            stream(wff[1], AT_FF[1], 0, NJ[1] // 2, WFF, odd=NJ[1] % 2)
            for half in (0, 1):
                sp.wait_ge(sem("res1"), 2 * half + 2)
                sp.dma_start(out.rearrange("(t p) d -> p t d", p=P)[:, half * 4:half * 4 + 4, :],
                             xres[:, half * 4:half * 4 + 4, :]).then_inc(s_out, 16)
            sp.wait_ge(s_out, 32)

        @block.gpsimd
        def _(pool):
            consts = sem("consts")
            nc.gpsimd.memset(ident[:], 0.0).then_inc(consts, 1)
            nc.gpsimd.memset(mask_f[:], 0.0).then_inc(consts, 1)
            nc.gpsimd.memset(eps_c[:], EPS).then_inc(consts, 1)
            pool.wait_ge(consts, 3)
            nc.gpsimd.affine_select(out=ident[:], in_=ident[:], compare_op=ALU.not_equal, fill=1.0,
                                    base=0, pattern=[[-1, P]], channel_multiplier=1).then_inc(consts, 1)
            nc.gpsimd.affine_select(out=mask_f[:, 0:P], in_=mask_f[:, 0:P], compare_op=ALU.is_gt, fill=MASKED,
                                    base=0, pattern=[[1, P]], channel_multiplier=-1).then_inc(consts, 1)
            nc.gpsimd.affine_select(out=mask_f[:, P:2 * P], in_=mask_f[:, P:2 * P], compare_op=ALU.is_ge, fill=MASKED,
                                    base=0, pattern=[[-1, P]], channel_multiplier=1).then_inc(consts, 1)
            pool.wait_ge(consts, 6)
            nc.gpsimd.tensor_copy(ident_r[:], ident[:]).then_inc(consts, 1)
            nc.gpsimd.tensor_copy(ident_b[:], ident[:]).then_inc(consts, 1)
            nc.gpsimd.tensor_copy(mask_b[:], mask_f[:]).then_inc(consts, 1)
            nc.gpsimd.memset(zeros_b[:], 0.0).then_inc(consts, 1)
            nc.gpsimd.memset(cw_s[:].bitcast(F32), 0.0).then_inc(consts, 1)
            nc.gpsimd.memset(vp[:], 0.0).then_inc(consts, 1)
            split_chunk(pool, 0, 0, 0, 0, WQ)
            split_chunk(pool, 1, 1, 0, 1, WQ)
            pool.wait_ge(s_small, 16 * NSMALL)
            nc.gpsimd.tensor_copy(gate_hi[:], gate_f[:]).then_inc(consts, 1)
            nc.gpsimd.tensor_copy(b2_hi[:], b2_f[:]).then_inc(consts, 1)
            pool.wait_ge(consts, 14)
            nc.gpsimd.tensor_tensor(gate_lo[:], gate_f[:], gate_hi[:].bitcast(F32), ALU.subtract).then_inc(consts, 1)
            nc.gpsimd.tensor_scalar(bq_s[:], bq_c[:], SCALE0, None, ALU.mult).then_inc(consts, 1)

            with pool.Fori(1, N_Q0 // 2) as i:
                for slot in (0, 1):
                    split_chunk(pool, None, i * 2 + slot, i, slot, WQ)

            def split_high(n, pair, slot, width):
                pool.wait_ge(w_in[slot], pair * 16 + 16)
                wait_apart(pool, w_used, n - 1)
                nc.gpsimd.tensor_copy(w_hi[:, slot, 0:width], raw[:, slot, 0:width]).then_inc(w_half, 1)

            def split_low(n, slot, width):
                pool.wait_ge(w_half, n + 1)
                nc.gpsimd.tensor_tensor(w_lo[:, slot, 0:width], raw[:, slot, 0:width],
                                        w_hi[:, slot, 0:width].bitcast(F32), ALU.subtract).then_inc(w_split, 1)

            split_chunk(pool, None, AT_KV0, AT_KV0 // 2, 0, WKV)
            pool.wait_ge(sem("q0_evac_act"), N_Q0 * 2)
            pool.wait_ge(sem("q0_evac_dve"), N_Q0 * 2)

            def heads0(g, par, first=False, last=False):
                for v in range(UNITS):
                    b, hh = v // 2, v % 2
                    if not (first and v < 2):
                        wait_apart(pool, sem("scores1"), g * 8 + (v - 1))
                    nc.gpsimd.tensor_copy(qs[:, v % 2, :], qo[:, bass.ds(g * 2 * T + (b * H0 * T + hh * T), T)])\
                        .then_inc(sem("q_slot"), 1)
                    half = g // 2 if isinstance(g, int) else pool_i[0]
                    if v == 2:
                        split_high(g + (AT_KV0 + 1), half + AT_KV0 // 2 + (1 if par else 0), 1 - par, WKV)
                    if v == 3:
                        split_low(g + (AT_KV0 + 1), 1 - par, WKV)

            pool_i = [None]

            def groups_pool(body):
                body(0, 0, first=True)
                with pool.Fori(0, N_KV0 // 2 - 1) as i:
                    pool_i[0] = i
                    body(i * 2 + 1, 1)
                    pool_i[0] = i + 1
                    body(i * 2 + 2, 0)
                body(N_KV0 - 1, 1, last=True)

            groups_pool(heads0)

            def splits(at, first, count, width, hi_only=0):
                j = first
                if j % 2:
                    split_chunk(pool, None, at + j, (at + j) // 2, 1, width, hi_only)
                    j += 1
                pairs = (count - j) // 2
                with pool.Fori(0, pairs) as i:
                    for slot in (0, 1):
                        split_chunk(pool, None, i * 2 + (at + j + slot), i + (at + j) // 2, slot, width, hi_only)
                j += 2 * pairs
                if j < count:
                    split_chunk(pool, None, at + j, (at + j) // 2, 0, width, hi_only)

            splits(AT_OUT[0], 1, N_OUT, WOC)
            splits(AT_FF[0], 0, NJ[0], WFF, P)

            split_chunk(pool, None, AT_QKV1, AT_QKV1 // 2, 0, WQKV)

            def rope(g, t):
                N = g * 8 + t
                pool.wait_ge(sem("rope_cos"), N + 1)
                qv = qkb[:, t % 2, :].rearrange("p (h s d) -> p h s d", s=2, d=DH1 // 2)
                rv = rb[:, t % 2, :].rearrange("p (h s d) -> p h s d", s=2, d=DH1 // 2)
                sv = sin_c[:, t % 2, :].rearrange("p (h s d) -> p h s d", s=2, d=DH1 // 2)
                for s in (0, 1):
                    nc.gpsimd.tensor_tensor(rv[:, :, s, :], qv[:, :, 1 - s, :], sv[:, :, s, :],
                                            ALU.mult).then_inc(sem("rope_sin"), 1)
                pool.wait_ge(sem("rope_sin"), g * 16 + (2 * t + 2))
                nc.gpsimd.tensor_tensor(qkr[:, t % 4, 0:QK1], ra[:, t % 2, :], rb[:, t % 2, :], ALU.add)\
                    .then_inc(sem("rope_sum"), 1)
                nc.gpsimd.tensor_tensor(qkr[:, t % 4, QK1:QKV1], ra[:, t % 2, M1 * DH1:QK1], rb[:, t % 2, M1 * DH1:QK1],
                                        ALU.add).then_inc(sem("roped"), 1)

            for t in range(4):
                rope(0, t)

            def heads1(g, par, first=False, last=False):
                for v in range(UNITS):
                    if v < 4:
                        rope(g, v + 4)
                    elif not last:
                        rope(g + 1, v - 4)
                    half = g // 2 if isinstance(g, int) else pool_i[0]
                    if v == 0:
                        split_high(g + (AT_QKV1 + 1), half + AT_QKV1 // 2 + (1 if par else 0), 1 - par, WQKV)
                    if v == 1:
                        split_low(g + (AT_QKV1 + 1), 1 - par, WQKV)
            groups_pool(heads1)
            nc.gpsimd.tensor_copy(w_hi[:, 0, WQKV:WOC], raw[:, 0, WQKV:WOC]).then_inc(w_rest, 1)
            pool.wait_ge(w_rest, 1)
            nc.gpsimd.tensor_tensor(w_lo[:, 0, WQKV:WOC], raw[:, 0, WQKV:WOC],
                                    w_hi[:, 0, WQKV:WOC].bitcast(F32), ALU.subtract).then_inc(w_rest, 1)
            splits(AT_OUT[1], 1, N_OUT, WOC)
            splits(AT_FF[1], 0, NJ[1], WFF, P)

        @block.tensor
        def _(pe):
            def norm_and_logits(l):
                pe.wait_ge(sem("consts"), 16)
                for t in range(NT):
                    pe.wait_ge(sem(f"xn{l}"), t + 1)
                    for k in range(KD):
                        last = nc.tensor.transpose(ps[:, k + 2 * (t // 4), (t % 4) * P:(t % 4 + 1) * P],
                                                   xn[:, t, k * P:(k + 1) * P], ident[:])
                    if t % 4 == 3:
                        last.then_inc(sem(f"xn_t{l}"), 1)
                for half in (0, 1):
                    pe.wait_ge(sem(f"xt{l}"), 2 * half + 2)
                    for k in range(KD):
                        g = slice(k * P, (k + 1) * P)
                        r = slice(half * HALF, (half + 1) * HALF)
                        last = mm3(ps[:, 4 + half, :], gate_hi[:, l, g], gate_lo[:, l, g],
                                   xt_hi[:, k, r], xt_lo[:, k, r], k == 0, k == KD - 1)
                    last.then_inc(sem(f"lg{l}"), 1)
                for half in (0, 1):
                    pe.wait_ge(sem(f"lg_t{l}"), half + 1)
                    for t in range(4):
                        last = nc.tensor.transpose(ps[:, 6 + half, t * P:(t + 1) * P],
                                                   lg_t[:, (half * 4 + t) * P:(half * 4 + t + 1) * P], ident[:])
                    last.then_inc(sem(f"lg_tok{l}"), 1)

            def transposes_of(u, U, parts, bank):
                pe.wait_ge(sem(f"normed{parts}"), U + 1)
                for hh in range(parts):
                    for c in range(3):
                        last = nc.tensor.transpose(ps[:, bank + hh, c * P:(c + 1) * P],
                                                   prb[parts][:, u % 2, hh, c * P:(c + 1) * P], ident[:])
                last.then_inc(sem(f"p_t{parts}"), 1)

            def out_projection(l):
                for bank in range(4):
                    nc.tensor.matmul(ps[:, bank, :], zeros_b[:, 0:P], zeros_b[:], start=True, stop=False)
                with pe.Fori(0, N_OUT // 2) as i:
                    for slot in (0, 1):
                        pe.wait_ge(w_split, i * 2 + (AT_OUT[l] + slot + 1))
                        if l == 1 and slot == 0:
                            pe.wait_ge(w_rest, 2)
                        for r in range(4):
                            pe.wait_ge(sem(f"o_split{l}"), i * 8 + (slot * 4 + r + 1))
                            for m in range(KD):
                                c = r * D + m * P
                                for half in (0, 1):
                                    h = slice(half * HALF, (half + 1) * HALF)
                                    last = mm3(ps[:, m + 2 * half, :], w_hi[:, slot, c:c + P], w_lo[:, slot, c:c + P],
                                               o_hi[:, r % 2, h], o_lo[:, r % 2, h], False, False)
                            last.then_inc(sem(f"o_used{l}") if r < 3 else w_used, 1)
                for bank in range(4):
                    last = nc.tensor.matmul(ps[:, bank, :], zeros_b[:, 0:P], zeros_b[:], start=False, stop=True)
                last.then_inc(sem(f"s_acc{l}"), 1)

            def experts(l):
                pe.wait_ge(sem(f"cw{l}"), 1)
                for t in range(NT):
                    last = nc.tensor.transpose(ps[:, 4 + t // 4, (t % 4) * P:(t % 4 + 1) * P].bitcast(F32R),
                                               cw_s[:, t, :], ident_r[:])
                last.then_inc(sem(f"cw_tp{l}"), 1)
                pe.wait_ge(sem(f"cw_t{l}"), 2)
                pe.wait_ge(sem("b2"), 2)
                pe.wait_ge(sem(f"s_t{l}"), 4)
                for half in (0, 1):
                    for m in range(KD):
                        if l == 1:
                            nc.tensor.matmul(ps[:, m + 2 * half, :], b2_st[:, m * P:(m + 1) * P],
                                             cw_t[:, half * HALF:(half + 1) * HALF], start=True, stop=False)
                        else:
                            nc.tensor.matmul(ps[:, m + 2 * half, :], zeros_b[:, 0:P], zeros_b[:], start=True, stop=False)

                def up(j, slot, half, st, first=False):
                    if half == 0:
                        pe.wait_ge(w_split, j + (AT_FF[l] + 1))
                    proj(ps[:, 4 if half == 0 else 7, :], slot, 0, P, P, half).then_inc(sem(f"g{l}"), 1)
                    if not first:
                        pe.wait_ge(sem(f"gu{l}"), st)
                    proj(ps[:, 5, :], slot, 2 * P, P, P, half).then_inc(sem(f"u{l}"), 1)
                    if not first:
                        pe.wait_ge(sem(f"gw{l}"), st)
                    nc.tensor.matmul(ps[:, 6, :], w_hi[:, slot, 6 * P:7 * P], cw_t[:, half * HALF:(half + 1) * HALF],
                                     start=True, stop=True).then_inc(sem(f"wr{l}"), 1)

                def down(slot, half, st, stop=False):
                    pe.wait_ge(sem(f"h_lo{l}"), st + 1)
                    for m in range(KD):
                        c = 4 * P + m * P
                        last = mm3(ps[:, m + 2 * half, :], w_hi[:, slot, c:c + P], w_lo[:, slot, c:c + P],
                                   h_hi[:, half, :], h_lo[:, half, :], False, stop)
                    last.then_inc(w_used if half else sem(f"h_used{l}"), 1)

                steps = 2 * NJ[l]
                loops = (steps - 1) // 4
                up(0, 0, 0, 0, first=True)
                def four(i):
                    for k in (1, 2, 3, 4):
                        st = i * 4 + k
                        jj = k // 2
                        up(i * 2 + jj, jj % 2, k % 2, st)
                        down(((k - 1) // 2) % 2, (k - 1) % 2, st - 1)
                with pe.Fori(0, loops) as i:
                    four(i)
                for st in range(4 * loops + 1, steps):
                    up(st // 2, (st // 2) % 2, st % 2, st)
                    down(((st - 1) // 2) % 2, (st - 1) % 2, st - 1, stop=st - 1 >= steps - 2)
                down(((steps - 1) // 2) % 2, 1, steps - 1, stop=True)

            def gate_and_back(l):
                for half in (0, 1):
                    pe.wait_ge(sem(f"prod{l}"), 2 * half + 2)
                    for t in range(4):
                        for m in range(KD):
                            c = (half * 4 + t) * P
                            last = nc.tensor.transpose(ps[:, 4 + half * 2 + t // 2, (t % 2) * D + m * P:(t % 2) * D + (m + 1) * P],
                                                       s_t[:, m, c:c + P], ident[:])
                        if t % 2:
                            last.then_inc(sem(f"prod_t{l}"), 1)

            norm_and_logits(0)
            def queries(i, first):
                for slot in (0, 1):
                    pe.wait_ge(w_split, i * 2 + (slot + 1))
                    for cc in (0, 1):
                        for half in (0, 1):
                            if not (first and slot == 0):
                                pe.wait_ge(sem("q0_evac_act" if half == 0 else "q0_evac_dve"), i * 4 + (slot * 2 + cc - 1))
                            last = proj(ps[:, cc * 2 + half, :], slot, cc * 2 * P, P, P, half)
                            last.then_inc(w_used if (cc, half) == (1, 1) else sem(f"q0_ps{half}"), 1)
            pe.wait_ge(sem("xt0"), 4)
            queries(0, True)
            with pe.Fori(1, N_Q0 // 2) as i:
                queries(i, False)

            def keys0(g, par, hh, half, n, first=False):
                if not first:
                    pe.wait_ge(sem("k0"), g * 4 + n)
                proj(ps[:, 6, :], par, hh * KD * P, P, P, half).then_inc(sem("k0_ps"), 1)

            def values0(g, par, n, first=False):
                if not first:
                    pe.wait_ge(sem("v0"), g * 4 + n)
                proj_tok(ps[:, 7, 0:T], par, 4 * P, T, 2 * n)
                proj_tok(ps[:, 7, T:2 * T], par, 4 * P, T, 2 * n + 1).then_inc(sem("v0_ps") if n < 3 else w_used, 1)

            def scores0(g, v, first):
                b, hh = v // 2, v % 2
                pe.wait_ge(sem("q_slot"), g * 8 + (v + 1))
                if v in (0, 1, 4, 5):
                    pe.wait_ge(sem("k0"), g * 4 + (1 + hh + v // 4 * 2))
                if not (first and v < 2):
                    pe.wait_ge(sem("exp1"), g * 8 + (v - 1))
                bank = v % 2
                nc.tensor.matmul(ps[:, bank, 0:P], qs[:, bank, 0:P], kt0[:, hh, b * T:b * T + P], start=True, stop=False)
                nc.tensor.matmul(ps[:, bank, 0:P], ident_b[:], mask_b[:, P:2 * P], start=False, stop=True)
                nc.tensor.matmul(ps[:, bank, P:3 * P], qs[:, bank, P:T], kt0[:, hh, b * T:b * T + T], start=True, stop=False)
                nc.tensor.matmul(ps[:, bank, 2 * P:3 * P], ident_b[:], mask_b[:, P:2 * P], start=False, stop=True)\
                    .then_inc(sem("scores1"), 1)

            def heads_out0(g, v, first):
                b, hh = v % 8 // 2, v % 2
                pe.wait_ge(sem("pt1"), g * 8 + (v + 1))
                if not (first and v < 2):
                    pe.wait_ge(sem("o_evac1"), g * 8 + (v - 1))
                if hh == 0:
                    pe.wait_ge(sem("v0"), g * 4 + (v // 2 + 1))
                bank = 4 + v % 2
                nc.tensor.matmul(ps[:, bank, 0:T], v0[:, 2 * b, hh * P:(hh + 1) * P], pt1[:, v % 2, 0, 0:T],
                                 start=True, stop=False)
                nc.tensor.matmul(ps[:, bank, P:T], v0[:, 2 * b + 1, hh * P:(hh + 1) * P], pt1[:, v % 2, 0, T:3 * P],
                                 start=False, stop=True).then_inc(sem("o_ps1"), 1)

            def transposed0(g, v, first):
                if not (first and v < 2):
                    pe.wait_ge(sem("pt1"), g * 8 + (v - 1))
                transposes_of(v, g * 8 + v, 1, 2 + v % 2)

            pe.wait_ge(w_split, AT_KV0 + 1)
            keys0(0, 0, 0, 0, 0, first=True)
            keys0(0, 0, 1, 0, 1)
            values0(0, 0, 0, first=True)

            def heads0(g, par, first=False, last=False):
                for v in range(UNITS):
                    scores0(g, v, first)
                    if not (first and v < 2):
                        transposed0(g, v - 2, first)
                    if not (first and v < 3):
                        heads_out0(g, v - 3, first)
                    if v in (0, 2, 4):
                        values0(g, par, v // 2 + 1)
                    if v in (1, 3):
                        keys0(g, par, v // 2, 1, 2 + v // 2)
                    if v >= 5 and not last:
                        if v == 5:
                            pe.wait_ge(w_split, g + (AT_KV0 + 2))
                        if v < 7:
                            keys0(g, 1 - par, v - 5, 0, 4 + v - 5)
                        else:
                            values0(g + 1, 1 - par, 0)
            groups(pe, heads0)
            g = N_KV0 - 1
            transposed0(g, 6, False)
            heads_out0(g, 5, False)
            transposed0(g, 7, False)
            heads_out0(g, 6, False)
            heads_out0(g, 7, False)
            pe.wait_ge(sem("o_evac1"), N_KV0 * UNITS)
            out_projection(0)
            experts(0)
            gate_and_back(0)

            norm_and_logits(1)
            pe.wait_ge(sem("xt1"), 4)
            def projected1(g, par, t, first=False):
                if not first:
                    pe.wait_ge(sem("qkv1"), g * 8 + t)
                proj_tok(ps[:, 7, 0:QKV1], par, 0, QKV1, t).then_inc(sem("qkv1_ps") if t < NT - 1 else w_used, 1)

            def transposed_qk(g, b):
                pe.wait_ge(sem("roped"), g * 8 + (2 * b + 2))
                for t in (2 * b, 2 * b + 1):
                    for c in range(3):
                        at = (c % 2) * T + (t % 2) * P
                        last = nc.tensor.transpose(ps[:, 4 + c // 2, at:at + P], qkr[:, t % 4, c * P:(c + 1) * P], ident[:])
                last.then_inc(sem("qk_t"), 1)

            def scores1(g, v, first):
                b, pr = v // 2, v % 2
                if v % 2 == 0:
                    pe.wait_ge(sem("qt1"), g * 4 + (b + 1))
                    pe.wait_ge(sem("kt1"), g * 8 + (2 * b + 2))
                if not (first and v < 2):
                    pe.wait_ge(sem("exp2"), g * 8 + (v - 1))
                for hh in (0, 1):
                    bank = (v % 2) * 2 + hh
                    nc.tensor.matmul(ps[:, bank, 0:P], qt1[:, pr, b * T:b * T + P], kt1[:, hh, b * T:b * T + P],
                                     start=True, stop=False)
                    nc.tensor.matmul(ps[:, bank, 0:P], ident_b[:], mask_b[:, P:2 * P], start=False, stop=True)
                    nc.tensor.matmul(ps[:, bank, P:3 * P], qt1[:, pr, b * T + P:b * T + T], kt1[:, hh, b * T:b * T + T],
                                     start=True, stop=False)
                    last = nc.tensor.matmul(ps[:, bank, P:3 * P], ident_b[:], mask_b[:, :], start=False, stop=True)
                last.then_inc(sem("scores2"), 1)

            def transposed1(g, v, first, qk_done):
                if not (first and v < 1):
                    pe.wait_ge(sem("pt2"), g * 8 + v)
                pe.wait_ge(sem("qt1"), g * 4 + qk_done)
                pe.wait_ge(sem("kt1"), g * 8 + 2 * qk_done)
                transposes_of(v, g * 8 + v, 2, 4)

            def heads_out1(g, v, first):
                b = v % 8 // 2
                pe.wait_ge(sem("pt2"), g * 8 + (v + 1))
                if not (first and v < 1):
                    pe.wait_ge(sem("o_evac2"), g * 8 + v)
                for hh in (0, 1):
                    c = slice(DH1 * (1 - hh), DH1 * (1 - hh) + P)
                    nc.tensor.matmul(ps[:, 6, 0:T], vp[:, 2 * b, c], pt2[:, v % 2, hh, 0:T], start=hh == 0, stop=False)
                    last = nc.tensor.matmul(ps[:, 6, P:T], vp[:, 2 * b + 1, c], pt2[:, v % 2, hh, T:3 * P],
                                            start=False, stop=hh == 1)
                last.then_inc(sem("o_ps2"), 1)

            pe.wait_ge(w_split, AT_QKV1 + 1)
            pe.wait_ge(sem("shifted"), 1)
            for t in range(4):
                projected1(0, 0, t, first=t == 0)
            transposed_qk(0, 0)

            def heads1(g, par, first=False, last=False):
                for v in range(UNITS):
                    if v % 2 and not (last and v == 7):
                        if not (first and v < 3):
                            pe.wait_ge(sem("pt2"), g * 8 + (v - 2))
                        transposed_qk(g + 1 if v == 7 else g, (v + 1) // 2 % 4)
                    scores1(g, v, first)
                    if not (first and v < 2):
                        transposed1(g, v - 2, first, (v + 1) // 2 + (0 if last and v == 7 else 1))
                    if not (first and v < 3):
                        heads_out1(g, v - 3, first)
                    if v < 4:
                        projected1(g, par, v + 4)
                    elif not last:
                        if v == 4:
                            pe.wait_ge(w_split, g + (AT_QKV1 + 2))
                        projected1(g + 1, 1 - par, v - 4)
            groups(pe, heads1)
            g = N_QKV1 - 1
            transposed1(g, 6, False, 4)
            heads_out1(g, 5, False)
            transposed1(g, 7, False, 4)
            heads_out1(g, 6, False)
            heads_out1(g, 7, False)
            pe.wait_ge(sem("o_evac2"), N_QKV1 * UNITS)
            out_projection(1)
            experts(1)
            gate_and_back(1)

        @block.scalar
        def _(act):
            def load_table(func):
                nc.scalar.activation(warm[:, 1:2], warm[:, 0:1], func)

            def norm_and_logits(l):
                act.wait_ge(sem(f"mv{l}"), NT)
                nc.scalar.activation(std[:], mv[:, :, 1], ACT.Sqrt, bias=eps_c[:], scale=1.0).then_inc(sem(f"std{l}"), 1)
                for half in (0, 1):
                    act.wait_ge(sem(f"xn_t{l}"), half + 1)
                    for k in range(KD):
                        nc.scalar.activation(xt_hi[:, k, half * HALF:(half + 1) * HALF], ps[:, k + 2 * half, :], ACT.Copy)\
                            .then_inc(sem(f"xt_hi{l}"), 1)
                for half in (0, 1):
                    act.wait_ge(sem(f"lg{l}"), half + 1)
                    nc.scalar.activation(lg_t[:, half * HALF:(half + 1) * HALF], ps[:, 4 + half, :], ACT.Copy)\
                        .then_inc(sem(f"lg_t{l}"), 1)
                if l == 0:
                    act.wait_ge(sem("lg_tok0"), 2)
                    for half in (0, 1):
                        nc.scalar.activation(prob[:, half * 4:half * 4 + 4, 0:E[0]],
                                             ps[:, 6 + half, :].rearrange("p (t c) -> p t c", c=P)[:, :, 0:E[0]],
                                             ACT.Sigmoid).then_inc(sem("prob0"), 1)
                else:
                    act.wait_ge(sem("shifted"), 1)
                    nc.scalar.activation(prob[:], lg[:], ACT.Exp).then_inc(sem("prob1"), 1)

            def exps(g, u, parts, first):
                act.wait_ge(sem(f"max{parts}"), g * 8 + (u + 1))
                if not (first and u < 2):
                    act.wait_ge(sem(f"p_t{parts}"), g * 8 + (u - 1))
                for hh in range(parts):
                    bank = u % 2 if parts == 1 else (u % 2) * 2 + hh
                    for qt in (0, 1):
                        c = slice(0, P) if qt == 0 else slice(P, 3 * P)
                        last = nc.scalar.activation(prb[parts][:, u % 2, hh, c], ps[:, bank, c], ACT.Exp,
                                                    bias=negmax[:, u % 2, qt, hh:hh + 1], scale=1.0,
                                                    accum_out=rsum[:, u % 2, qt, hh:hh + 1])
                if parts == 2:
                    last = nc.scalar.activation(sink_e[:, u % 2], sink_d[:, u % 2], ACT.Exp)
                last.then_inc(sem(f"exp{parts}"), 1)

            def evac_transposed(g, u, parts, bank, first):
                act.wait_ge(sem(f"p_t{parts}"), g * 8 + (u + 1))
                if not (first and u < 2):
                    act.wait_ge(sem(f"o_ps{parts}"), g * 8 + (u - 1))
                nc.scalar.activation(pt[parts][:, u % 2, 0:parts, :], ps[:, bank:bank + parts, 0:3 * P], ACT.Copy)\
                    .then_inc(sem(f"pt{parts}"), 1)

            def out_projection(l):
                def high(i, r, first=False):
                    if first and r < 2:
                        act.wait_ge(sem(f"o_evac{l + 1}"), N_KV0 * UNITS)
                    else:
                        c, at = divmod(r - 2, 4)
                        if at < 3:
                            act.wait_ge(sem(f"o_used{l}"), i * 6 + (3 * c + at + 1))
                        else:
                            act.wait_ge(w_used, i * 2 + (AT_OUT[l] + c + 1))
                    nc.scalar.activation(o_hi[:, r % 2, :].rearrange("p (b t) -> p b t", b=B), heads(l, i, r), ACT.Copy)\
                        .then_inc(sem(f"o_hi{l}"), 1)
                for r in range(8):
                    high(0, r, first=True)
                with act.Fori(1, N_OUT // 2) as i:
                    for r in range(8):
                        high(i, r)
                act.wait_ge(sem(f"s_acc{l}"), 1)
                for half in (0, 1):
                    for m in range(KD):
                        nc.scalar.activation(s_t[:, m, half * HALF:(half + 1) * HALF], ps[:, m + 2 * half, :], ACT.Identity,
                                             bias=bo_c[:, l, m:m + 1], scale=1.0).then_inc(sem(f"s_t{l}"), 1)

            def experts(l):
                act.wait_ge(sem(f"cw_tp{l}"), 1)
                for half in (0, 1):
                    nc.scalar.activation(cw_t[:, half * HALF:(half + 1) * HALF], ps[:, 4 + half, :], ACT.Copy)\
                        .then_inc(sem(f"cw_t{l}"), 1)
                load_table(ACT.Silu)

                def silu(j, half, st):
                    if not (isinstance(st, int) and st < 2):
                        act.wait_ge(sem(f"gu{l}"), st - 1)
                    wait_apart(act, sem(f"g{l}"), st + 1)
                    nc.scalar.activation(sg[:, half, :], ps[:, 4 if half == 0 else 7, :], ACT.Silu,
                                         bias=b1_c[l][:, bass.ds(j, 1)], scale=1.0).then_inc(sem(f"silu{l}"), 1)

                def high(j, half, st):
                    act.wait_ge(sem(f"gw{l}"), st + 1)
                    if not (isinstance(st, int) and st < 2):
                        if half:
                            act.wait_ge(w_used, j + AT_FF[l])
                        else:
                            act.wait_ge(sem(f"h_used{l}"), j)
                    nc.scalar.activation(h_hi[:, half, :], hw[:, half, :], ACT.Copy).then_inc(sem(f"h_hi{l}"), 1)

                def four(i, first):
                    for k in range(4):
                        st = k if first else i * 4 + k
                        j = (0 if first else i * 2) + k // 2
                        silu(j, k % 2, st)
                        high(j, k % 2, st)
                four(0, True)
                steps = 2 * NJ[l]
                with act.Fori(1, steps // 4) as i:
                    four(i, False)
                for st in range(steps // 4 * 4, steps):
                    silu(st // 2, st % 2, st)
                    high(st // 2, st % 2, st)
                act.wait_ge(w_used, AT_FF[l] + NJ[l])
                for half in (0, 1):
                    for m in range(KD):
                        nc.scalar.activation(xn[:, half * 4 + m * 2:half * 4 + m * 2 + 2, :].rearrange("p a b -> p (a b)"),
                                             ps[:, m + 2 * half, :], ACT.Silu).then_inc(sem(f"gate{l}"), 1)

            def heads(l, i, r):
                if l == 0:
                    return qo[:].rearrange("p (b h t) -> p b h t", b=B, t=T)[:, :, bass.ds(i * 8 + r, 1), :]\
                        .rearrange("p b h t -> p b (h t)")
                return qo[:].rearrange("p (g n) -> p g n", n=TOK)[:, bass.ds(i * 8 + r, 1), :]\
                    .rearrange("p g (b t) -> p (g b) t", b=B)

            act.wait_ge(sem("consts"), 16)
            nc.scalar.activation(warm[:, 0:1], eps_c[:], ACT.Copy).then_inc(sem("warm"), 1)
            act.wait_ge(sem("warm"), 1)
            act.wait_ge(s_small, 16 * NSMALL)
            norm_and_logits(0)

            q_view = qo[:].rearrange("p (t c) -> p t c", c=H0)
            load_table(ACT.Exp)
            with act.Fori(0, N_Q0 // 2) as i:
                for c in range(4):
                    act.wait_ge(sem("q0_ps0"), i * 4 + (c + 1))
                    nc.scalar.activation(q_view[:, 0:HALF, bass.ds(i * 4 + c, 1)].rearrange("p t c -> p (t c)"), ps[:, (c % 2) * 2, :],
                                         ACT.Identity, bias=bq_s[:, bass.ds(i * 4 + c, 1)], scale=SCALE0)\
                        .then_inc(sem("q0_evac_act"), 1)

            def keys0(g, hh, half, n):
                wait_apart(act, sem("k0_ps"), g * 4 + (n + 1))
                nc.scalar.activation(kt0[:, hh, half * HALF:(half + 1) * HALF], ps[:, 6, :], ACT.Identity,
                                     bias=bk_c[:, bass.ds((g + n // 4) * 2 + hh, 1)], scale=1.0).then_inc(sem("k0"), 1)
            keys0(0, 0, 0, 0)
            keys0(0, 1, 0, 1)

            def heads0(g, par, first=False, last=False):
                for v in range(UNITS):
                    if not (first and v < 2):
                        evac_transposed(g, v - 2, 1, 2 + v % 2, first)
                    exps(g, v, 1, first)
                    if v in (1, 3):
                        keys0(g, v // 2, 1, 2 + v // 2)
                    if v in (5, 6) and not last:
                        keys0(g, v - 5, 0, 4 + v - 5)
            groups(act, heads0)
            for v in (6, 7):
                evac_transposed(N_KV0 - 1, v, 1, 2 + v % 2, False)
            out_projection(0)
            experts(0)

            norm_and_logits(1)
            load_table(ACT.Exp)

            def queries1(g, b):
                act.wait_ge(sem("qk_t"), g * 4 + (b + 1))
                nc.scalar.activation(qt1[:, :, b * T:(b + 1) * T], ps[:, 4, :].rearrange("p (c t) -> p c t", c=2), ACT.Copy)\
                    .then_inc(sem("qt1"), 1)
            queries1(0, 0)

            def heads1(g, par, first=False, last=False):
                for v in range(UNITS):
                    if v % 2 and not (last and v == 7):
                        queries1(g + 1 if v == 7 else g, (v + 1) // 2 % 4)
                    if not (first and v < 2):
                        evac_transposed(g, v - 2, 2, 4, first)
                    exps(g, v, 2, first)
            groups(act, heads1)
            for v in (6, 7):
                evac_transposed(N_QKV1 - 1, v, 2, 4, False)
            out_projection(1)
            experts(1)

        @block.vector
        def _(dve):
            def heads(l, i, r):
                if l == 0:
                    return qo[:].rearrange("p (b h t) -> p b h t", b=B, t=T)[:, :, bass.ds(i * 8 + r, 1), :]\
                        .rearrange("p b h t -> p b (h t)")
                return qo[:].rearrange("p (g n) -> p g n", n=TOK)[:, bass.ds(i * 8 + r, 1), :]\
                    .rearrange("p g (b t) -> p (g b) t", b=B)

            def norm(l):
                for t in range(NT):
                    if l == 1 and t % 2 == 0:
                        dve.wait_ge(sem("res0"), t // 2 + 1)
                    nc.vector.bn_stats(stats[:, t, :], xres[:, t, :]).then_inc(sem(f"stats{l}"), 1)
                for t in range(NT):
                    dve.wait_ge(sem(f"stats{l}"), t + 1)
                    nc.vector.bn_aggr(mv[:, t, :], stats[:, t, :]).then_inc(sem(f"mv{l}"), 1)
                dve.wait_ge(sem(f"std{l}"), 1)
                nc.vector.reciprocal(rstd[:], std[:]).then_inc(sem(f"rstd{l}"), 1)
                dve.wait_ge(sem(f"rstd{l}"), 1)
                for t in range(NT):
                    nc.vector.tensor_scalar(xn[:, t, :], xres[:, t, :], mv[:, t, 0:1], rstd[:, t:t + 1],
                                            ALU.subtract, ALU.mult).then_inc(sem(f"xn{l}"), 1)
                for half in (0, 1):
                    for k in range(KD):
                        h = slice(half * HALF, (half + 1) * HALF)
                        dve.wait_ge(sem(f"xt_hi{l}"), 2 * half + k + 1)
                        nc.vector.tensor_tensor(xt_lo[:, k, h], ps[:, k + 2 * half, :], xt_hi[:, k, h].bitcast(F32),
                                                ALU.subtract).then_inc(sem(f"xt{l}"), 1)

            def route(l):
                e = E[l]
                chain = sem(f"route{l}")
                n = [0]

                def step(ins):
                    n[0] += 1
                    ins.then_inc(chain, 1)

                def settle():
                    dve.wait_ge(chain, n[0])

                sc = prob[:, :, 0:e]
                if l == 1:
                    dve.wait_ge(sem("lg_tok1"), 2)
                    for half in (0, 1):
                        src = ps[:, 6 + half, :].rearrange("p (t c) -> p t c", c=P)[:, :, 0:e]
                        step(nc.vector.tensor_copy(lg[:, half * 4:half * 4 + 4, :], src))
                    settle()
                    step(nc.vector.tensor_reduce(red[:, 0, :], lg[:], AX.X, ALU.max))
                    settle()
                    nc.vector.tensor_tensor(lg[:], lg[:], red[:, 0, :].unsqueeze(2).to_broadcast([P, NT, e]),
                                            ALU.subtract).then_inc(sem("shifted"), 1)
                    dve.wait_ge(sem("prob1"), 1)
                    step(nc.vector.tensor_reduce(red[:, 1, :], sc, AX.X, ALU.add))
                    settle()
                    step(nc.vector.reciprocal(red[:, 2, :], red[:, 1, :]))
                    settle()
                    step(nc.vector.tensor_tensor(sc, sc, red[:, 2, :].unsqueeze(2).to_broadcast([P, NT, e]), ALU.mult))
                    settle()
                    step(nc.vector.tensor_tensor(val[:, :, 0:e], sc, gate_b_c[:].unsqueeze(1).to_broadcast([P, NT, e]), ALU.add))
                else:
                    dve.wait_ge(sem("prob0"), 2)
                    step(nc.vector.tensor_copy(val[:, :, 0:e], sc))
                step(nc.vector.memset(val[:, :, e:e + 8], PAD))
                settle()
                for t in range(NT):
                    step(nc.vector.max(top8[:, t, :], val[:, t, 0:e + 8]))
                settle()
                step(nc.vector.memset(top8[:, :, TOPK[l]:8], PAD))
                settle()
                for t in range(NT):
                    step(nc.vector.match_replace(rep[:, t, 0:e + 8], top8[:, t, :], val[:, t, 0:e + 8], CHOSEN))
                settle()
                step(nc.vector.tensor_scalar(cw[:, :, 0:e], rep[:, :, 0:e], CHOSEN, None, ALU.is_equal))
                settle()
                step(nc.vector.tensor_tensor(cw[:, :, 0:e], cw[:, :, 0:e], sc, ALU.mult))
                settle()
                if l == 0:
                    step(nc.vector.tensor_reduce(red[:, 0, :], cw[:, :, 0:e], AX.X, ALU.add))
                    settle()
                    step(nc.vector.tensor_scalar(red[:, 1, :], red[:, 0, :], 1e-20, None, ALU.add))
                    settle()
                    step(nc.vector.reciprocal(red[:, 2, :], red[:, 1, :]))
                    settle()
                    step(nc.vector.tensor_tensor(cw[:, :, 0:e], cw[:, :, 0:e],
                                                 red[:, 2, :].unsqueeze(2).to_broadcast([P, NT, e]), ALU.mult))
                    settle()
                    step(nc.vector.tensor_scalar(cw[:, :, 0:e], cw[:, :, 0:e], ROUTE_SCALE0, None, ALU.mult))
                    settle()
                else:
                    step(nc.vector.memset(cw_s[:, :, 0:P].bitcast(F32), 0.0))
                    settle()
                for q in (0, 2):
                    step(nc.vector.tensor_copy(cw_s[:, :, 32 * q:32 * q + e], cw[:, :, 0:e]))
                    step(nc.vector.memset(cw_s[:, :, 32 * q + e:32 * q + e + 1].bitcast(F32), 1.0))
                settle()
                for q in (1, 3):
                    step(nc.vector.tensor_tensor(cw_s[:, :, 32 * q:32 * q + e], cw[:, :, 0:e],
                                                 cw_s[:, :, 0:e].bitcast(F32), ALU.subtract))
                settle()
                nc.vector.memset(red[:, 3, 0:1], 0.0).then_inc(sem(f"cw{l}"), 1)

            def maxima(g, u, parts, first):
                U = g * 8 + u
                dve.wait_ge(sem(f"scores{parts}"), U + 1)
                b0 = u % 2 if parts == 1 else (u % 2) * 2
                nc.vector.tensor_reduce(negmax[:, u % 2, 0, 0:parts], ps[:, b0:b0 + parts, 0:P], AX.X, ALU.max, negate=True)\
                    .then_inc(sem(f"negmax{parts}"), 1)
                last = nc.vector.tensor_reduce(negmax[:, u % 2, 1, 0:parts], ps[:, b0:b0 + parts, P:3 * P], AX.X, ALU.max,
                                               negate=True)
                if parts == 2:
                    last.then_inc(sem("negmax2"), 1)
                    dve.wait_ge(sem("negmax2"), U * 2 + 2)
                    sk = sinks_c[:, bass.ds(g * 4 + (u % 2) * 2, 2)]
                    last = nc.vector.tensor_tensor(sink_d[:, u % 2], negmax[:, u % 2], sk.unsqueeze(1).to_broadcast([P, 2, 2]), ALU.add)
                last.then_inc(sem(f"max{parts}"), 1)

            def normalised(g, u, parts):
                U = g * 8 + u
                dve.wait_ge(sem(f"exp{parts}"), U + 1)
                src = rsum[:, u % 2, :, 0:parts]
                if parts == 2:
                    nc.vector.tensor_tensor(den[:, u % 2], rsum[:, u % 2], sink_e[:, u % 2], ALU.add).then_inc(sem("den2"), 1)
                    dve.wait_ge(sem("den2"), U + 1)
                    src = den[:, u % 2]
                nc.vector.reciprocal(rinv[:, u % 2, :, 0:parts], src).then_inc(sem(f"recip{parts}"), 1)
                dve.wait_ge(sem(f"recip{parts}"), U + 1)
                for hh in range(parts):
                    for qt in (0, 1):
                        c = slice(0, P) if qt == 0 else slice(P, 3 * P)
                        last = nc.vector.tensor_scalar(prb[parts][:, u % 2, hh, c], prb[parts][:, u % 2, hh, c],
                                                       rinv[:, u % 2, qt, hh:hh + 1], None, ALU.mult)
                last.then_inc(sem(f"normed{parts}"), 1)

            def out_projection(l):
                with dve.Fori(0, N_OUT // 2) as i:
                    for r in range(8):
                        dve.wait_ge(sem(f"o_hi{l}"), i * 8 + (r + 1))
                        nc.vector.tensor_tensor(o_lo[:, r % 2, :].rearrange("p (b t) -> p b t", b=B), heads(l, i, r),
                                                o_hi[:, r % 2, :].bitcast(F32).rearrange("p (b t) -> p b t", b=B), ALU.subtract)\
                            .then_inc(sem(f"o_split{l}"), 1)

            def experts(l):
                def step(j, half, st):
                    first = isinstance(st, int) and st < 2
                    dve.wait_ge(sem(f"silu{l}"), st + 1)
                    dve.wait_ge(sem(f"u{l}"), st + 1)
                    nc.vector.scalar_tensor_tensor(hf[:, half, :], ps[:, 5, :], b3_c[l][:, bass.ds(j, 1)], sg[:, half, :],
                                                   ALU.add, ALU.mult).then_inc(sem(f"gu{l}"), 1)
                    dve.wait_ge(sem(f"gu{l}"), st + 1)
                    dve.wait_ge(sem(f"wr{l}"), st + 1)
                    if not first:
                        dve.wait_ge(sem(f"h_hi{l}"), st - 1)
                    nc.vector.tensor_tensor(hw[:, half, :], ps[:, 6, :], hf[:, half, :], ALU.mult).then_inc(sem(f"gw{l}"), 1)
                    dve.wait_ge(sem(f"h_hi{l}"), st + 1)
                    nc.vector.tensor_tensor(h_lo[:, half, :], hw[:, half, :], h_hi[:, half, :].bitcast(F32), ALU.subtract)\
                        .then_inc(sem(f"h_lo{l}"), 1)

                def four(i, first):
                    for k in range(4):
                        step((0 if first else i * 2) + k // 2, k % 2, k if first else i * 4 + k)
                four(0, True)
                steps = 2 * NJ[l]
                with dve.Fori(1, steps // 4) as i:
                    four(i, False)
                for st in range(steps // 4 * 4, steps):
                    step(st // 2, st % 2, st)
                for half in (0, 1):
                    for m in range(KD):
                        dve.wait_ge(sem(f"gate{l}"), 2 * half + m + 1)
                        h = slice(half * HALF, (half + 1) * HALF)
                        nc.vector.tensor_tensor(s_t[:, m, h], s_t[:, m, h],
                                                xn[:, half * 4 + m * 2:half * 4 + m * 2 + 2, :].rearrange("p a b -> p (a b)"),
                                                ALU.mult).then_inc(sem(f"prod{l}"), 1)
                for n in range(4):
                    dve.wait_ge(sem(f"prod_t{l}"), n + 1)
                    xv = xres[:, 2 * n:2 * n + 2, :].rearrange("p a b -> p (a b)")
                    nc.vector.tensor_tensor(xv, xv, ps[:, 4 + n, :], ALU.add).then_inc(sem(f"res{l}"), 1)

            dve.wait_ge(s_x, 16)
            norm(0)
            dve.wait_ge(sem("consts"), 16)
            dve.wait_ge(s_small, 16 * NSMALL)
            nc.vector.tensor_copy(b2_st[0:64, :], b2_f[0:64, :]).then_inc(sem("b2"), 1)
            nc.vector.tensor_tensor(b2_st[64:P, :], b2_f[64:P, :], b2_hi[64:P, :].bitcast(F32), ALU.subtract)\
                .then_inc(sem("b2"), 1)
            route(0)
            q_view = qo[:].rearrange("p (t c) -> p t c", c=H0)
            with dve.Fori(0, N_Q0 // 2) as i:
                for c in range(4):
                    if c % 2:
                        dve.wait_ge(w_used, i * 2 + (AT_Q0 + c // 2 + 1))
                    else:
                        dve.wait_ge(sem("q0_ps1"), i * 2 + (c // 2 + 1))
                    nc.vector.tensor_scalar(q_view[:, HALF:TOK, bass.ds(i * 4 + c, 1)].rearrange("p t c -> p (t c)"),
                                            ps[:, (c % 2) * 2 + 1, :], bq_c[:, bass.ds(i * 4 + c, 1)], SCALE0, ALU.add,
                                            ALU.mult)\
                        .then_inc(sem("q0_evac_dve"), 1)


            def values0(g, n):
                if n < 3:
                    dve.wait_ge(sem("v0_ps"), g * 3 + (n + 1))
                else:
                    dve.wait_ge(w_used, g + (AT_KV0 + 1))
                nc.vector.tensor_copy(v0[:, 2 * n:2 * n + 2, :].rearrange("p a b -> p (a b)"), ps[:, 7, :]).then_inc(sem("v0"), 1)

            def results0(g, v):
                b, hh = v % 8 // 2, v % 2
                g_of, U = (g - 1 if v < 0 else g), g * 8 + v
                dve.wait_ge(sem("o_ps1"), U + 1)
                nc.vector.tensor_scalar(qo[:, bass.ds(g_of * 2 * T + (b * H0 * T + hh * T), T)], ps[:, 4 + v % 2, 0:T],
                                        bv_c[:, bass.ds(g_of * 2 + hh, 1)], None, ALU.add).then_inc(sem("o_evac1"), 1)
            values0(0, 0)

            def heads0(g, par, first=False, last=False):
                for v in range(UNITS):
                    maxima(g, v, 1, first)
                    if not (first and v < 1):
                        normalised(g, v - 1, 1)
                    if not (first and v < 3):
                        results0(g, v - 3)
                    if v in (0, 2, 4):
                        values0(g, v // 2 + 1)
                    if v == 7 and not last:
                        values0(g + 1, 0)
            groups(dve, heads0)
            normalised(N_KV0 - 1, 7, 1)
            for v in (5, 6, 7):
                results0(N_KV0 - 1, v)
            out_projection(0)
            experts(0)

            norm(1)
            route(1)
            nc.vector.memset(kt1[64:P, 0, :], 0.0)
            nc.vector.memset(kt1[0:64, 1, :], 0.0)

            def tile1(g, t):
                N = g * 8 + t
                if t < NT - 1:
                    dve.wait_ge(sem("qkv1_ps"), g * 7 + (t + 1))
                else:
                    dve.wait_ge(w_used, g + (AT_QKV1 + 1))
                if not (isinstance(g, int) and g == 0 and t < 2):
                    dve.wait_ge(sem("roped"), N - 1)
                bias = bqkv_c[:, bass.ds(g * QKV1, QKV1)]
                nc.vector.tensor_tensor(qkb[:, t % 2, :], ps[:, 7, 0:QK1], bias[:, 0:QK1], ALU.add).then_inc(sem("qkb"), 1)
                nc.vector.tensor_tensor(vp[:, t, DH1:2 * DH1], ps[:, 7, QK1:QKV1], bias[:, QK1:QKV1], ALU.add)\
                    .then_inc(sem("qkv1"), 1)
                dve.wait_ge(sem("qkb"), N + 1)
                nc.vector.tensor_tensor(ra[:, t % 2, :], qkb[:, t % 2, :], cos_c[:, t % 2, :], ALU.mult).then_inc(sem("rope_cos"), 1)

            def keys1(g, b):
                dve.wait_ge(sem("qk_t"), g * 4 + (b + 1))
                for a in (0, 1):
                    rows = slice(64 * a, 64 * a + 64)
                    nc.vector.tensor_copy(kt1[rows, a, b * T:(b + 1) * T], ps[rows, 5, 0:T]).then_inc(sem("kt1"), 1)

            def results1(g, v):
                b, pr = v % 8 // 2, v % 2
                g_of, U = (g - 1 if v < 0 else g), g * 8 + v
                dve.wait_ge(sem("o_ps2"), U + 1)
                nc.vector.tensor_copy(qo[:, bass.ds(g_of * 2 * TOK + (pr * TOK + b * T), T)], ps[:, 6, 0:T])\
                    .then_inc(sem("o_evac2"), 1)

            for t in range(4):
                tile1(0, t)
            keys1(0, 0)

            def heads1(g, par, first=False, last=False):
                for v in range(UNITS):
                    if v % 2 and not (last and v == 7):
                        keys1(g + 1 if v == 7 else g, (v + 1) // 2 % 4)
                    maxima(g, v, 2, first)
                    if not (first and v < 1):
                        normalised(g, v - 1, 2)
                    if not (first and v < 3):
                        results1(g, v - 3)
                    if v < 4:
                        tile1(g, v + 4)
                    elif not last:
                        tile1(g + 1, v - 4)
            groups(dve, heads1)
            normalised(N_QKV1 - 1, 7, 2)
            for v in (5, 6, 7):
                results1(N_QKV1 - 1, v)
            out_projection(1)
            experts(1)


def rope_tables():
    theta, scaling, alpha, beta, icl = 150000.0, 32.0, 1.0, 32.0, 128
    d_half = DH1 // 2
    freq = theta ** (np.arange(0, DH1, 2, dtype=np.float32) / DH1)
    concentration = 0.1 * math.log(scaling) + 1.0
    low = d_half * math.log(icl / (beta * 2 * math.pi)) / math.log(theta)
    high = d_half * math.log(icl / (alpha * 2 * math.pi)) / math.log(theta)
    ramp = np.clip((np.arange(d_half, dtype=np.float32) - low) / (high - low), 0.0, 1.0)
    mask = 1.0 - ramp
    inv_freq = 1.0 / (scaling * freq) * (1.0 - mask) + 1.0 / freq * mask
    freqs = np.outer(np.arange(T, dtype=np.float32), inv_freq)
    cos = np.asarray(np.cos(freqs) * concentration, np.float32)
    sin = np.asarray(np.sin(freqs) * concentration, np.float32)
    c = np.concatenate([cos, cos], 1)
    s = np.concatenate([-sin, sin], 1)
    q = np.float32(1.0 / math.sqrt(DH1))
    c = np.concatenate([c * q] * M1 + [c], 1).astype(np.float32)
    s = np.concatenate([s * q] * M1 + [s], 1).astype(np.float32)
    return c.reshape(2, P, QK1), s.reshape(2, P, QK1)


def selection(l):
    sel = np.zeros((NJ[l] * P, P), np.float32)
    for f in range((E[l] + 2) * FF):
        e = min(f // FF, E[l])
        sel[f, e] = sel[f, 32 + e] = 1.0
    return sel.reshape(NJ[l], P, P).transpose(0, 2, 1)


def rows(parts, l):
    width = parts[0].shape[-1]
    parts = [a.reshape(-1, width) for a in parts]
    have = sum(a.shape[0] for a in parts)
    return np.concatenate(parts + [np.zeros((NJ[l] * P - have, width), np.float32)], 0)


def pack_experts(l, gate, up, down):
    g, u, d = (rows(a, l) for a in (gate, up, down))

    def stationary(a):
        return a.reshape(NJ[l], P, KD, P).transpose(0, 3, 2, 1).reshape(NJ[l], P, KD * P)
    return np.concatenate([stationary(g), stationary(u), d.reshape(NJ[l], P, D), selection(l)], 2)


def columns(v, l):
    return rows([a.reshape(-1, 1) for a in v], l).reshape(NJ[l], P).T


def kernel(**inputs):
    import concourse.bacc as bacc
    from concourse.bass_utils import run_bass_kernel_spmd

    a = {k: np.asarray(v) for k, v in inputs.items()}
    f = lambda k: a[k]

    def by_pairs(w):
        return w.reshape(KD, P, 8, 2, P).transpose(2, 1, 3, 0, 4).reshape(8, P, 4 * P)

    def out_rows(w):
        return w.reshape(4, 4, P, D).transpose(0, 2, 1, 3).reshape(4, P, 4 * D)

    wv = f("L0_attn_Wv").reshape(KD, P, 8, 2 * P).transpose(2, 1, 0, 3).reshape(8, P, 4 * P)
    w1, b1 = f("L1_attn_qkv_w"), f("L1_attn_qkv_b")
    nq, nkv = G1 * M1 * DH1, G1 * DH1
    wg = np.concatenate([w1[:nq].reshape(G1, M1 * DH1, D), w1[nq:nq + nkv].reshape(G1, DH1, D),
                         w1[nq + nkv:].reshape(G1, DH1, D)], 1)
    bg = np.concatenate([b1[:nq].reshape(G1, M1 * DH1), b1[nq:nq + nkv].reshape(G1, DH1),
                         b1[nq + nkv:].reshape(G1, DH1)], 1)
    b2_rows = np.zeros((4, 32, D), np.float32)
    b2_rows[:, :E[1]] = f("L1_ffn_b2")
    b2_rows[:, E[1]] = f("L1_ffn_bs2")
    gates = np.zeros((2, KD, P, P), np.float32)
    for l, name in enumerate(("L0_ffn_gate_w", "L1_ffn_gate_w")):
        gates[l, :, :, :E[l]] = f(name).T.reshape(KD, P, E[l])
    t = lambda w: w.transpose(0, 2, 1)
    nothing = np.zeros(((E[0] + 2) * FF,), np.float32)
    cos, sin = rope_tables()
    arrays = {
        "x": f("L0_attn_x").reshape(TOK, D),
        "wq0": by_pairs(f("L0_attn_Wq")),
        "wkv0": np.concatenate([by_pairs(f("L0_attn_Wk")), wv], 2),
        "bq0": f("L0_attn_bq").reshape(H0, P).T, "bk0": f("L0_attn_bk").reshape(H0, P).T,
        "bv0": f("L0_attn_bv").reshape(H0, P).T,
        "wo_0": out_rows(f("L0_attn_Wo")), "wo_1": out_rows(f("L1_attn_out_w").T),
        "bo": np.stack([f("L0_attn_bo").reshape(KD, P).T, f("L1_attn_out_b").reshape(KD, P).T], 1),
        "wff_0": pack_experts(0, [f("L0_ffn_exp_wg"), f("L0_ffn_shared_wg")], [f("L0_ffn_exp_wu"), f("L0_ffn_shared_wu")],
                              [t(f("L0_ffn_exp_wd")), f("L0_ffn_shared_wd").T]),
        "wff_1": pack_experts(1, [f("L1_ffn_w1"), f("L1_ffn_ws1")], [f("L1_ffn_w3"), f("L1_ffn_ws3")],
                              [t(f("L1_ffn_w2")), f("L1_ffn_ws2").T]),
        "b1_0": columns([nothing], 0), "b3_0": columns([nothing], 0),
        "b1_1": columns([f("L1_ffn_b1"), f("L1_ffn_bs1")], 1), "b3_1": columns([f("L1_ffn_b3"), f("L1_ffn_bs3")], 1),
        "b2": b2_rows.reshape(P, D),
        "gates": gates.transpose(0, 2, 1, 3).reshape(2, P, KD * P),
        "gate_b": f("L1_ffn_gate_b").reshape(1, E[1]),
        "wqkv1": wg.reshape(G1, QKV1, KD, P).transpose(0, 3, 2, 1).reshape(G1, P, KD * QKV1),
        "bqkv1": bg.reshape(1, G1 * QKV1), "sinks": f("L1_attn_sinks").reshape(1, G1 * M1),
        "rope_cos": cos, "rope_sin": sin,
    }
    nc = bacc.Bacc("TRN2", target_bir_lowering=False, num_devices=1)
    ap, host = {}, {}
    for name, v in arrays.items():
        v = np.ascontiguousarray(v)
        host[f"in_{name}"] = v
        ap[name] = nc.dram_tensor(f"in_{name}", v.shape, mybir.dt.from_np(v.dtype), kind="ExternalInput").ap()
    out = nc.dram_tensor("out", (TOK, D), F32, kind="ExternalOutput").ap()
    program(nc, ap["x"], ap["wq0"], ap["wkv0"], ap["bq0"], ap["bk0"], ap["bv0"], (ap["wo_0"], ap["wo_1"]), ap["bo"],
            (ap["wff_0"], ap["wff_1"]), (ap["b1_0"], ap["b1_1"]), (ap["b3_0"], ap["b3_1"]), ap["b2"], ap["gates"],
            ap["gate_b"], ap["wqkv1"], ap["bqkv1"], ap["sinks"], ap["rope_cos"], ap["rope_sin"], out)
    r = run_bass_kernel_spmd(nc, [host], core_ids=[0])
    return r.results[0]["out"].reshape(B, T, D)
```

```python
import math
from contextlib import ExitStack

import concourse.bass as bass
import numpy as np
from concourse import mybir

F32 = mybir.dt.float32
F32R = mybir.dt.float32r
BF16 = mybir.dt.bfloat16
ALU = mybir.AluOpType
ACT = mybir.ActivationFunctionType
AX = mybir.AxisListType

P = 128
B, T, D = 4, 256, 256
TOK = B * T
NT = TOK // P
KD = D // P
HALF = TOK // 2
H0, DH0 = 16, 128
G1, M1, DH1 = 8, 4, 64
WINDOW = 128
FF = 176
E = (8, 16)
TOPK = (2, 6)
NJ = tuple(-(-(e + 2) * FF // P) for e in E)
ROUTE_SCALE0 = 2.5
EPS = 1e-5
SCALE0 = 1.0 / math.sqrt(DH0)
MASKED = -1e30
PAD = -1e30
CHOSEN = 1e30
WQ, WKV, WOC, WFF, WQKV = 512, 1024, 1024, 896, 768
SEL, DOWN = 2 * D, 2 * D + P
QKV1 = (M1 + 2) * DH1
QK1 = (M1 + 1) * DH1
UNITS = 8

N_Q0, N_KV0, N_OUT, N_QKV1 = 8, 8, 4, 8
AT_Q0 = 0
AT_KV0 = AT_Q0 + N_Q0
AT_OUT = (AT_KV0 + N_KV0, AT_KV0 + N_KV0 + N_OUT + NJ[0] + N_QKV1)
AT_FF = (AT_OUT[0] + N_OUT, AT_OUT[1] + N_OUT)
AT_QKV1 = AT_FF[0] + NJ[0]
LOGITS = (4, 0)
assert all(n % 2 == 0 for n in (AT_KV0, *AT_OUT, *AT_FF, AT_QKV1))


def program(nc, x, wq0, wkv0, bq0, bk0, bv0, wo, bo, wff, b1, b3, b2, gates, gate_b,
            wqkv1, bqkv1, sinks, rope_cos, rope_sin, out):
    with ExitStack() as ctx:
        def sb(name, shape, dt=F32):
            return ctx.enter_context(nc.sbuf_tensor(name, shape, dt))

        sems = {}

        def sem(name):
            if name not in sems:
                sems[name] = ctx.enter_context(nc.semaphore(name))
            return sems[name]

        xres = sb("xres", [P, NT, D])
        xt_hi = sb("xt_hi", [P, KD, TOK], F32R)
        xt_lo = sb("xt_lo", [P, KD, TOK], F32R)
        raw = sb("raw", [P, 2, 1024])
        w_hi = sb("w_hi", [P, 2, 1024], F32R)
        w_lo = sb("w_lo", [P, 2, 1024], F32R)
        qo = sb("qo", [P, 16 * TOK])
        cw_t = sb("cw_t", [P, TOK], F32R)
        ident = sb("ident", [P, P])
        ident_r = sb("ident_r", [P, P], F32R)
        masks = sb("masks", [P, 4 * P])
        zeros_b = sb("zeros_b", [P, HALF], BF16)
        eps_c = sb("eps_c", [P, 1])
        warm = sb("warm", [P, 2])
        bq_c, bq_s, bk_c, bv_c = (sb(n, [P, H0]) for n in ("bq_c", "bq_s", "bk_c", "bv_c"))
        bo_c = sb("bo_c", [P, 2, KD])
        b1_c = [sb(f"b1_c{l}", [P, NJ[l]]) for l in (0, 1)]
        b3_c = [sb(f"b3_c{l}", [P, NJ[l]]) for l in (0, 1)]
        b2_f = sb("b2_f", [P, D])
        b2_hi = sb("b2_hi", [P, D], F32R)
        b2_st = sb("b2_st", [P, D], F32R)
        gate_f = sb("gate_f", [P, 2, KD * P])
        gate_hi = sb("gate_hi", [P, 2, KD * P], F32R)
        gate_lo = sb("gate_lo", [P, 2, KD * P], F32R)
        gate_b_c = sb("gate_b_c", [P, E[1]])
        bqkv_c = sb("bqkv_c", [P, G1 * QKV1])
        sinks_c = sb("sinks_c", [P, G1 * M1])
        cos_c = sb("cos_c", [P, 2, QK1])
        sin_c = sb("sin_c", [P, 2, QK1])
        stats = sb("stats", [P, NT, 6])
        mv = sb("mv", [P, NT, 2])
        std = sb("std", [P, NT])
        rstd = sb("rstd", [P, NT])
        lg = sb("lg", [P, NT, E[1]])
        val = sb("val", [P, NT, E[1] + 8])
        rep = sb("rep", [P, NT, E[1] + 8])
        top8 = sb("top8", [P, NT, 8])
        red = sb("red", [P, 4, NT])
        prob = sb("prob", [P, NT, E[1]])
        cw = sb("cw", [P, NT, E[1]])
        cw_s = sb("cw_s", [P, NT, P], F32R)
        negmax = sb("negmax", [P, 2, 2, 2])
        rsum = sb("rsum", [P, 2, 2, 2])
        rinv = sb("rinv", [P, 2, 2, 2])
        sink_d = sb("sink_d", [P, 2, 2, 2])
        sink_e = sb("sink_e", [P, 2, 2, 2])
        den = sb("den", [P, 2, 2, 2])
        vp = sb("vp", [P, NT, 3 * DH1])

        def group(**tiles):
            with ExitStack() as some:
                return [some.enter_context(nc.sbuf_tensor(n, shape, dt)) for n, (shape, dt) in tiles.items()]

        kt0, v0, qs, prb1, pt1 = group(
            kt0=([P, 2, TOK], F32), v0=([P, NT, 2 * DH0], F32), qs=([P, 2, T], F32),
            prb1=([P, 2, 1, 3 * P], F32), pt1=([P, 2, 1, 3 * P], F32))
        prb2, pt2, kt1, qt1, qkb, ra, rb, qks = group(
            prb2=([P, 2, 2, 3 * P], F32), pt2=([P, 2, 2, 3 * P], F32), kt1=([P, 2, 2, T], F32R),
            qt1=([P, 2, M1, T], F32R), qkb=([P, 2, QK1], F32), ra=([P, 2, QK1], F32), rb=([P, 2, QK1], F32),
            qks=([P, 2, M1 + 2, P], F32R))
        with nc.sbuf_tensor("xn", [P, NT, D], F32) as xn, nc.sbuf_tensor("lg_t", [P, TOK], F32) as lg_t, \
                nc.sbuf_tensor("s_t", [P, KD, TOK], F32) as s_t:
            _, o_sp = group(behind=([P, 8 * P], F32), o_sp=([P, 2, 2, TOK], F32R))
            o_hi = [o_sp[:, 1 - slot, 0, :] for slot in (0, 1)]
            o_lo = [o_sp[:, 1 - slot, 1, :] for slot in (0, 1)]
            sg, hf, hw, h_hi, h_lo = group(
                sg=([P, 2, HALF], F32), hf=([P, 2, HALF], F32), hw=([P, 2, HALF], F32),
                h_hi=([P, 2, HALF], F32R), h_lo=([P, 2, HALF], F32R))
        prb, pt = {1: prb1, 2: prb2}, {1: pt1, 2: pt2}
        ps = ctx.enter_context(nc.psum_tensor("ps", [P, 8, 512], F32))

        s_x, s_out = [sem("x_in0"), sem("x_in1"), sem("x_in2")], sem("out_written")
        s_first, s_small = sem("first_small_in"), sem("small_in")
        w_in = [sem("w_in0"), sem("w_in1")]
        w_half, w_split, w_used = sem("w_half"), sem("w_split"), sem("w_used")
        w_rest = sem("w_rest")
        NFIRST, NSMALL = 4, 14

        def wait_apart(eng, semaphore, value):
            eng.wait_ge(semaphore, value)
            eng.sem_inc(sem("waits_apart"), 1)

        def load_chunk(sp, src, n_static, n, slot, width):
            if n_static is None or n_static >= 2:
                sp.wait_ge(w_split, n - 1)
            sp.dma_start(raw[:, slot, 0:width], src).then_inc(w_in[slot], 16)

        def split_chunk(pool, n_static, n, pair, slot, width):
            pool.wait_ge(w_in[slot], pair * 16 + 16)
            if n_static is None or n_static >= 2:
                wait_apart(pool, w_used, n - 1)
            nc.gpsimd.tensor_copy(w_hi[:, slot, 0:width], raw[:, slot, 0:width]).then_inc(w_half, 1)
            pool.wait_ge(w_half, n + 1)
            nc.gpsimd.tensor_tensor(w_lo[:, slot, 0:width], raw[:, slot, 0:width],
                                    w_hi[:, slot, 0:width].bitcast(F32), ALU.subtract).then_inc(w_split, 1)

        def mm3(dst, l_hi, l_lo, r_hi, r_lo, start, stop):
            nc.tensor.matmul(dst, l_hi, r_hi, start=start, stop=False)
            nc.tensor.matmul(dst, l_hi, r_lo, start=False, stop=False)
            return nc.tensor.matmul(dst, l_lo, r_hi, start=False, stop=stop)

        def proj(dst, slot, col, width, stride, half):
            for k in range(KD):
                c = col + k * stride
                last = mm3(dst, w_hi[:, slot, c:c + width], w_lo[:, slot, c:c + width],
                           xt_hi[:, k, half * HALF:(half + 1) * HALF],
                           xt_lo[:, k, half * HALF:(half + 1) * HALF], k == 0, k == KD - 1)
            return last

        def proj_tok(dst, slot, col, width, t):
            for k in range(KD):
                c = col + k * width
                last = mm3(dst, xt_hi[:, k, t * P:(t + 1) * P], xt_lo[:, k, t * P:(t + 1) * P],
                           w_hi[:, slot, c:c + width], w_lo[:, slot, c:c + width], k == 0, k == KD - 1)
            return last

        def score_columns(parts, qt):
            at = qt * (P if parts == 1 else T)
            return slice(at, at + (qt + 1) * P)

        def groups(eng, body):
            body(0, 0, first=True)
            with eng.Fori(0, N_KV0 // 2 - 1) as i:
                body(i * 2 + 1, 1)
                body(i * 2 + 2, 0)
            body(N_KV0 - 1, 1, last=True)

        block = ctx.enter_context(nc.Block())

        @block.sync
        def _(sp):
            x_tiles = x.rearrange("(t p) d -> p t d", p=P)
            for n, t in enumerate((slice(0, 2), slice(2, 4), slice(4, 8))):
                sp.dma_start(xres[:, t, :], x_tiles[:, t, :]).then_inc(s_x[n], 16)
                if n == 1:
                    load_chunk(sp, wq0[0], 0, 0, 0, WQ)
            for dst, src in ((bq_c[:], bq0), (gate_f[:, 0, :], gates[0]), (gate_f[:, 1, :], gates[1]), (b2_f[:], b2)):
                sp.dma_start(dst, src).then_inc(s_first, 16)
            load_chunk(sp, wq0[1], 1, 1, 1, WQ)
            for dst, src in ((bk_c[:], bk0), (bv_c[:], bv0), (bo_c[:], bo),
                             (b1_c[0][:], b1[0]), (b1_c[1][:], b1[1]), (b3_c[0][:], b3[0]), (b3_c[1][:], b3[1]),
                             (gate_b_c[:], gate_b.to_broadcast([P, E[1]])),
                             (bqkv_c[:], bqkv1.to_broadcast([P, G1 * QKV1])),
                             (sinks_c[:], sinks.to_broadcast([P, G1 * M1])),
                             (cos_c[:, 0, :], rope_cos[0]), (cos_c[:, 1, :], rope_cos[1]),
                             (sin_c[:, 0, :], rope_sin[0]), (sin_c[:, 1, :], rope_sin[1])):
                sp.dma_start(dst, src).then_inc(s_small, 16)

            def stream(src, at, first, pairs, width, odd=0):
                with sp.Fori(first, pairs) as i:
                    for slot in (0, 1):
                        load_chunk(sp, src[bass.ds(i * 2 + slot, 1)].rearrange("a p n -> (a p) n"),
                                   None, i * 2 + (at + slot), slot, width)
                if odd:
                    load_chunk(sp, src[2 * pairs], None, at + 2 * pairs, 0, width)

            stream(wq0, AT_Q0, 1, N_Q0 // 2, WQ)
            stream(wkv0, AT_KV0, 0, N_KV0 // 2, WKV)
            stream(wo[0], AT_OUT[0], 0, N_OUT // 2, WOC)
            stream(wff[0], AT_FF[0], 0, NJ[0] // 2, WFF)
            stream(wqkv1, AT_QKV1, 0, N_QKV1 // 2, WQKV)
            stream(wo[1], AT_OUT[1], 0, 1, WOC)
            sp.wait_ge(w_rest, 2)
            stream(wo[1], AT_OUT[1], 1, N_OUT // 2, WOC)
            stream(wff[1], AT_FF[1], 0, NJ[1] // 2, WFF, odd=NJ[1] % 2)
            for n in range(4):
                sp.wait_ge(sem("res1"), n + 1)
                sp.dma_start(out.rearrange("(t p) d -> p t d", p=P)[:, 2 * n:2 * n + 2, :],
                             xres[:, 2 * n:2 * n + 2, :]).then_inc(s_out, 16)
            sp.wait_ge(s_out, 64)

        @block.gpsimd
        def _(pool):
            nc.gpsimd.memset(ident[:], 0.0).then_inc(sem("ident"), 1)
            nc.gpsimd.memset(eps_c[:], EPS).then_inc(sem("eps"), 1)
            pool.wait_ge(sem("ident"), 1)
            nc.gpsimd.affine_select(out=ident[:], in_=ident[:], compare_op=ALU.not_equal, fill=1.0,
                                    base=0, pattern=[[-1, P]], channel_multiplier=1).then_inc(sem("ident"), 1)
            split_chunk(pool, 0, 0, 0, 0, WQ)
            pool.wait_ge(s_first, 16 * NFIRST)
            nc.gpsimd.tensor_scalar(bq_s[:], bq_c[:], SCALE0, None, ALU.mult).then_inc(sem("bq_s"), 1)
            nc.gpsimd.tensor_copy(gate_hi[:], gate_f[:]).then_inc(sem("gates"), 1)
            pool.wait_ge(sem("gates"), 1)
            nc.gpsimd.tensor_tensor(gate_lo[:], gate_f[:], gate_hi[:].bitcast(F32), ALU.subtract).then_inc(sem("gates"), 1)
            split_chunk(pool, 1, 1, 0, 1, WQ)
            nc.gpsimd.memset(masks[:], 0.0).then_inc(sem("masks"), 1)
            pool.wait_ge(sem("masks"), 1)
            for at in (P, 3 * P):
                nc.gpsimd.affine_select(out=masks[:, at:at + P], in_=masks[:, at:at + P], compare_op=ALU.is_ge,
                                        fill=MASKED, base=0, pattern=[[-1, P]], channel_multiplier=1)\
                    .then_inc(sem("masks"), 1)
            nc.gpsimd.affine_select(out=masks[:, 2 * P:3 * P], in_=masks[:, 2 * P:3 * P], compare_op=ALU.is_gt,
                                    fill=MASKED, base=0, pattern=[[1, P]], channel_multiplier=-1)\
                .then_inc(sem("masks"), 1)
            nc.gpsimd.tensor_copy(ident_r[:], ident[:]).then_inc(sem("consts"), 1)
            nc.gpsimd.memset(zeros_b[:], 0.0).then_inc(sem("consts"), 1)
            nc.gpsimd.memset(vp[:], 0.0).then_inc(sem("consts"), 1)

            with pool.Fori(1, N_Q0 // 2) as i:
                for slot in (0, 1):
                    split_chunk(pool, None, i * 2 + slot, i, slot, WQ)

            def split_high(n, pair, slot, width):
                pool.wait_ge(w_in[slot], pair * 16 + 16)
                wait_apart(pool, w_used, n - 1)
                nc.gpsimd.tensor_copy(w_hi[:, slot, 0:width], raw[:, slot, 0:width]).then_inc(w_half, 1)

            def split_low(n, slot, width):
                pool.wait_ge(w_half, n + 1)
                nc.gpsimd.tensor_tensor(w_lo[:, slot, 0:width], raw[:, slot, 0:width],
                                        w_hi[:, slot, 0:width].bitcast(F32), ALU.subtract).then_inc(w_split, 1)

            pool.wait_ge(s_small, 16 * NSMALL)

            pool.wait_ge(w_in[0], AT_KV0 // 2 * 16 + 16)
            pool.wait_ge(w_used, AT_KV0 - 1)
            for part, half, done, n in ((slice(0, 2 * D), sem("first_half"), sem("first_keys"), 1),
                                        (slice(2 * D, WKV), w_half, w_split, AT_KV0 + 1)):
                nc.gpsimd.tensor_copy(w_hi[:, 0, part], raw[:, 0, part]).then_inc(half, 1)
                pool.wait_ge(half, n)
                nc.gpsimd.tensor_tensor(w_lo[:, 0, part], raw[:, 0, part], w_hi[:, 0, part].bitcast(F32),
                                        ALU.subtract).then_inc(done, 1)
            nc.gpsimd.tensor_copy(b2_hi[:], b2_f[:]).then_inc(sem("b2_hi"), 1)
            pool.wait_ge(sem("q0_evac_act"), N_Q0 * 2)
            pool.wait_ge(sem("q0_evac_dve"), N_Q0 * 2)

            def heads0(g, par, first=False, last=False):
                for v in range(UNITS):
                    b, hh = v // 2, v % 2
                    if not (first and v < 2):
                        wait_apart(pool, sem("scores1"), g * 8 + (v - 1))
                    nc.gpsimd.tensor_copy(qs[:, v % 2, :], qo[:, bass.ds(g * 2 * T + (b * H0 * T + hh * T), T)])\
                        .then_inc(sem("q_slot"), 1)
                    half = g // 2 if isinstance(g, int) else pool_i[0]
                    if v == 2:
                        split_high(g + (AT_KV0 + 1), half + AT_KV0 // 2 + (1 if par else 0), 1 - par, WKV)
                    if v == 3:
                        split_low(g + (AT_KV0 + 1), 1 - par, WKV)

            pool_i = [None]

            def groups_pool(body):
                body(0, 0, first=True)
                with pool.Fori(0, N_KV0 // 2 - 1) as i:
                    pool_i[0] = i
                    body(i * 2 + 1, 1)
                    pool_i[0] = i + 1
                    body(i * 2 + 2, 0)
                body(N_KV0 - 1, 1, last=True)

            groups_pool(heads0)

            def split_out(l):
                split_chunk(pool, None, AT_OUT[l] + 1, AT_OUT[l] // 2, 1, WOC)
                with pool.Fori(1, N_OUT // 2) as i:
                    for slot in (0, 1):
                        split_chunk(pool, None, i * 2 + (AT_OUT[l] + slot), i + AT_OUT[l] // 2, slot, WOC)

            def split_experts(l):
                def one(j, pair, slot, early=False):
                    n = j + AT_FF[l]
                    pool.wait_ge(w_in[slot], pair * 16 + (AT_FF[l] // 2 * 16 + 16))
                    if early:
                        wait_apart(pool, w_used, n - 1)
                    else:
                        wait_apart(pool, sem(f"wr{l}"), j * 2 - 2)
                    nc.gpsimd.tensor_copy(w_hi[:, slot, 0:DOWN], raw[:, slot, 0:DOWN]).then_inc(w_half, 1)
                    pool.wait_ge(w_half, n + 1)
                    nc.gpsimd.tensor_tensor(w_lo[:, slot, 0:SEL], raw[:, slot, 0:SEL],
                                            w_hi[:, slot, 0:SEL].bitcast(F32), ALU.subtract).then_inc(sem(f"up_split{l}"), 1)
                    if not early:
                        wait_apart(pool, w_used, n - 1)
                    nc.gpsimd.tensor_copy(w_hi[:, slot, DOWN:WFF], raw[:, slot, DOWN:WFF]).then_inc(sem(f"down_half{l}"), 1)
                    pool.wait_ge(sem(f"down_half{l}"), j + 1)
                    nc.gpsimd.tensor_tensor(w_lo[:, slot, DOWN:WFF], raw[:, slot, DOWN:WFF],
                                            w_hi[:, slot, DOWN:WFF].bitcast(F32), ALU.subtract).then_inc(w_split, 1)

                one(0, 0, 0, early=True)
                one(1, 0, 1, early=True)
                with pool.Fori(1, NJ[l] // 2) as i:
                    for slot in (0, 1):
                        one(i * 2 + slot, i, slot)
                if NJ[l] % 2:
                    one(NJ[l] - 1, NJ[l] // 2, 0)

            split_out(0)
            split_experts(0)

            split_chunk(pool, None, AT_QKV1, AT_QKV1 // 2, 0, WQKV)
            for m in range(KD):
                pool.wait_ge(sem("gate0"), KD + m + 1)
                nc.gpsimd.tensor_tensor(s_t[:, m, HALF:TOK], s_t[:, m, HALF:TOK],
                                        xn[:, 4 + m * 2:6 + m * 2, :].rearrange("p a b -> p (a b)"),
                                        ALU.mult).then_inc(sem("prod_second"), 1)


            def rope(g, t):
                N = g * 8 + t
                pool.wait_ge(sem("qkb"), N + 1)
                qv = qkb[:, t % 2, :].rearrange("p (h s d) -> p h s d", s=2, d=DH1 // 2)
                rv = rb[:, t % 2, :].rearrange("p (h s d) -> p h s d", s=2, d=DH1 // 2)
                sv = sin_c[:, t % 2, :].rearrange("p (h s d) -> p h s d", s=2, d=DH1 // 2)
                for s in (0, 1):
                    nc.gpsimd.tensor_tensor(rv[:, :, s, :], qv[:, :, 1 - s, :], sv[:, :, s, :],
                                            ALU.mult).then_inc(sem("rope_sin"), 1)
                if not (isinstance(g, int) and g == 0 and t < 2):
                    pool.wait_ge(sem("qk_lo"), N - 1)
                nc.gpsimd.tensor_tensor(ra[:, t % 2, :], qkb[:, t % 2, :], cos_c[:, t % 2, :], ALU.mult).then_inc(sem("rope_cos"), 1)
                pool.wait_ge(sem("rope_sin"), g * 16 + (2 * t + 2))
                pool.wait_ge(sem("rope_cos"), N + 1)
                nc.gpsimd.tensor_tensor(ra[:, t % 2, :], ra[:, t % 2, :], rb[:, t % 2, :], ALU.add)\
                    .then_inc(sem("rotated"), 1)

            for t in range(3):
                rope(0, t)

            def heads1(g, par, first=False, last=False):
                for v in range(UNITS):
                    if not (last and v >= 5):
                        rope(g if v < 5 else g + 1, (v + 3) % 8)
                    n, slot = g + (AT_QKV1 + 1), 1 - par
                    part = slice(v % 2 * WQKV // 2, (v % 2 + 1) * WQKV // 2)
                    if v == 0:
                        half = g // 2 if isinstance(g, int) else pool_i[0]
                        pool.wait_ge(w_in[slot], (half + AT_QKV1 // 2 + (1 if par else 0)) * 16 + 16)
                        wait_apart(pool, w_used, n - 1)
                    if v < 2:
                        nc.gpsimd.tensor_copy(w_hi[:, slot, part], raw[:, slot, part])\
                            .then_inc(w_half if v else sem("quarter_hi"), 1)
                    elif v < 4:
                        pool.wait_ge(w_half, n + 1)
                        if v == 2:
                            pool.wait_ge(sem("quarter_hi"), g + 1)
                        nc.gpsimd.tensor_tensor(w_lo[:, slot, part], raw[:, slot, part],
                                                w_hi[:, slot, part].bitcast(F32), ALU.subtract)\
                            .then_inc(w_split if v == 3 else sem("quarter_lo"), 1)
            groups_pool(heads1)
            nc.gpsimd.tensor_copy(w_hi[:, 0, WQKV:WOC], raw[:, 0, WQKV:WOC]).then_inc(w_rest, 1)
            pool.wait_ge(w_rest, 1)
            nc.gpsimd.tensor_tensor(w_lo[:, 0, WQKV:WOC], raw[:, 0, WQKV:WOC],
                                    w_hi[:, 0, WQKV:WOC].bitcast(F32), ALU.subtract).then_inc(w_rest, 1)
            split_out(1)
            split_experts(1)

        @block.tensor
        def _(pe):
            def transpose_norm(l, half):
                for t in range(half * 4, half * 4 + 4):
                    pe.wait_ge(sem(f"xn{l}"), t + 1)
                    for k in range(KD):
                        last = nc.tensor.transpose(ps[:, k + 2 * (t // 4), (t % 4) * P:(t % 4 + 1) * P],
                                                   xn[:, t, k * P:(k + 1) * P], ident[:])
                    if t % 4 == 3:
                        last.then_inc(sem(f"xn_t{l}"), 1)

            def logits(l, half):
                for k in range(KD):
                    g = slice(k * P, (k + 1) * P)
                    r = slice(half * HALF, (half + 1) * HALF)
                    last = mm3(ps[:, LOGITS[l] + half, :], gate_hi[:, l, g], gate_lo[:, l, g],
                               xt_hi[:, k, r], xt_lo[:, k, r], k == 0, k == KD - 1)
                last.then_inc(sem(f"lg{l}"), 1)

            def logits_back(l):
                for half in (0, 1):
                    pe.wait_ge(sem(f"lg_t{l}"), half + 1)
                    for t in range(4):
                        last = nc.tensor.transpose(ps[:, LOGITS[l] + 2 + half, t * P:(t + 1) * P],
                                                   lg_t[:, (half * 4 + t) * P:(half * 4 + t + 1) * P], ident[:])
                    last.then_inc(sem(f"lg_tok{l}"), 1)

            def transposes_of(u, U, parts, bank):
                pe.wait_ge(sem(f"normed{parts}"), U + 1)
                for hh in range(parts):
                    for c in range(3):
                        last = nc.tensor.transpose(ps[:, bank + hh, c * P:(c + 1) * P],
                                                   prb[parts][:, u % 2, hh, c * P:(c + 1) * P], ident[:])
                last.then_inc(sem(f"p_t{parts}"), 1)

            def out_row(l, i, slot, r):
                if r == 0:
                    pe.wait_ge(w_split, i * 2 + (AT_OUT[l] + slot + 1))
                if (l, i, slot, r) == (1, 0, 0, 3):
                    pe.wait_ge(w_rest, 2)
                pe.wait_ge(sem(f"o_split{l}"), i * 8 + (slot * 4 + r + 1))
                for m in range(KD):
                    c = r * D + m * P
                    for half in (0, 1):
                        h = slice(half * HALF, (half + 1) * HALF)
                        last = mm3(ps[:, m + 2 * half, :], w_hi[:, slot, c:c + P], w_lo[:, slot, c:c + P],
                                   o_hi[r % 2][:, h], o_lo[r % 2][:, h], False, False)
                last.then_inc(sem(f"o_used{l}") if r < 3 else w_used, 1)

            def out_first(l):
                pe.wait_ge(sem(f"exp{l + 1}"), N_KV0 * UNITS)
                for bank in range(4):
                    if l == 0 and bank == 2:
                        pe.wait_ge(sem("pt1"), N_KV0 * UNITS)
                    nc.tensor.matmul(ps[:, bank, :], zeros_b[:, 0:P], zeros_b[:], start=True, stop=False)
                out_row(l, 0, 0, 0)

            def out_projection(l):
                for i in range(N_OUT // 2):
                    if i == 1:
                        pe.wait_ge(sem(f"o_evac{l + 1}"), N_KV0 * UNITS)
                        pe.wait_ge(sem(f"cw{l}"), 1)
                        for t in range(NT):
                            last = nc.tensor.transpose(ps[:, 4 + t // 4, (t % 4) * P:(t % 4 + 1) * P].bitcast(F32R),
                                                       cw_s[:, t, :], ident_r[:])
                        last.then_inc(sem(f"cw_tp{l}"), 1)
                    for slot in (0, 1):
                        for r in range(4):
                            if i or slot or r:
                                out_row(l, i, slot, r)
                for bank in range(4):
                    last = nc.tensor.matmul(ps[:, bank, :], zeros_b[:, 0:P], zeros_b[:], start=False, stop=True)
                last.then_inc(sem(f"s_acc{l}"), 1)

            def experts(l):
                def up(j, slot, half, st, first=False):
                    if half == 0:
                        pe.wait_ge(sem(f"up_split{l}"), j + 1)
                    proj(ps[:, 4 if half == 0 else 7, :], slot, 0, P, P, half).then_inc(sem(f"g{l}"), 1)
                    if not first:
                        pe.wait_ge(sem(f"gu{l}"), st)
                    proj(ps[:, 5, :], slot, 2 * P, P, P, half).then_inc(sem(f"u{l}"), 1)
                    if not first:
                        pe.wait_ge(sem(f"gw{l}"), st)
                    nc.tensor.matmul(ps[:, 6, :], w_hi[:, slot, SEL:DOWN], cw_t[:, half * HALF:(half + 1) * HALF],
                                     start=True, stop=True).then_inc(sem(f"wr{l}"), 1)

                def down(j, slot, half, st, stop=False):
                    if half == 0:
                        pe.wait_ge(w_split, j + (AT_FF[l] + 1))
                    pe.wait_ge(sem(f"h_lo{l}"), st + 1)
                    for m in range(KD):
                        c = DOWN + m * P
                        last = mm3(ps[:, m + 2 * half, :], w_hi[:, slot, c:c + P], w_lo[:, slot, c:c + P],
                                   h_hi[:, half, :], h_lo[:, half, :], False, stop)
                    last.then_inc(w_used if half else sem(f"h_used{l}"), 1)

                steps = 2 * NJ[l]
                loops = (steps - 1) // 4
                pe.wait_ge(sem(f"cw_t{l}"), 2)
                up(0, 0, 0, 0, first=True)
                pe.wait_ge(sem("b2"), 2)
                pe.wait_ge(sem(f"s_t{l}"), 4)
                for half in (0, 1):
                    for m in range(KD):
                        if l == 1:
                            nc.tensor.matmul(ps[:, m + 2 * half, :], b2_st[:, m * P:(m + 1) * P],
                                             cw_t[:, half * HALF:(half + 1) * HALF], start=True, stop=False)
                        else:
                            nc.tensor.matmul(ps[:, m + 2 * half, :], zeros_b[:, 0:P], zeros_b[:], start=True, stop=False)
                def four(i):
                    for k in (1, 2, 3, 4):
                        st = i * 4 + k
                        jj = k // 2
                        up(i * 2 + jj, jj % 2, k % 2, st)
                        down(i * 2 + (k - 1) // 2, ((k - 1) // 2) % 2, (k - 1) % 2, st - 1)
                with pe.Fori(0, loops) as i:
                    four(i)
                for st in range(4 * loops + 1, steps):
                    up(st // 2, (st // 2) % 2, st % 2, st)
                    down((st - 1) // 2, ((st - 1) // 2) % 2, (st - 1) % 2, st - 1, stop=st - 1 >= steps - 2)
                down(NJ[l] - 1, ((steps - 1) // 2) % 2, 1, steps - 1, stop=True)

            def gate_and_back(l):
                for half in (0, 1):
                    if (l, half) == (0, 1):
                        pe.wait_ge(sem("prod_second"), KD)
                    else:
                        pe.wait_ge(sem(f"prod{l}"), 2 * half + 2)
                    for t in range(4):
                        for m in range(KD):
                            c = (half * 4 + t) * P
                            last = nc.tensor.transpose(ps[:, 4 + half * 2 + t // 2, (t % 2) * D + m * P:(t % 2) * D + (m + 1) * P],
                                                       s_t[:, m, c:c + P], ident[:])
                        if t % 2:
                            last.then_inc(sem(f"prod_t{l}"), 1)

            pe.wait_ge(sem("ident"), 2)
            transpose_norm(0, 0)

            def queries(i, first):
                for slot in (0, 1):
                    pe.wait_ge(w_split, i * 2 + (slot + 1))
                    for cc in (0, 1):
                        for half in (0, 1):
                            if first and slot == 0 and cc == 0:
                                if half:
                                    transpose_norm(0, 1)
                                    pe.wait_ge(sem("gates"), 2)
                                    logits(0, 0)
                                pe.wait_ge(sem("xt0"), 2 * half + 2)
                            if not (first and slot == 0):
                                pe.wait_ge(sem("q0_evac_act" if half == 0 else "q0_evac_dve"), i * 4 + (slot * 2 + cc - 1))
                            last = proj(ps[:, cc * 2 + half, :], slot, cc * 2 * P, P, P, half)
                            last.then_inc(w_used if (cc, half) == (1, 1) else sem(f"q0_ps{half}"), 1)
                        if first and (slot, cc) == (0, 0):
                            logits(0, 1)
                        if first and (slot, cc) == (0, 1):
                            logits_back(0)
            queries(0, True)
            with pe.Fori(1, N_Q0 // 2) as i:
                queries(i, False)

            def keys0(g, par, hh, half, n, first=False):
                if not first:
                    pe.wait_ge(sem("k0"), g * 4 + n)
                proj(ps[:, 6, :], par, hh * KD * P, P, P, half).then_inc(sem("k0_ps"), 1)

            def values0(g, par, n, first=False):
                if not first:
                    pe.wait_ge(sem("v0"), g * 4 + n)
                proj_tok(ps[:, 7, 0:T], par, 4 * P, T, 2 * n)
                proj_tok(ps[:, 7, T:2 * T], par, 4 * P, T, 2 * n + 1).then_inc(sem("v0_ps") if n < 3 else w_used, 1)

            def scores0(g, v, first):
                b, hh = v // 2, v % 2
                pe.wait_ge(sem("q_slot"), g * 8 + (v + 1))
                if v in (0, 1, 4, 5):
                    pe.wait_ge(sem("k0"), g * 4 + (1 + hh + v // 4 * 2))
                if not (first and v < 2):
                    pe.wait_ge(sem("exp1"), g * 8 + (v - 1))
                bank = v % 2
                nc.tensor.matmul(ps[:, bank, 0:P], qs[:, bank, 0:P], kt0[:, hh, b * T:b * T + P], start=True, stop=True)
                nc.tensor.matmul(ps[:, bank, P:3 * P], qs[:, bank, P:T], kt0[:, hh, b * T:b * T + T], start=True, stop=True)\
                    .then_inc(sem("scores1"), 1)

            def heads_out0(g, v, first):
                b, hh = v % 8 // 2, v % 2
                pe.wait_ge(sem("pt1"), g * 8 + (v + 1))
                if not (first and v < 2):
                    pe.wait_ge(sem("o_evac1"), g * 8 + (v - 1))
                if hh == 0:
                    pe.wait_ge(sem("v0"), g * 4 + (v // 2 + 1))
                bank = 4 + v % 2
                nc.tensor.matmul(ps[:, bank, 0:T], v0[:, 2 * b, hh * P:(hh + 1) * P], pt1[:, v % 2, 0, 0:T],
                                 start=True, stop=False)
                nc.tensor.matmul(ps[:, bank, P:T], v0[:, 2 * b + 1, hh * P:(hh + 1) * P], pt1[:, v % 2, 0, T:3 * P],
                                 start=False, stop=True).then_inc(sem("o_ps1"), 1)

            def transposed0(g, v, first):
                if not (first and v < 2):
                    pe.wait_ge(sem("pt1"), g * 8 + (v - 1))
                transposes_of(v, g * 8 + v, 1, 2 + v % 2)

            pe.wait_ge(sem("consts"), 3)
            pe.wait_ge(sem("first_keys"), 1)
            keys0(0, 0, 0, 0, 0, first=True)
            keys0(0, 0, 1, 0, 1)
            pe.wait_ge(w_split, AT_KV0 + 1)
            values0(0, 0, 0, first=True)

            def heads0(g, par, first=False, last=False):
                for v in range(UNITS):
                    scores0(g, v, first)
                    if not (first and v < 2):
                        transposed0(g, v - 2, first)
                    if not (first and v < 3):
                        heads_out0(g, v - 3, first)
                    if v in (0, 2, 4):
                        values0(g, par, v // 2 + 1)
                    if v in (1, 3):
                        keys0(g, par, v // 2, 1, 2 + v // 2)
                    if v >= 5 and not last:
                        if v == 5:
                            pe.wait_ge(w_split, g + (AT_KV0 + 2))
                        if v < 7:
                            keys0(g, 1 - par, v - 5, 0, 4 + v - 5)
                        else:
                            values0(g + 1, 1 - par, 0)
            groups(pe, heads0)
            g = N_KV0 - 1
            transposed0(g, 6, False)
            heads_out0(g, 5, False)
            transposed0(g, 7, False)
            heads_out0(g, 6, False)
            out_first(0)
            heads_out0(g, 7, False)
            out_projection(0)
            experts(0)
            gate_and_back(0)

            transpose_norm(1, 0)
            def projected1(g, par, t, first=False):
                if not first:
                    pe.wait_ge(sem("qkv1"), g * 8 + t)
                proj_tok(ps[:, 7, 0:QKV1], par, 0, QKV1, t).then_inc(sem("qkv1_ps") if t < NT - 1 else w_used, 1)

            def transposed_qk(g, t):
                pe.wait_ge(sem("qk_lo"), g * 8 + (t + 1))
                for c in range(M1 + 2):
                    last = nc.tensor.transpose(ps[:, 4 + c // 4, (c % 4) * P:(c % 4 + 1) * P].bitcast(F32R),
                                               qks[:, t % 2, c, :], ident_r[:])
                last.then_inc(sem("qk_t"), 1)

            def scores1(g, v, first):
                b, pr = v // 2, v % 2
                if v % 2 == 0:
                    pe.wait_ge(sem("qk_out"), g * 8 + (2 * b + 2))
                if not (first and v < 2):
                    pe.wait_ge(sem("exp2"), g * 8 + (v - 1))
                for hh in (0, 1):
                    bank = (v % 2) * 2 + hh
                    for qt in (0, 1):
                        at = slice(qt * T, qt * T + T)
                        q = qt1[:, b % 2, 2 * pr + hh, qt * P:(qt + 1) * P]
                        nc.tensor.matmul(ps[:, bank, at], q, kt1[:, b % 2, 0, :], start=True, stop=False)
                        last = nc.tensor.matmul(ps[:, bank, at], q, kt1[:, b % 2, 1, :], start=False, stop=True)
                last.then_inc(sem("scores2"), 1)

            def transposed1(g, v, first, tiles):
                if not (first and v < 1):
                    pe.wait_ge(sem("pt2"), g * 8 + v)
                pe.wait_ge(sem("qk_out"), g * 8 + tiles)
                transposes_of(v, g * 8 + v, 2, 4)

            def heads_out1(g, v, first):
                b = v % 8 // 2
                pe.wait_ge(sem("pt2"), g * 8 + (v + 1))
                if not (first and v < 1):
                    pe.wait_ge(sem("o_evac2"), g * 8 + v)
                for hh in (0, 1):
                    c = slice(DH1 * (1 - hh), DH1 * (1 - hh) + P)
                    nc.tensor.matmul(ps[:, 6, 0:T], vp[:, 2 * b, c], pt2[:, v % 2, hh, 0:T], start=hh == 0, stop=False)
                    last = nc.tensor.matmul(ps[:, 6, P:T], vp[:, 2 * b + 1, c], pt2[:, v % 2, hh, T:3 * P],
                                            start=False, stop=hh == 1)
                last.then_inc(sem("o_ps2"), 1)

            pe.wait_ge(w_split, AT_QKV1 + 1)
            pe.wait_ge(sem("xt1"), 2)
            for t in range(4):
                projected1(0, 0, t, first=t == 0)
                if t == 0:
                    logits(1, 0)
                elif t == 1:
                    transpose_norm(1, 1)
                elif t == 2:
                    transposed_qk(0, 0)
                    pe.wait_ge(sem("xt1"), 4)
                    logits(1, 1)
            pe.wait_ge(sem("qk_out"), 1)
            transposed_qk(0, 1)
            logits_back(1)

            def heads1(g, par, first=False, last=False):
                for v in range(UNITS):
                    scores1(g, v, first)
                    if not (first and v < 2):
                        transposed1(g, v - 2, first, 8 if last and v == 7 else v + 2)
                    if first and v == 0:
                        pe.wait_ge(sem("lg"), 2)
                    if not (first and v < 3):
                        heads_out1(g, v - 3, first)
                    if not (last and v >= 6):
                        if first and v < 2:
                            pe.wait_ge(sem("qk_out"), v + 2)
                        else:
                            pe.wait_ge(sem("pt2"), g * 8 + (v - 1))
                        transposed_qk(g if v < 6 else g + 1, (v + 2) % 8)
                    if v < 4:
                        projected1(g, par, v + 4)
                    elif not last:
                        if v == 4:
                            pe.wait_ge(w_split, g + (AT_QKV1 + 2))
                        projected1(g + 1, 1 - par, v - 4)
            groups(pe, heads1)
            g = N_QKV1 - 1
            transposed1(g, 6, False, 8)
            heads_out1(g, 5, False)
            out_first(1)
            transposed1(g, 7, False, 8)
            heads_out1(g, 6, False)
            heads_out1(g, 7, False)
            out_projection(1)
            experts(1)
            gate_and_back(1)

        @block.scalar
        def _(act):
            def load_table(func):
                nc.scalar.activation(warm[:, 1:2], warm[:, 0:1], func)

            def norm(l):
                for half in (0, 1):
                    act.wait_ge(sem(f"mv{l}"), 4 * half + 4)
                    t = slice(4 * half, 4 * half + 4)
                    nc.scalar.activation(std[:, t], mv[:, t, 1], ACT.Sqrt, bias=eps_c[:], scale=1.0).then_inc(sem(f"std{l}"), 1)
                    act.wait_ge(sem(f"xn_t{l}"), half + 1)
                    for k in range(KD):
                        nc.scalar.activation(xt_hi[:, k, half * HALF:(half + 1) * HALF], ps[:, k + 2 * half, :], ACT.Copy)\
                            .then_inc(sem(f"xt_hi{l}"), 1)

            def logits_out(l, half):
                act.wait_ge(sem(f"lg{l}"), half + 1)
                nc.scalar.activation(lg_t[:, half * HALF:(half + 1) * HALF], ps[:, LOGITS[l] + half, :], ACT.Copy)\
                    .then_inc(sem(f"lg_t{l}"), 1)

            def token_logits(l, dst, func, done):
                act.wait_ge(sem(f"lg_tok{l}"), 2)
                for half in (0, 1):
                    nc.scalar.activation(dst[:, half * 4:half * 4 + 4, 0:E[l]],
                                         ps[:, LOGITS[l] + 2 + half, :].rearrange("p (t c) -> p t c", c=P)[:, :, 0:E[l]],
                                         func).then_inc(done, 1)

            def exps(g, u, parts, first, hh=0):
                if hh == 0:
                    act.wait_ge(sem(f"max{parts}"), g * 8 + (u + 1))
                    if not (first and u < 2):
                        act.wait_ge(sem(f"p_t{parts}"), g * 8 + (u - 1))
                bank = u % 2 if parts == 1 else (u % 2) * 2 + hh
                for qt in (0, 1):
                    c = slice(0, P) if qt == 0 else slice(P, 3 * P)
                    last = nc.scalar.activation(prb[parts][:, u % 2, hh, c], ps[:, bank, score_columns(parts, qt)], ACT.Exp,
                                                bias=negmax[:, u % 2, qt, hh:hh + 1], scale=-1.0,
                                                accum_out=rsum[:, u % 2, qt, hh:hh + 1])
                if hh == parts - 1:
                    if parts == 2:
                        last = nc.scalar.activation(sink_e[:, u % 2], sink_d[:, u % 2], ACT.Exp)
                    last.then_inc(sem(f"exp{parts}"), 1)

            def evac_transposed(g, u, parts, bank, first):
                act.wait_ge(sem(f"p_t{parts}"), g * 8 + (u + 1))
                if not (first and u < 2):
                    act.wait_ge(sem(f"o_ps{parts}"), g * 8 + (u - 1))
                nc.scalar.activation(pt[parts][:, u % 2, 0:parts, :], ps[:, bank:bank + parts, 0:3 * P], ACT.Copy)\
                    .then_inc(sem(f"pt{parts}"), 1)

            def high(l, i, r):
                if i == 0 and r < 2:
                    act.wait_ge(sem(f"o_evac{l + 1}"), UNITS)
                else:
                    if i == 0 and r == 2:
                        act.wait_ge(sem(f"o_evac{l + 1}"), N_KV0 * UNITS)
                    c, at = divmod(r - 2, 4)
                    if at < 3:
                        act.wait_ge(sem(f"o_used{l}"), i * 6 + (3 * c + at + 1))
                    else:
                        act.wait_ge(w_used, i * 2 + (AT_OUT[l] + c + 1))
                nc.scalar.activation(o_hi[r % 2].rearrange("p (b t) -> p b t", b=B), heads(l, i, r), ACT.Copy)\
                    .then_inc(sem(f"o_hi{l}"), 1)

            def out_projection(l, ahead):
                for i in range(N_OUT // 2):
                    for r in range(8):
                        if i or r >= ahead:
                            high(l, i, r)
                        if (i, r) == (1, 1):
                            act.wait_ge(sem(f"cw_tp{l}"), 1)
                            for half in (0, 1):
                                nc.scalar.activation(cw_t[:, half * HALF:(half + 1) * HALF], ps[:, 4 + half, :], ACT.Copy)\
                                    .then_inc(sem(f"cw_t{l}"), 1)
                act.wait_ge(sem(f"s_acc{l}"), 1)
                for half in (0, 1):
                    for m in range(KD):
                        nc.scalar.activation(s_t[:, m, half * HALF:(half + 1) * HALF], ps[:, m + 2 * half, :], ACT.Identity,
                                             bias=bo_c[:, l, m:m + 1], scale=1.0).then_inc(sem(f"s_t{l}"), 1)

            def experts(l):
                load_table(ACT.Silu)

                def silu(j, half, st):
                    if not (isinstance(st, int) and st < 2):
                        act.wait_ge(sem(f"gu{l}"), st - 1)
                    wait_apart(act, sem(f"g{l}"), st + 1)
                    nc.scalar.activation(sg[:, half, :], ps[:, 4 if half == 0 else 7, :], ACT.Silu,
                                         bias=b1_c[l][:, bass.ds(j, 1)], scale=1.0).then_inc(sem(f"silu{l}"), 1)

                def high(j, half, st):
                    act.wait_ge(sem(f"gw{l}"), st + 1)
                    if not (isinstance(st, int) and st < 2):
                        if half:
                            act.wait_ge(w_used, j + AT_FF[l])
                        else:
                            act.wait_ge(sem(f"h_used{l}"), j)
                    nc.scalar.activation(h_hi[:, half, :], hw[:, half, :], ACT.Copy).then_inc(sem(f"h_hi{l}"), 1)

                def four(i, first):
                    for k in range(4):
                        st = k if first else i * 4 + k
                        j = (0 if first else i * 2) + k // 2
                        silu(j, k % 2, st)
                        high(j, k % 2, st)
                four(0, True)
                steps = 2 * NJ[l]
                with act.Fori(1, steps // 4) as i:
                    four(i, False)
                for st in range(steps // 4 * 4, steps):
                    silu(st // 2, st % 2, st)
                    high(st // 2, st % 2, st)
                for half in (0, 1):
                    if half == 0:
                        act.wait_ge(sem(f"h_used{l}"), NJ[l])
                    else:
                        act.wait_ge(w_used, AT_FF[l] + NJ[l])
                    for m in range(KD):
                        nc.scalar.activation(xn[:, half * 4 + m * 2:half * 4 + m * 2 + 2, :].rearrange("p a b -> p (a b)"),
                                             ps[:, m + 2 * half, :], ACT.Silu).then_inc(sem(f"gate{l}"), 1)
                if l == 0:
                    load_table(ACT.Sqrt)

            def heads(l, i, r):
                if l == 0:
                    return qo[:].rearrange("p (b h t) -> p b h t", b=B, t=T)[:, :, bass.ds(i * 8 + r, 1), :]\
                        .rearrange("p b h t -> p b (h t)")
                return qo[:].rearrange("p (g n) -> p g n", n=TOK)[:, bass.ds(i * 8 + r, 1), :]\
                    .rearrange("p g (b t) -> p (g b) t", b=B)

            act.wait_ge(sem("eps"), 1)
            nc.scalar.activation(warm[:, 0:1], eps_c[:], ACT.Copy).then_inc(sem("warm"), 1)
            act.wait_ge(sem("warm"), 1)
            load_table(ACT.Sqrt)
            norm(0)

            q_view = qo[:].rearrange("p (t c) -> p t c", c=H0)

            def queries(i):
                for c in range(4):
                    act.wait_ge(sem("q0_ps0"), i * 4 + (c + 1))
                    nc.scalar.activation(q_view[:, 0:HALF, bass.ds(i * 4 + c, 1)].rearrange("p t c -> p (t c)"), ps[:, (c % 2) * 2, :],
                                         ACT.Identity, bias=bq_s[:, bass.ds(i * 4 + c, 1)], scale=SCALE0)\
                        .then_inc(sem("q0_evac_act"), 1)
                    if isinstance(i, int) and c == 0:
                        logits_out(0, 0)
                        logits_out(0, 1)
                    if isinstance(i, int) and c == 1:
                        token_logits(0, prob, ACT.Sigmoid, sem("prob0"))
            act.wait_ge(sem("bq_s"), 1)
            queries(0)
            load_table(ACT.Exp)
            act.wait_ge(s_small, 16 * NSMALL)
            with act.Fori(1, N_Q0 // 2) as i:
                queries(i)

            def keys0(g, hh, half, n):
                wait_apart(act, sem("k0_ps"), g * 4 + (n + 1))
                nc.scalar.activation(kt0[:, hh, half * HALF:(half + 1) * HALF], ps[:, 6, :], ACT.Identity,
                                     bias=bk_c[:, bass.ds((g + n // 4) * 2 + hh, 1)], scale=1.0).then_inc(sem("k0"), 1)
            keys0(0, 0, 0, 0)
            keys0(0, 1, 0, 1)

            def heads0(g, par, first=False, last=False):
                for v in range(UNITS):
                    if not (first and v < 2):
                        evac_transposed(g, v - 2, 1, 2 + v % 2, first)
                    exps(g, v, 1, first)
                    if v in (1, 3):
                        keys0(g, v // 2, 1, 2 + v // 2)
                    if v in (5, 6) and not last:
                        keys0(g, v - 5, 0, 4 + v - 5)
                    if v in (1, 3) and last:
                        high(0, 0, v // 2)
            groups(act, heads0)
            for v in (6, 7):
                evac_transposed(N_KV0 - 1, v, 1, 2 + v % 2, False)
            out_projection(0, 2)
            experts(0)

            def qk_high(g, t):
                N = g * 8 + t
                act.wait_ge(sem("rotated"), N + 1)
                if not (isinstance(g, int) and g == 0 and t < 2):
                    act.wait_ge(sem("qk_t"), N - 1)
                nc.scalar.activation(qks[:, t % 2, 0:M1 + 1, 0:DH1], ra[:, t % 2, :].rearrange("p (h d) -> p h d", d=DH1),
                                     ACT.Copy)
                nc.scalar.activation(qks[:, t % 2, M1 + 1, DH1:P], ra[:, t % 2, M1 * DH1:QK1], ACT.Copy)\
                    .then_inc(sem("qk_hi"), 1)

            def qk_out(g, t):
                act.wait_ge(sem("qk_t"), g * 8 + (t + 1))
                at = slice(t % 2 * P, (t % 2 + 1) * P)
                nc.scalar.activation(qt1[:, t // 2 % 2, :, at], ps[:, 4, :].rearrange("p (h t) -> p h t", h=M1), ACT.Copy)
                nc.scalar.activation(kt1[:, t // 2 % 2, :, at], ps[:, 5, 0:2 * P].rearrange("p (h t) -> p h t", h=2),
                                     ACT.Copy).then_inc(sem("qk_out"), 1)

            norm(1)
            logits_out(1, 0)
            qk_high(0, 0)
            qk_high(0, 1)
            qk_out(0, 0)
            logits_out(1, 1)
            qk_high(0, 2)
            qk_out(0, 1)
            token_logits(1, lg, ACT.Copy, sem("lg"))
            load_table(ACT.Exp)

            def heads1(g, par, first=False, last=False):
                for v in range(UNITS):
                    if not (first and v < 2):
                        evac_transposed(g, v - 2, 2, 4, first)
                    if not (last and v >= 6):
                        qk_out(g if v < 6 else g + 1, (v + 2) % 8)
                    exps(g, v, 2, first, 0)
                    if not (last and v >= 5):
                        qk_high(g if v < 5 else g + 1, (v + 3) % 8)
                    exps(g, v, 2, first, 1)
                    if last and v == 4:
                        act.wait_ge(sem("shifted"), 1)
                        nc.scalar.activation(prob[:], lg[:], ACT.Exp).then_inc(sem("prob1"), 1)
                    if last and v >= 6:
                        act.wait_ge(sem("qk_t"), N_QKV1 * NT)
                        high(1, 0, v - 6)
            groups(act, heads1)
            for v in (6, 7):
                evac_transposed(N_QKV1 - 1, v, 2, 4, False)
            out_projection(1, 2)
            experts(1)

        @block.vector
        def _(dve):
            def heads(l, i, r):
                if l == 0:
                    return qo[:].rearrange("p (b h t) -> p b h t", b=B, t=T)[:, :, bass.ds(i * 8 + r, 1), :]\
                        .rearrange("p b h t -> p b (h t)")
                return qo[:].rearrange("p (g n) -> p g n", n=TOK)[:, bass.ds(i * 8 + r, 1), :]\
                    .rearrange("p g (b t) -> p (g b) t", b=B)

            def norm_stats(l, half):
                for t in range(half * 4, half * 4 + 4):
                    if l == 0 and t in (0, 2, 4):
                        dve.wait_ge(s_x[t // 2], 16)
                    if l == 1 and t % 2 == 0:
                        dve.wait_ge(sem("res0"), t // 2 + 1)
                    nc.vector.bn_stats(stats[:, t, :], xres[:, t, :]).then_inc(sem(f"stats{l}"), 1)
                for t in range(half * 4, half * 4 + 4):
                    dve.wait_ge(sem(f"stats{l}"), t + 1)
                    nc.vector.bn_aggr(mv[:, t, :], stats[:, t, :]).then_inc(sem(f"mv{l}"), 1)

            def norm_apply(l, half):
                h = slice(half * 4, half * 4 + 4)
                dve.wait_ge(sem(f"std{l}"), half + 1)
                nc.vector.reciprocal(rstd[:, h], std[:, h]).then_inc(sem(f"rstd{l}"), 1)
                dve.wait_ge(sem(f"rstd{l}"), half + 1)
                for t in range(half * 4, half * 4 + 4):
                    nc.vector.tensor_scalar(xn[:, t, :], xres[:, t, :], mv[:, t, 0:1], rstd[:, t:t + 1],
                                            ALU.subtract, ALU.mult).then_inc(sem(f"xn{l}"), 1)

            def norm_low(l, half):
                for k in range(KD):
                    h = slice(half * HALF, (half + 1) * HALF)
                    dve.wait_ge(sem(f"xt_hi{l}"), 2 * half + k + 1)
                    nc.vector.tensor_tensor(xt_lo[:, k, h], ps[:, k + 2 * half, :], xt_hi[:, k, h].bitcast(F32),
                                            ALU.subtract).then_inc(sem(f"xt{l}"), 1)

            routed = {0: 0, 1: 0}

            def step(l, ins):
                routed[l] += 1
                ins.then_inc(sem(f"route{l}"), 1)

            def settle(l):
                dve.wait_ge(sem(f"route{l}"), routed[l])

            def shift_logits():
                dve.wait_ge(sem("lg"), 2)
                step(1, nc.vector.tensor_reduce(red[:, 0, :], lg[:], AX.X, ALU.max))
                settle(1)
                nc.vector.tensor_tensor(lg[:], lg[:], red[:, 0, :].unsqueeze(2).to_broadcast([P, NT, E[1]]),
                                        ALU.subtract).then_inc(sem("shifted"), 1)

            def scores_of(l):
                e = E[l]
                sc = prob[:, :, 0:e]
                step(l, nc.vector.memset(val[:, :, e:e + 8], PAD))
                if l == 1:
                    dve.wait_ge(sem("prob1"), 1)
                    step(l, nc.vector.tensor_reduce(red[:, 1, :], sc, AX.X, ALU.add))
                    settle(l)
                    step(l, nc.vector.reciprocal(red[:, 2, :], red[:, 1, :]))
                    settle(l)
                    step(l, nc.vector.tensor_tensor(sc, sc, red[:, 2, :].unsqueeze(2).to_broadcast([P, NT, e]), ALU.mult))
                    settle(l)
                    step(l, nc.vector.tensor_tensor(val[:, :, 0:e], sc, gate_b_c[:].unsqueeze(1).to_broadcast([P, NT, e]), ALU.add))
                else:
                    dve.wait_ge(sem("prob0"), 2)
                    step(l, nc.vector.tensor_copy(val[:, :, 0:e], sc))

            def choose(l):
                e = E[l]
                settle(l)
                for t in range(NT):
                    step(l, nc.vector.max(top8[:, t, :], val[:, t, 0:e + 8]))
                settle(l)
                step(l, nc.vector.memset(top8[:, :, TOPK[l]:8], PAD))
                settle(l)
                for t in range(NT):
                    step(l, nc.vector.match_replace(rep[:, t, 0:e + 8], top8[:, t, :], val[:, t, 0:e + 8], CHOSEN))

            def weigh(l):
                e = E[l]
                sc = prob[:, :, 0:e]
                if l == 0:
                    step(l, nc.vector.memset(cw_s[:].bitcast(F32), 0.0))
                    settle(l)
                step(l, nc.vector.tensor_scalar(cw[:, :, 0:e], rep[:, :, 0:e], CHOSEN, None, ALU.is_equal))
                settle(l)
                step(l, nc.vector.tensor_tensor(cw[:, :, 0:e], cw[:, :, 0:e], sc, ALU.mult))
                settle(l)
                if l == 0:
                    step(l, nc.vector.tensor_reduce(red[:, 0, :], cw[:, :, 0:e], AX.X, ALU.add))
                    settle(l)
                    step(l, nc.vector.tensor_scalar(red[:, 1, :], red[:, 0, :], 1e-20, None, ALU.add))
                    settle(l)
                    step(l, nc.vector.reciprocal(red[:, 2, :], red[:, 1, :]))
                    settle(l)
                    step(l, nc.vector.tensor_tensor(cw[:, :, 0:e], cw[:, :, 0:e],
                                                    red[:, 2, :].unsqueeze(2).to_broadcast([P, NT, e]), ALU.mult))
                    settle(l)
                    step(l, nc.vector.tensor_scalar(cw[:, :, 0:e], cw[:, :, 0:e], ROUTE_SCALE0, None, ALU.mult))
                    settle(l)
                for q in (0, 2):
                    step(l, nc.vector.tensor_copy(cw_s[:, :, 32 * q:32 * q + e], cw[:, :, 0:e]))
                    step(l, nc.vector.memset(cw_s[:, :, 32 * q + e:32 * q + e + 1].bitcast(F32), 1.0))
                settle(l)
                for q in (1, 3):
                    step(l, nc.vector.tensor_tensor(cw_s[:, :, 32 * q:32 * q + e], cw[:, :, 0:e],
                                                    cw_s[:, :, 0:e].bitcast(F32), ALU.subtract))
                settle(l)
                nc.vector.memset(red[:, 3, 0:1], 0.0).then_inc(sem(f"cw{l}"), 1)

            def maxima(g, u, parts, first):
                U = g * 8 + u
                wait_apart(dve, sem(f"scores{parts}"), U + 1)
                for hh in range(parts):
                    for qt in (0, 1):
                        bank = u % 2 if parts == 1 else (u % 2) * 2 + hh
                        scores = ps[:, bank, score_columns(parts, qt)]
                        mask = masks[:, P:2 * P] if qt == 0 else masks[:, (parts - 1) * T:parts * T]
                        last = nc.vector.tensor_tensor_reduce(scores, scores, mask, -1.0, -MASKED, ALU.add, ALU.min,
                                                              negmax[:, u % 2, qt, hh:hh + 1])
                        if (qt, hh) != (1, parts - 1) or parts == 2:
                            last.then_inc(sem(f"negmax{parts}"), 1)
                if parts == 2:
                    dve.wait_ge(sem("negmax2"), U * 4 + 4)
                    sk = sinks_c[:, bass.ds(g * 4 + (u % 2) * 2, 2)]
                    last = nc.vector.tensor_tensor(sink_d[:, u % 2], negmax[:, u % 2], sk.unsqueeze(1).to_broadcast([P, 2, 2]), ALU.add)
                last.then_inc(sem(f"max{parts}"), 1)

            def normalised(g, u, parts):
                U = g * 8 + u
                dve.wait_ge(sem(f"exp{parts}"), U + 1)
                src = rsum[:, u % 2, :, 0:parts]
                if parts == 2:
                    nc.vector.tensor_tensor(den[:, u % 2], rsum[:, u % 2], sink_e[:, u % 2], ALU.add).then_inc(sem("den2"), 1)
                    dve.wait_ge(sem("den2"), U + 1)
                    src = den[:, u % 2]
                nc.vector.reciprocal(rinv[:, u % 2, :, 0:parts], src).then_inc(sem(f"recip{parts}"), 1)
                dve.wait_ge(sem(f"recip{parts}"), U + 1)
                for hh in range(parts):
                    for qt in (0, 1):
                        c = slice(0, P) if qt == 0 else slice(P, 3 * P)
                        last = nc.vector.tensor_scalar(prb[parts][:, u % 2, hh, c], prb[parts][:, u % 2, hh, c],
                                                       rinv[:, u % 2, qt, hh:hh + 1], None, ALU.mult)
                last.then_inc(sem(f"normed{parts}"), 1)

            def low(l, i, r):
                dve.wait_ge(sem(f"o_hi{l}"), i * 8 + (r + 1))
                nc.vector.tensor_tensor(o_lo[r % 2].rearrange("p (b t) -> p b t", b=B), heads(l, i, r),
                                        o_hi[r % 2].bitcast(F32).rearrange("p (b t) -> p b t", b=B), ALU.subtract)\
                    .then_inc(sem(f"o_split{l}"), 1)

            def out_projection(l, ahead):
                for i in range(N_OUT // 2):
                    for r in range(8):
                        if i or r >= ahead:
                            low(l, i, r)
                        if (l, i, r) == (1, 0, 2):
                            scores_of(1)
                        if (l, i, r) == (1, 0, 4):
                            choose(1)
                        if (l, i, r) == (1, 1, 0):
                            weigh(1)

            def experts(l):
                def step(j, half, st):
                    first = isinstance(st, int) and st < 2
                    dve.wait_ge(sem(f"silu{l}"), st + 1)
                    dve.wait_ge(sem(f"u{l}"), st + 1)
                    nc.vector.scalar_tensor_tensor(hf[:, half, :], ps[:, 5, :], b3_c[l][:, bass.ds(j, 1)], sg[:, half, :],
                                                   ALU.add, ALU.mult).then_inc(sem(f"gu{l}"), 1)
                    dve.wait_ge(sem(f"gu{l}"), st + 1)
                    dve.wait_ge(sem(f"wr{l}"), st + 1)
                    if not first:
                        dve.wait_ge(sem(f"h_hi{l}"), st - 1)
                    nc.vector.tensor_tensor(hw[:, half, :], ps[:, 6, :], hf[:, half, :], ALU.mult).then_inc(sem(f"gw{l}"), 1)
                    dve.wait_ge(sem(f"h_hi{l}"), st + 1)
                    nc.vector.tensor_tensor(h_lo[:, half, :], hw[:, half, :], h_hi[:, half, :].bitcast(F32), ALU.subtract)\
                        .then_inc(sem(f"h_lo{l}"), 1)

                def four(i, first):
                    for k in range(4):
                        step((0 if first else i * 2) + k // 2, k % 2, k if first else i * 4 + k)
                four(0, True)
                steps = 2 * NJ[l]
                with dve.Fori(1, steps // 4) as i:
                    four(i, False)
                for st in range(steps // 4 * 4, steps):
                    step(st // 2, st % 2, st)
                for half in (0, 1) if l == 1 else (0,):
                    for m in range(KD):
                        dve.wait_ge(sem(f"gate{l}"), 2 * half + m + 1)
                        h = slice(half * HALF, (half + 1) * HALF)
                        nc.vector.tensor_tensor(s_t[:, m, h], s_t[:, m, h],
                                                xn[:, half * 4 + m * 2:half * 4 + m * 2 + 2, :].rearrange("p a b -> p (a b)"),
                                                ALU.mult).then_inc(sem(f"prod{l}"), 1)
                for n in range(4):
                    dve.wait_ge(sem(f"prod_t{l}"), n + 1)
                    xv = xres[:, 2 * n:2 * n + 2, :].rearrange("p a b -> p (a b)")
                    nc.vector.tensor_tensor(xv, xv, ps[:, 4 + n, :], ALU.add).then_inc(sem(f"res{l}"), 1)
                    if l == 0 and n == 1:
                        norm_stats(1, 0)
                        norm_apply(1, 0)

            norm_stats(0, 0)
            norm_apply(0, 0)
            norm_stats(0, 1)
            norm_low(0, 0)
            norm_apply(0, 1)
            norm_low(0, 1)
            q_view = qo[:].rearrange("p (t c) -> p t c", c=H0)

            def queries(i):
                for c in range(4):
                    if c % 2:
                        dve.wait_ge(w_used, i * 2 + (AT_Q0 + c // 2 + 1))
                    else:
                        dve.wait_ge(sem("q0_ps1"), i * 2 + (c // 2 + 1))
                    nc.vector.tensor_scalar(q_view[:, HALF:TOK, bass.ds(i * 4 + c, 1)].rearrange("p t c -> p (t c)"),
                                            ps[:, (c % 2) * 2 + 1, :], bq_c[:, bass.ds(i * 4 + c, 1)], SCALE0, ALU.add,
                                            ALU.mult)\
                        .then_inc(sem("q0_evac_dve"), 1)
                    if isinstance(i, int) and c:
                        (scores_of, choose, weigh)[c - 1](0)
            dve.wait_ge(s_first, 16 * NFIRST)
            queries(0)
            with dve.Fori(1, N_Q0 // 2) as i:
                queries(i)
            dve.wait_ge(s_small, 16 * NSMALL)
            def values0(g, n):
                if n < 3:
                    dve.wait_ge(sem("v0_ps"), g * 3 + (n + 1))
                else:
                    dve.wait_ge(w_used, g + (AT_KV0 + 1))
                nc.vector.tensor_copy(v0[:, 2 * n:2 * n + 2, :].rearrange("p a b -> p (a b)"), ps[:, 7, :]).then_inc(sem("v0"), 1)

            def results0(g, v):
                b, hh = v % 8 // 2, v % 2
                g_of, U = (g - 1 if v < 0 else g), g * 8 + v
                dve.wait_ge(sem("o_ps1"), U + 1)
                nc.vector.tensor_scalar(qo[:, bass.ds(g_of * 2 * T + (b * H0 * T + hh * T), T)], ps[:, 4 + v % 2, 0:T],
                                        bv_c[:, bass.ds(g_of * 2 + hh, 1)], None, ALU.add).then_inc(sem("o_evac1"), 1)
            values0(0, 0)
            dve.wait_ge(sem("masks"), 4)

            def heads0(g, par, first=False, last=False):
                for v in range(UNITS):
                    maxima(g, v, 1, first)
                    if not (first and v < 1):
                        normalised(g, v - 1, 1)
                    if not (first and v < 3):
                        results0(g, v - 3)
                    if v in (0, 2, 4):
                        values0(g, v // 2 + 1)
                    if v == 7 and not last:
                        values0(g + 1, 0)
                    if v in (2, 4) and last:
                        low(0, 0, v // 2 - 1)
            groups(dve, heads0)
            normalised(N_KV0 - 1, 7, 1)
            for v in (5, 6, 7):
                results0(N_KV0 - 1, v)
            dve.wait_ge(sem("b2_hi"), 1)
            nc.vector.tensor_copy(b2_st[0:64, :], b2_f[0:64, :]).then_inc(sem("b2"), 1)
            nc.vector.tensor_tensor(b2_st[64:P, :], b2_f[64:P, :], b2_hi[64:P, :].bitcast(F32), ALU.subtract)\
                .then_inc(sem("b2"), 1)
            out_projection(0, 2)
            experts(0)

            norm_low(1, 0)
            norm_stats(1, 1)

            def tile1(g, t):
                N = g * 8 + t
                if t < NT - 1:
                    dve.wait_ge(sem("qkv1_ps"), g * 7 + (t + 1))
                else:
                    dve.wait_ge(w_used, g + (AT_QKV1 + 1))
                if not (isinstance(g, int) and g == 0 and t < 2):
                    dve.wait_ge(sem("rotated"), N - 1)
                bias = bqkv_c[:, bass.ds(g * QKV1, QKV1)]
                nc.vector.tensor_tensor(qkb[:, t % 2, :], ps[:, 7, 0:QK1], bias[:, 0:QK1], ALU.add).then_inc(sem("qkb"), 1)
                nc.vector.tensor_tensor(vp[:, t, DH1:2 * DH1], ps[:, 7, QK1:QKV1], bias[:, QK1:QKV1], ALU.add)\
                    .then_inc(sem("qkv1"), 1)

            def qk_low(g, t):
                dve.wait_ge(sem("qk_hi"), g * 8 + (t + 1))
                rotated = ra[:, t % 2, :]
                nc.vector.tensor_tensor(qks[:, t % 2, 0:M1 + 1, DH1:P], rotated.rearrange("p (h d) -> p h d", d=DH1),
                                        qks[:, t % 2, 0:M1 + 1, 0:DH1].bitcast(F32), ALU.subtract)
                nc.vector.tensor_tensor(qks[:, t % 2, M1 + 1, 0:DH1], rotated[:, M1 * DH1:QK1],
                                        qks[:, t % 2, M1 + 1, DH1:P].bitcast(F32), ALU.subtract).then_inc(sem("qk_lo"), 1)

            def results1(g, v):
                b, pr = v % 8 // 2, v % 2
                g_of, U = (g - 1 if v < 0 else g), g * 8 + v
                dve.wait_ge(sem("o_ps2"), U + 1)
                nc.vector.tensor_copy(qo[:, bass.ds(g_of * 2 * TOK + (pr * TOK + b * T), T)], ps[:, 6, 0:T])\
                    .then_inc(sem("o_evac2"), 1)

            tile1(0, 0)
            norm_apply(1, 1)
            tile1(0, 1)
            norm_low(1, 1)
            qk_low(0, 0)
            tile1(0, 2)
            qk_low(0, 1)

            def heads1(g, par, first=False, last=False):
                for v in range(UNITS):
                    if not (last and v >= 5):
                        tile1(g if v < 5 else g + 1, (v + 3) % 8)
                    if not (last and v >= 6):
                        qk_low(g if v < 6 else g + 1, (v + 2) % 8)
                    maxima(g, v, 2, first)
                    if not (first and v < 1):
                        normalised(g, v - 1, 2)
                    if not (first and v < 3):
                        results1(g, v - 3)
                    if last and v == 4:
                        shift_logits()
                    if last and v == 7:
                        low(1, 0, 0)
            groups(dve, heads1)
            normalised(N_QKV1 - 1, 7, 2)
            for v in (5, 6, 7):
                results1(N_QKV1 - 1, v)
                if v == 6:
                    low(1, 0, 1)
            out_projection(1, 2)
            experts(1)


def rope_tables():
    theta, scaling, alpha, beta, icl = 150000.0, 32.0, 1.0, 32.0, 128
    d_half = DH1 // 2
    freq = theta ** (np.arange(0, DH1, 2, dtype=np.float32) / DH1)
    concentration = 0.1 * math.log(scaling) + 1.0
    low = d_half * math.log(icl / (beta * 2 * math.pi)) / math.log(theta)
    high = d_half * math.log(icl / (alpha * 2 * math.pi)) / math.log(theta)
    ramp = np.clip((np.arange(d_half, dtype=np.float32) - low) / (high - low), 0.0, 1.0)
    mask = 1.0 - ramp
    inv_freq = 1.0 / (scaling * freq) * (1.0 - mask) + 1.0 / freq * mask
    freqs = np.outer(np.arange(T, dtype=np.float32), inv_freq)
    cos = np.asarray(np.cos(freqs) * concentration, np.float32)
    sin = np.asarray(np.sin(freqs) * concentration, np.float32)
    c = np.concatenate([cos, cos], 1)
    s = np.concatenate([-sin, sin], 1)
    q = np.float32(1.0 / math.sqrt(DH1))
    c = np.concatenate([c * q] * M1 + [c], 1).astype(np.float32)
    s = np.concatenate([s * q] * M1 + [s], 1).astype(np.float32)
    return c.reshape(2, P, QK1), s.reshape(2, P, QK1)


def selection(l):
    sel = np.zeros((NJ[l] * P, P), np.float32)
    for f in range((E[l] + 2) * FF):
        e = min(f // FF, E[l])
        sel[f, e] = sel[f, 32 + e] = 1.0
    return sel.reshape(NJ[l], P, P).transpose(0, 2, 1)


def rows(parts, l):
    width = parts[0].shape[-1]
    parts = [a.reshape(-1, width) for a in parts]
    have = sum(a.shape[0] for a in parts)
    return np.concatenate(parts + [np.zeros((NJ[l] * P - have, width), np.float32)], 0)


def pack_experts(l, gate, up, down):
    g, u, d = (rows(a, l) for a in (gate, up, down))

    def stationary(a):
        return a.reshape(NJ[l], P, KD, P).transpose(0, 3, 2, 1).reshape(NJ[l], P, KD * P)
    return np.concatenate([stationary(g), stationary(u), selection(l), d.reshape(NJ[l], P, D)], 2)


def columns(v, l):
    return rows([a.reshape(-1, 1) for a in v], l).reshape(NJ[l], P).T


def kernel(**inputs):
    import concourse.bacc as bacc
    from concourse.bass_utils import run_bass_kernel_spmd

    a = {k: np.asarray(v) for k, v in inputs.items()}
    f = lambda k: a[k]

    def by_pairs(w):
        return w.reshape(KD, P, 8, 2, P).transpose(2, 1, 3, 0, 4).reshape(8, P, 4 * P)

    def out_rows(w):
        return w.reshape(4, 4, P, D).transpose(0, 2, 1, 3).reshape(4, P, 4 * D)

    wv = f("L0_attn_Wv").reshape(KD, P, 8, 2 * P).transpose(2, 1, 0, 3).reshape(8, P, 4 * P)
    w1, b1 = f("L1_attn_qkv_w"), f("L1_attn_qkv_b")
    nq, nkv = G1 * M1 * DH1, G1 * DH1
    wg = np.concatenate([w1[:nq].reshape(G1, M1 * DH1, D), w1[nq:nq + nkv].reshape(G1, DH1, D),
                         w1[nq + nkv:].reshape(G1, DH1, D)], 1)
    bg = np.concatenate([b1[:nq].reshape(G1, M1 * DH1), b1[nq:nq + nkv].reshape(G1, DH1),
                         b1[nq + nkv:].reshape(G1, DH1)], 1)
    b2_rows = np.zeros((4, 32, D), np.float32)
    b2_rows[:, :E[1]] = f("L1_ffn_b2")
    b2_rows[:, E[1]] = f("L1_ffn_bs2")
    gates = np.zeros((2, KD, P, P), np.float32)
    for l, name in enumerate(("L0_ffn_gate_w", "L1_ffn_gate_w")):
        gates[l, :, :, :E[l]] = f(name).T.reshape(KD, P, E[l])
    t = lambda w: w.transpose(0, 2, 1)
    nothing = np.zeros(((E[0] + 2) * FF,), np.float32)
    cos, sin = rope_tables()
    arrays = {
        "x": f("L0_attn_x").reshape(TOK, D),
        "wq0": by_pairs(f("L0_attn_Wq")),
        "wkv0": np.concatenate([by_pairs(f("L0_attn_Wk")), wv], 2),
        "bq0": f("L0_attn_bq").reshape(H0, P).T, "bk0": f("L0_attn_bk").reshape(H0, P).T,
        "bv0": f("L0_attn_bv").reshape(H0, P).T,
        "wo_0": out_rows(f("L0_attn_Wo")), "wo_1": out_rows(f("L1_attn_out_w").T),
        "bo": np.stack([f("L0_attn_bo").reshape(KD, P).T, f("L1_attn_out_b").reshape(KD, P).T], 1),
        "wff_0": pack_experts(0, [f("L0_ffn_exp_wg"), f("L0_ffn_shared_wg")], [f("L0_ffn_exp_wu"), f("L0_ffn_shared_wu")],
                              [t(f("L0_ffn_exp_wd")), f("L0_ffn_shared_wd").T]),
        "wff_1": pack_experts(1, [f("L1_ffn_w1"), f("L1_ffn_ws1")], [f("L1_ffn_w3"), f("L1_ffn_ws3")],
                              [t(f("L1_ffn_w2")), f("L1_ffn_ws2").T]),
        "b1_0": columns([nothing], 0), "b3_0": columns([nothing], 0),
        "b1_1": columns([f("L1_ffn_b1"), f("L1_ffn_bs1")], 1), "b3_1": columns([f("L1_ffn_b3"), f("L1_ffn_bs3")], 1),
        "b2": b2_rows.reshape(P, D),
        "gates": gates.transpose(0, 2, 1, 3).reshape(2, P, KD * P),
        "gate_b": f("L1_ffn_gate_b").reshape(1, E[1]),
        "wqkv1": wg.reshape(G1, QKV1, KD, P).transpose(0, 3, 2, 1).reshape(G1, P, KD * QKV1),
        "bqkv1": bg.reshape(1, G1 * QKV1), "sinks": f("L1_attn_sinks").reshape(1, G1 * M1),
        "rope_cos": cos, "rope_sin": sin,
    }
    nc = bacc.Bacc("TRN2", target_bir_lowering=False, num_devices=1)
    ap, host = {}, {}
    for name, v in arrays.items():
        v = np.ascontiguousarray(v)
        host[f"in_{name}"] = v
        ap[name] = nc.dram_tensor(f"in_{name}", v.shape, mybir.dt.from_np(v.dtype), kind="ExternalInput").ap()
    out = nc.dram_tensor("out", (TOK, D), F32, kind="ExternalOutput").ap()
    program(nc, ap["x"], ap["wq0"], ap["wkv0"], ap["bq0"], ap["bk0"], ap["bv0"], (ap["wo_0"], ap["wo_1"]), ap["bo"],
            (ap["wff_0"], ap["wff_1"]), (ap["b1_0"], ap["b1_1"]), (ap["b3_0"], ap["b3_1"]), ap["b2"], ap["gates"],
            ap["gate_b"], ap["wqkv1"], ap["bqkv1"], ap["sinks"], ap["rope_cos"], ap["rope_sin"], out)
    r = run_bass_kernel_spmd(nc, [host], core_ids=[0])
    return r.results[0]["out"].reshape(B, T, D)
```
